# Optimizing a Trainium2 kernel written in Bass

```python
import numpy as np
import jax
import jax.numpy as jnp

def _softmax(x, axis=-1):
    return jax.nn.softmax(x, axis=axis)

def _gelu(x):
    return jax.nn.gelu(x, approximate=True)

def _silu(x):
    return jax.nn.silu(x)

def _sigmoid(x):
    return jax.nn.sigmoid(x)

def _layernorm(x, axis=-1, eps=1e-05):
    m = jnp.mean(x, axis=axis, keepdims=True)
    v = jnp.var(x, axis=axis, keepdims=True)
    return (x - m) / jnp.sqrt(v + eps)

def _scatter_add(tgt, idx, src, axis=0):
    return tgt.at[idx].add(src)

def _segment_sum(src, seg, n):
    return jax.ops.segment_sum(src, seg, n)
kernel_name = 'mk_gnn_resnorm_d2_gnn_r8_3e3e88'

def setup_inputs(seed: int=0):
    np.random.seed(seed)
    _w = jnp.asarray

    def _rec_inputs():
        import jax
        import jax.numpy as jnp
        _gk = jax.random.key(seed)
        x = -0.0002117 + 1 * jax.random.normal(jax.random.fold_in(_gk, 1), (6250, 256), jnp.float32)
        src = jax.random.randint(jax.random.fold_in(_gk, 2), (200000,), 0, 6250, jnp.int32)
        dst = jax.random.randint(jax.random.fold_in(_gk, 3), (200000,), 0, 6250, jnp.int32)
        _o = jnp.argsort(dst, stable=True)
        src = src[_o]
        dst = dst[_o]
        edge_attr_64 = jax.random.uniform(jax.random.fold_in(_gk, 11), (200000, 64), jnp.float32, 0.0, 1)
        edge_weight = -0.00278149 + 0.998712 * jax.random.normal(jax.random.fold_in(_gk, 13), (200000,), jnp.float32)
        return (x, src, dst, edge_attr_64, edge_weight)
    x, src, dst, edge_attr_64, edge_weight = _rec_inputs()

    def _L0_gnn_setup():
        import jax, jax.numpy as jnp
        import numpy as np
        N = 12500
        E = 200000
        D_NODE = 256
        D_MSG = 128
        D_RAD = 64
        HEADS = 4
        OUTC = D_MSG // HEADS

        def _w(key, shape):
            fan_in = shape[-1]
            return jax.random.normal(key, shape, dtype=jnp.float32) / jnp.sqrt(jnp.float32(fan_in))
        key = jax.random.key(seed)
        ks = jax.random.split(key, 16)
        x = jax.random.normal(ks[0], (N, D_NODE), dtype=jnp.float32)
        edge_attr = jax.random.uniform(ks[1], (E, D_RAD), dtype=jnp.float32)
        edge_index = jax.random.randint(ks[2], (2, E), 0, N, dtype=jnp.int64)
        return {'x': x, 'edge_attr': edge_attr, 'edge_index': edge_index, 'W_edge': _w(ks[3], (D_RAD, D_RAD)), 'W_n2m': _w(ks[4], (D_MSG, D_NODE)), 'Wq': _w(ks[5], (D_MSG, D_MSG)), 'bq': jnp.zeros((D_MSG,), jnp.float32), 'Wk': _w(ks[6], (D_MSG, D_MSG)), 'bk': jnp.zeros((D_MSG,), jnp.float32), 'Wv': _w(ks[7], (D_MSG, D_MSG)), 'bv': jnp.zeros((D_MSG,), jnp.float32), 'We': _w(ks[8], (D_MSG, D_RAD)), 'Wskip': _w(ks[9], (D_MSG, D_MSG)), 'bskip': jnp.zeros((D_MSG,), jnp.float32), 'Wbeta': _w(ks[10], (1, 3 * D_MSG)), 'W_m2n': _w(ks[11], (D_NODE, D_MSG))}
    _L0_gnn_all = _L0_gnn_setup()
    _L0_gnn_in = {k: v for k, v in _L0_gnn_all.items() if k in ('W_edge', 'W_n2m', 'Wq', 'bq', 'Wk', 'bk', 'Wv', 'bv', 'We', 'Wskip', 'bskip', 'Wbeta', 'W_m2n')}
    del _L0_gnn_all

    def _L1_gnn_setup():
        import jax, jax.numpy as jnp
        import numpy as np
        N = 1250
        E = 40000
        D = 256
        EPS = 1e-05

        def layer_norm(x, g, b):
            mu = jnp.mean(x, axis=-1, keepdims=True)
            var = jnp.mean(jnp.square(x - mu), axis=-1, keepdims=True)
            return (x - mu) * jax.lax.rsqrt(var + EPS) * g + b

        def linear(x, w, b):
            return x @ w + b
        key = jax.random.key(seed)
        ks = jax.random.split(key, 20)
        s = 1.0 / np.sqrt(D)
        inp = {'x': jax.random.normal(ks[0], (N, D), jnp.float32), 'edge_index': jax.random.randint(ks[1], (2, E), 0, N, jnp.int64), 'edge_weight': jax.random.normal(ks[2], (E,), jnp.float32), 'wq': jax.random.normal(ks[3], (D, D), jnp.float32) * s, 'bq': jnp.zeros((D,), jnp.float32), 'wk': jax.random.normal(ks[4], (D, D), jnp.float32) * s, 'bk': jnp.zeros((D,), jnp.float32), 'wv': jax.random.normal(ks[5], (D, D), jnp.float32) * s, 'bv': jnp.zeros((D,), jnp.float32), 'ws': jax.random.normal(ks[6], (D, D), jnp.float32) * s, 'bs': jnp.zeros((D,), jnp.float32), 'we': jax.random.normal(ks[7], (1, 1), jnp.float32), 'be': jnp.zeros((1,), jnp.float32), 'g1': jnp.ones((D,), jnp.float32), 'b1': jnp.zeros((D,), jnp.float32), 'g2': jnp.ones((D,), jnp.float32), 'b2': jnp.zeros((D,), jnp.float32), 'w_ff1': jax.random.normal(ks[8], (D, 2 * D), jnp.float32) * s, 'b_ff1': jnp.zeros((2 * D,), jnp.float32), 'w_ff2': jax.random.normal(ks[9], (2 * D, D), jnp.float32) * (1.0 / np.sqrt(2 * D)), 'b_ff2': jnp.zeros((D,), jnp.float32)}
        return inp
    _L1_gnn_all = _L1_gnn_setup()
    _L1_gnn_in = {k: v for k, v in _L1_gnn_all.items() if k in ('wq', 'bq', 'wk', 'bk', 'wv', 'bv', 'ws', 'bs', 'we', 'be', 'g1', 'b1', 'g2', 'b2', 'w_ff1', 'b_ff1', 'w_ff2', 'b_ff2')}
    del _L1_gnn_all
    return {'x': x, 'src': src, 'dst': dst, 'edge_attr_64': edge_attr_64, 'edge_weight': edge_weight, 'L0_gnn_W_edge': _L0_gnn_in['W_edge'], 'L0_gnn_W_n2m': _L0_gnn_in['W_n2m'], 'L0_gnn_Wq': _L0_gnn_in['Wq'], 'L0_gnn_bq': _L0_gnn_in['bq'], 'L0_gnn_Wk': _L0_gnn_in['Wk'], 'L0_gnn_bk': _L0_gnn_in['bk'], 'L0_gnn_Wv': _L0_gnn_in['Wv'], 'L0_gnn_bv': _L0_gnn_in['bv'], 'L0_gnn_We': _L0_gnn_in['We'], 'L0_gnn_Wskip': _L0_gnn_in['Wskip'], 'L0_gnn_bskip': _L0_gnn_in['bskip'], 'L0_gnn_Wbeta': _L0_gnn_in['Wbeta'], 'L0_gnn_W_m2n': _L0_gnn_in['W_m2n'], 'L1_gnn_wq': _L1_gnn_in['wq'], 'L1_gnn_bq': _L1_gnn_in['bq'], 'L1_gnn_wk': _L1_gnn_in['wk'], 'L1_gnn_bk': _L1_gnn_in['bk'], 'L1_gnn_wv': _L1_gnn_in['wv'], 'L1_gnn_bv': _L1_gnn_in['bv'], 'L1_gnn_ws': _L1_gnn_in['ws'], 'L1_gnn_bs': _L1_gnn_in['bs'], 'L1_gnn_we': _L1_gnn_in['we'], 'L1_gnn_be': _L1_gnn_in['be'], 'L1_gnn_g1': _L1_gnn_in['g1'], 'L1_gnn_b1': _L1_gnn_in['b1'], 'L1_gnn_g2': _L1_gnn_in['g2'], 'L1_gnn_b2': _L1_gnn_in['b2'], 'L1_gnn_w_ff1': _L1_gnn_in['w_ff1'], 'L1_gnn_b_ff1': _L1_gnn_in['b_ff1'], 'L1_gnn_w_ff2': _L1_gnn_in['w_ff2'], 'L1_gnn_b_ff2': _L1_gnn_in['b_ff2']}

def reference(x, src, dst, edge_attr_64, edge_weight, L0_gnn_W_edge, L0_gnn_W_n2m, L0_gnn_Wq, L0_gnn_bq, L0_gnn_Wk, L0_gnn_bk, L0_gnn_Wv, L0_gnn_bv, L0_gnn_We, L0_gnn_Wskip, L0_gnn_bskip, L0_gnn_Wbeta, L0_gnn_W_m2n, L1_gnn_wq, L1_gnn_bq, L1_gnn_wk, L1_gnn_bk, L1_gnn_wv, L1_gnn_bv, L1_gnn_ws, L1_gnn_bs, L1_gnn_we, L1_gnn_be, L1_gnn_g1, L1_gnn_b1, L1_gnn_g2, L1_gnn_b2, L1_gnn_w_ff1, L1_gnn_b_ff1, L1_gnn_w_ff2, L1_gnn_b_ff2):
    import jax
    import jax.numpy as jnp

    def _L0_gnn_ref(x, edge_attr, edge_index, W_edge, W_n2m, Wq, bq, Wk, bk, Wv, bv, We, Wskip, bskip, Wbeta, W_m2n):
        import jax, jax.numpy as jnp
        import numpy as np
        N = 12500
        E = 200000
        D_NODE = 256
        D_MSG = 128
        D_RAD = 64
        HEADS = 4
        OUTC = D_MSG // HEADS

        def _w(key, shape):
            fan_in = shape[-1]
            return jax.random.normal(key, shape, dtype=jnp.float32) / jnp.sqrt(jnp.float32(fan_in))
        src = edge_index[0]
        dst = edge_index[1]
        n = x.shape[0]
        scale = 1.0 / jnp.sqrt(jnp.float32(OUTC))
        ee = edge_attr @ W_edge.T
        m = x @ W_n2m.T
        q = (m @ Wq.T + bq).reshape(n, HEADS, OUTC)
        k = (m @ Wk.T + bk).reshape(n, HEADS, OUTC)
        v = (m @ Wv.T + bv).reshape(n, HEADS, OUTC)
        e = (ee @ We.T).reshape(-1, HEADS, OUTC)
        kj = k[src] + e
        alpha = jnp.einsum('ehc,ehc->eh', q[dst], kj) * scale
        amax = jax.ops.segment_max(alpha, dst, num_segments=n)
        expa = jnp.exp(alpha - amax[dst])
        asum = jax.ops.segment_sum(expa, dst, num_segments=n)
        alpha = expa / (asum[dst] + 1e-16)
        msg = (v[src] + e) * alpha[..., None]
        out = jax.ops.segment_sum(msg, dst, num_segments=n)
        out = out.reshape(n, D_MSG)
        x_r = m @ Wskip.T + bskip
        beta = jax.nn.sigmoid(jnp.concatenate([out, x_r, out - x_r], axis=-1) @ Wbeta.T)
        out = beta * x_r + (1.0 - beta) * out
        return out @ W_m2n.T

    def _L1_gnn_ref(x, edge_index, edge_weight, wq, bq, wk, bk, wv, bv, ws, bs, we, be, g1, b1, g2, b2, w_ff1, b_ff1, w_ff2, b_ff2):
        import jax, jax.numpy as jnp
        import numpy as np
        N = 1250
        E = 40000
        D = 256
        EPS = 1e-05

        def layer_norm(x, g, b):
            mu = jnp.mean(x, axis=-1, keepdims=True)
            var = jnp.mean(jnp.square(x - mu), axis=-1, keepdims=True)
            return (x - mu) * jax.lax.rsqrt(var + EPS) * g + b

        def linear(x, w, b):
            return x @ w + b
        n = x.shape[0]
        scale = x.shape[-1] ** (-0.5)
        q = linear(x, wq, bq)
        k = linear(x, wk, bk)
        v = linear(x, wv, bv)
        src, dst = (edge_index[0], edge_index[1])
        scores = jnp.sum(q[dst] * k[src], axis=-1) * scale
        scores = scores + (edge_weight[:, None] @ we + be)[:, 0]
        seg_max = jax.ops.segment_max(scores, dst, num_segments=n)
        exp_s = jnp.exp(scores - seg_max[dst])
        denom = jax.ops.segment_sum(exp_s, dst, num_segments=n)
        attn = exp_s / jnp.maximum(denom[dst], 1e-12)
        message = v[src] * attn[:, None]
        out = jax.ops.segment_sum(message, dst, num_segments=n)
        x = layer_norm(x + out + linear(x, ws, bs), g1, b1)
        ffn = linear(jax.nn.gelu(linear(x, w_ff1, b_ff1)), w_ff2, b_ff2)
        x = layer_norm(x + ffn, g2, b2)
        return x
    edge_index = jnp.stack([src, dst])
    x = _layernorm(x + _L0_gnn_ref(x, edge_attr_64, edge_index, L0_gnn_W_edge, L0_gnn_W_n2m, L0_gnn_Wq, L0_gnn_bq, L0_gnn_Wk, L0_gnn_bk, L0_gnn_Wv, L0_gnn_bv, L0_gnn_We, L0_gnn_Wskip, L0_gnn_bskip, L0_gnn_Wbeta, L0_gnn_W_m2n), axis=-1)
    x = _layernorm(x + _L1_gnn_ref(x, edge_index, edge_weight, L1_gnn_wq, L1_gnn_bq, L1_gnn_wk, L1_gnn_bk, L1_gnn_wv, L1_gnn_bv, L1_gnn_ws, L1_gnn_bs, L1_gnn_we, L1_gnn_be, L1_gnn_g1, L1_gnn_b1, L1_gnn_g2, L1_gnn_b2, L1_gnn_w_ff1, L1_gnn_b_ff1, L1_gnn_w_ff2, L1_gnn_b_ff2), axis=-1)
    return x

_drawn_inputs = setup_inputs


def setup_inputs(seed=0):
    import zlib

    import numpy as np

    out = dict(_drawn_inputs(seed))
    spreads = {'L0_gnn_bq': (0.0, 0.8),
     'L0_gnn_bk': (0.0, 0.8),
     'L0_gnn_bv': (0.0, 0.1),
     'L0_gnn_bskip': (0.0, 0.1),
     'L1_gnn_bq': (0.0, 0.8),
     'L1_gnn_bk': (0.0, 0.8),
     'L1_gnn_bv': (0.0, 0.1),
     'L1_gnn_bs': (0.0, 0.1),
     'L1_gnn_g1': (1.0, 0.2),
     'L1_gnn_b1': (0.0, 0.1),
     'L1_gnn_g2': (1.0, 0.2),
     'L1_gnn_b2': (0.0, 0.1),
     'L1_gnn_b_ff1': (0.0, 0.1),
     'L1_gnn_b_ff2': (0.0, 0.1)}
    factors = {'edge_weight': 8.0}
    for name, (base, spread) in spreads.items():
        noise = np.random.default_rng([zlib.crc32(name.encode()), seed]).standard_normal(out[name].shape)
        drawn = base * np.exp(spread * noise) if base else spread * noise
        out[name] = jnp.asarray(drawn.astype(out[name].dtype))
    for name, factor in factors.items():
        out[name] = (out[name] * factor).astype(out[name].dtype)
    return out
```

```python
from contextlib import ExitStack

import numpy as np
import concourse.bass as bass
from concourse import mybir

F32, BF16, I32 = mybir.dt.float32, mybir.dt.bfloat16, mybir.dt.int32
ALU = mybir.AluOpType
ACT = mybir.ActivationFunctionType
AX = mybir.AxisListType

P = 128
N, E, D = 6250, 200000, 256
DM, DR, HEADS = 128, 64, 4
OUTC = DM // HEADS
NW = 50
NP = NW * P
JT = 4
SUPER = JT * P
NS = -(-E // SUPER)
EP = NS * SUPER
REAL_W = -(-N // P)
CH = 8
NI = CH * JT
NC = -(-(NS + REAL_W - 1) // CH)
NPAIR = NC * CH
SG = -(-NS // P)
BIG = 1e30
NO_NODE = 1 << 20
U = 2
EPS = 1e-5


def after(eng, sem, value):
    if not (isinstance(value, int) and value <= 0):
        eng.wait_ge(sem, value)


def stand_by(eng, gate, sem, value):
    if isinstance(value, int):
        after(eng, sem, value)
    else:
        eng.wait_ge(sem, value)
        eng.sem_inc(gate, 1)


def build(nc, a, out):
    ctx = ExitStack()
    with ctx:
        def sb(name, shape, dt=F32):
            return ctx.enter_context(nc.sbuf_tensor(name, shape, dt))

        def sem(name):
            return ctx.enter_context(nc.semaphore(name))

        def dram(name, shape, dt=F32):
            return nc.dram_tensor(name, shape, dt, kind="Internal").ap()

        kv_d = dram("kv_d", (NP, 2 * DM))
        q0_d = dram("q0_d", (NW, P, 3 * DM), BF16)
        xr_d = dram("xr_d", (NW, P, DM))
        acc0_d = dram("acc0_d", (NW, P, DM + HEADS))
        x1_d = dram("x1_d", (NP, D))
        q1_d = dram("q1_d", (NW, P, 3 * (D + 1)), BF16)
        acc1_d = dram("acc1_d", (NW, P, D + 1))

        ident = sb("ident", [P, P])
        iota_row = sb("iota_row", [P, P])
        iota_col = sb("iota_col", [P, 1])
        ones = sb("ones", [P, P])
        tri = sb("tri", [P, P])
        sel_j = {4: sb("sel_j4", [P, NI]), 1: sb("sel_j1", [P, NI])}
        sel_h = {4: sb("sel_h4", [P, 4]), 1: sb("sel_h1", [P, 1])}
        sel_ht = {4: sb("sel_ht4", [4, P]), 1: sb("sel_ht1", [1, P])}
        minus_half = sb("minus_half", [P, 1])
        zero_rows = sb("zero_rows", [P, D + 1])
        w_n2m = sb("w_n2m", [P, 2, DM])
        w_qkvs = sb("w_qkvs", [P, 4 * DM])
        b_qkvs = sb("b_qkvs", [P, 4 * DM])
        w_edge = sb("w_edge", [DR, DR])
        w_et = sb("w_et", [DR, DM])
        w_c = sb("w_c", [DR, DM])
        w_beta = sb("w_beta", [P, 3, DM])
        w_m2n = sb("w_m2n", [P, D])
        w_q1 = sb("w_q1", [P, 2, D])
        b_q1 = sb("b_q1", [P, 2])
        w_k1t = sb("w_k1t", [P, 2, D + 1])
        w_v1 = sb("w_v1", [P, 2, D])
        w_s1 = sb("w_s1", [P, 2, D])
        w_f1 = sb("w_f1", [P, 2, 2 * D])
        b_f1 = sb("b_f1", [P, 4])
        w_f2 = sb("w_f2", [P, 4, D])
        rows1 = sb("vecs1", [P, 7, D])
        we_be = sb("we_be", [P, 2])
        BV, BS, G1, B1, G2, B2, BF2 = range(7)
        sched = sb("sched", [P, SG, 3], I32)
        sched_w = sb("sched_w", [P, SG, 3], I32)
        sched_f = sb("sched_f", [P, SG, 3])
        n_win = sb("n_win", [P, SG])
        d_win = sb("d_win", [P, SG])
        start = sb("start", [P, SG])
        pair_no = sb("pair_no", [P, NPAIR])
        begun = sb("begun", [P, SG, NPAIR])
        stepped = sb("stepped", [P, SG, NPAIR])
        t_of = sb("t_of", [P, NPAIR])
        w_of = sb("w_of", [P, NPAIR])
        base_tab = sb("base_tab", [P, NPAIR])
        node_tab = sb("node_tab", [P, NPAIR])
        keep_tab = sb("keep_tab", [P, NPAIR])
        tw_int = sb("tw_int", [1, 2, NPAIR], I32)

        ps = ctx.enter_context(nc.psum_tensor("ps", [P, 8, 512], F32))

        idx = [sb(f"idx{b}", [P, CH, 4 * JT], I32) for b in range(2)]
        dst_row = [sb(f"dst_row{b}", [P, SUPER], I32) for b in range(2)]
        qw = [sb(f"qw{b}", [P, 3, D + 1], BF16) for b in range(2)]
        ea = [sb(f"ea{b}", [DR, SUPER]) for b in range(2)]
        ew = [sb(f"ew{b}", [P, NI]) for b in range(2)]
        rows = [sb(f"rows{b}", [P, CH, JT, D]) for b in range(2)]
        oht = [sb(f"oht{b}", [P, SUPER], BF16) for b in range(2)]
        oh = [sb(f"oh{b}", [P, JT, P]) for b in range(2)]
        prod = sb("prod", [P, JT, D])
        score = [sb(f"score{b}", [P, NI, HEADS]) for b in range(2)]
        rel_first = [sb(f"rel_first{b}", [HEADS, 1]) for b in range(2)]
        rel = [sb(f"rel{b}", [P, CH, JT]) for b in range(2)]
        same = sb("same", [P, NI])
        inside = sb("inside", [P, NI])
        outside = sb("outside", [P, NI])
        biased = sb("biased", [P, NI, HEADS])
        pen = sb("pen", [P, NI, HEADS])
        pen_r = sb("pen_r", [P, P + 1])
        fwd = sb("fwd", [P, P])
        bwd = sb("bwd", [P, P])
        full = sb("full", [P, P])
        spread = sb("spread", [P, 4, NI])
        runs = sb("runs", [HEADS, 4, NI + 1])
        pen_f = sb("pen_f", [HEADS, NI])
        pen_b = sb("pen_b", [HEADS, NI])
        run_f = [sb(f"run_f{b}", [HEADS, NI + 1]) for b in range(2)]
        run_b = sb("run_b", [HEADS, NI + 1])
        carry = sb("carry", [HEADS, 2, NI])
        carry_p = sb("carry_p", [P, 2, NI])
        carry_r = sb("carry_r", [P, 2])
        below = sb("below", [P, NI * HEADS])
        prob = [sb(f"prob{b}", [P, NI, HEADS]) for b in range(2)]
        shrink_in = sb("shrink_in", [HEADS, 1])
        shrink = sb("shrink", [HEADS, 1])
        shrink_d = sb("shrink_d", [HEADS, HEADS])
        first_oh = sb("first_oh", [HEADS, P])
        rescale = sb("rescale", [P, HEADS])
        msg = [sb(f"msg{b}", [P, JT, D + 1]) for b in range(2)]
        acc = [sb(f"acc{b}", [P, D + 1]) for b in range(2)]
        acc_scaled = sb("acc_scaled", [P, D + 1])

        nx = [sb(f"nx{b}", [P, 2, P]) for b in range(U)]
        nrow = [sb(f"nrow{b}", [P, D]) for b in range(U)]
        nT = [sb(f"nT{b}", [P, 4, P]) for b in range(U)]
        nT2 = [sb(f"nT2{b}", [P, 4, P]) for b in range(U)]
        nbig = [sb(f"nbig{b}", [P, 4 * DM]) for b in range(U)]
        nacc = [sb(f"nacc{b}", [P, D + 1]) for b in range(U)]
        nsum = [sb(f"nsum{b}", [P, D + 1]) for b in range(U)]
        nh = [sb(f"nh{b}", [P, D]) for b in range(U)]
        nh2 = [sb(f"nh2{b}", [P, D]) for b in range(U)]
        nres = [sb(f"nres{b}", [P, D + 1]) for b in range(U)]
        nq = [sb(f"nq{b}", [P, 3, D + 1], BF16) for b in range(U)]
        nxr = [sb(f"nxr{b}", [P, DM]) for b in range(U)]
        nden = [sb(f"nden{b}", [P, HEADS]) for b in range(U)]
        nz = [sb(f"nz{b}", [P, 8]) for b in range(U)]
        nst = [sb(f"nst{b}", [P, 6]) for b in range(U)]
        nmv = [sb(f"nmv{b}", [P, 2]) for b in range(U)]
        nve = [sb(f"nve{b}", [P, 1]) for b in range(U)]
        nrs = [sb(f"nrs{b}", [P, 1]) for b in range(U)]

        s_w = sem("weights_loaded")
        s_sched = sem("sched_loaded")
        s_iota = sem("iotas_ready")
        s_zero = sem("zero_rows_ready")
        s_zst = sem("zeros_stored")
        s_cst = sem("constants_ready")
        s_win = sem("windows_ready")
        s_start = sem("starts_ready")
        s_stp = sem("starts_copied")
        s_begun = sem("begun_ready")
        s_pairs = sem("pairs_ready")
        s_tab = sem("tables_ready")
        s_wcp, s_wc = sem("edge_weight_product"), sem("edge_weight_ready")
        s_phase = sem("phase_done")
        phases = [0]

        def end_phase(eng, n):
            eng.drain().then_inc(s_phase, 1)
            eng.wait_ge(s_phase, 5 * n)

        def window(ap, w):
            return ap[bass.ds(w, 1)].rearrange("o p c -> (o p) c")

        def node_rows(ap, w):
            return ap[bass.ds(w * P, P), :]

        def slots(name):
            return [sem(f"{name}{b}") for b in range(U)]

        n0 = dict(load=slots("n0_loaded"), store=slots("n0_stored"), m=sem("n0_m"), mT=sem("n0_mT"),
                  big=sem("n0_projected"), res=sem("n0_biased"))
        n1 = dict(load=slots("n1_loaded"), store=slots("n1_stored"), z=sem("n1_gate_sum"), en=sem("n1_gate_exp"),
                  mix=sem("n1_mixed"), tp=sem("n1_mixedT"), tc=sem("n1_mixedT_copied"), y=sem("n1_out"),
                  var=sem("n1_var"), rstd=sem("n1_rstd"), x1=sem("n1_x1"), xt=sem("n1_x1T"), xc=sem("n1_x1T_copied"),
                  q=sem("n1_qT"), qc=sem("n1_qT_copied"), qk=sem("n1_qk"), split=sem("n1_split"))
        n2 = dict(load=slots("n2_loaded"), store=slots("n2_stored"), mean=sem("n2_attention"), tp=sem("n2_T"),
                  tc=sem("n2_T_copied"), lin=sem("n2_linear"), var=sem("n2_var"), rstd=sem("n2_rstd"), x2=sem("n2_x2"),
                  xt=sem("n2_x2T"), xc=sem("n2_x2T_copied"), u=sem("n2_up"), g=sem("n2_gelu"), f=sem("n2_ffn"),
                  res=sem("n2_result"))

        def edge_sems(n):
            names = ("oht", "e", "q", "score", "masked", "turned", "pens", "ends", "arranged", "carries", "spreadback",
                     "full", "fullT", "below", "prob", "shrink_in", "shrink", "so_in", "so", "msg", "msgp", "agg",
                     "acc", "go")
            s = {x: sem(f"l{n}_{x}") for x in names}
            for x in ("ld_idx", "ld_row", "ld_q", "ld_ea", "gathered", "stored"):
                s[x] = [sem(f"l{n}_{x}{b}") for b in range(2)]
            return s

        s_l = [edge_sems(0), edge_sems(1)]

        block = ctx.enter_context(nc.Block())

        class Layer:
            pass

        L0, L1 = Layer(), Layer()
        L0.s, L0.H, L0.D, L0.table, L0.q_d, L0.acc_d, L0.AW = s_l[0], HEADS, DM, kv_d, q0_d, acc0_d, DM + HEADS
        L1.s, L1.H, L1.D, L1.table, L1.q_d, L1.acc_d, L1.AW = s_l[1], 1, D, x1_d, q1_d, acc1_d, D + 1
        L0.QD, L1.QD = DM, D + 1
        for L in (L0, L1):
            L.R = NI * L.H

        def chunks(eng, emit):
            emit(0, 0)
            emit(1, 1)
            with eng.Fori(1, NC // 2) as k:
                emit(2 * k, 0)
                emit(2 * k + 1, 1)
            if NC % 2:
                emit(NC - 1, 0)

        def windows(eng, emit):
            emit(0)
            with eng.Fori(1, NW // U) as k:
                emit(k)

        def q_ps(L, b):
            if L.H == HEADS:
                return ps[:, 2 * b, :]
            return ps[:, 2 * b:2 * b + 2, :].rearrange("p k n -> p (k n)")

        def e_ps(b):
            return ps[:, 2 * b + 1, :]

        def agg_ps(L, b):
            return ps[:, 4 + b, 0:L.AW]

        turn_ps = ps[:, 6, :]
        arr_ps, back_ps, so_ps = ps[:, 7, 0:P], ps[:, 7, P:P + 2 * NI], ps[:, 7, 192:192 + HEADS]
        qb_ps = [ps[:, 7, 208 + JT * b:208 + JT * (b + 1)] for b in range(2)]

        @block.sync
        def _(sp):
            gate = sem("sp_gate")

            def wait(s, value):
                stand_by(sp, gate, s, value)

            sp.dma_start(sched[:, :, :], a["sched"]).then_inc(s_sched, 16)
            loads = [
                (w_n2m[:, :, :], a["w_n2m"]), (w_qkvs[:, :], a["w_qkvs"]), (w_edge[:, :], a["w_edge"]),
                (w_et[:, :], a["w_et"]), (w_m2n[:, :], a["w_m2n"]), (w_q1[:, :, :], a["w_q1"]), (b_q1[:, :], a["b_q1"]),
                (w_k1t[:, :, :], a["w_k1t"]), (w_v1[:, :, :], a["w_v1"]), (w_s1[:, :, :], a["w_s1"]),
                (w_f1[:, :, :], a["w_f1"]), (b_f1[:, :], a["b_f1"]), (w_f2[:, :, :], a["w_f2"]),
                (b_qkvs[:, :], a["b_qkvs"].partition_broadcast(P)),
                (w_beta[:, :, :].rearrange("p k n -> p (k n)"), a["w_beta"].partition_broadcast(P)),
                (rows1[:, :, :].rearrange("p k n -> p (k n)"), a["rows1"].partition_broadcast(P)),
                (we_be[:, :], a["we_be"].partition_broadcast(P)),
            ]
            for dst, src in loads:
                sp.dma_start(dst, src).then_inc(s_w, 16)
            assert len(loads) == N_WEIGHTS

            def node0(k):
                for b in range(U):
                    w = k * U + b
                    wait(n0["m"], w - U + 1)
                    sp.dma_start(nx[b][:, :, :], a["xT"][:, :, bass.ds(w * P, P)]).then_inc(n0["load"][b], 16)
                for b in range(U):
                    w = k * U + b
                    wait(n0["res"], w + 1)
                    sp.dma_start(node_rows(kv_d, w), nres[b][:, 0:2 * DM]).then_inc(n0["store"][b], 16)
                    sp.dma_start(window(q0_d, w), nq[b][:, :, 0:DM]).then_inc(n0["store"][b], 16)
                    sp.dma_start(window(xr_d, w), nxr[b][:, :]).then_inc(n0["store"][b], 16)
            windows(sp, node0)
            for b in range(U):
                sp.wait_ge(n0["store"][b], 48 * (NW // U))
            for n in range(2):
                sp.wait_ge(s_zst, 16 * 2 * NW)
            sp.wait_ge(s_tab, 1)
            end_phase(sp, 1)

            def edge_loads(L):
                s = L.s

                def load_idx(c, par):
                    for st in range(CH):
                        b, n = st % 2, CH // 2 * c + st // 2
                        wait(s["ld_idx"][b], 16 * n)
                        if st == 0:
                            wait(s["below"], c - 1)
                            wait(s["go"], CH * (c - 1))
                            wait(s["gathered"][0], 64 * (CH // 2) * (c - 1))
                            wait(s["gathered"][1], 64 * (CH // 2) * (c - 1))
                        t = sp.value_load(tw_int[0:1, 0, bass.ds(CH * c + st, 1)], min_val=0, max_val=NS - 1)
                        sp.dma_start(idx[par][:, st, :], a["idx"][bass.ds(t, 1)].rearrange("o p c -> (o p) c"))\
                          .then_inc(s["ld_idx"][b], 16)

                def load_rows(c, par):
                    for st in range(CH):
                        g, b = CH * c + st, st % 2
                        t = sp.value_load(tw_int[0:1, 0, bass.ds(g, 1)], min_val=0, max_val=NS - 1)
                        w = sp.value_load(tw_int[0:1, 1, bass.ds(g, 1)], min_val=0, max_val=NW - 1)
                        wait(s["oht"], g - 1)
                        sp.dma_start(dst_row[b][:, :], a["dst_row"][bass.ds(t, 1), :].partition_broadcast(P))\
                          .then_inc(s["ld_row"][b], 16)
                        wait(s["q"], g - 1)
                        sp.dma_start(qw[b][:, :, 0:L.QD], window(L.q_d, w).rearrange("p (k n) -> p k n", k=3))\
                          .then_inc(s["ld_q"][b], 16)
                        if L is L0:
                            wait(s["e"], g - 1)
                            sp.dma_start(ea[b][:, :], a["eaT"][:, bass.ds(t * SUPER, SUPER)])\
                              .then_inc(s["ld_ea"][b], 16)
                        else:
                            if st == 0:
                                wait(s["masked"], c - 1)
                            wait(s["ld_ea"][b], 16 * (CH // 2 * c + st // 2))
                            sp.dma_start(ew[par][:, st * JT:(st + 1) * JT],
                                         a["ew"][bass.ds(t, 1)].rearrange("o p c -> (o p) c"))\
                              .then_inc(s["ld_ea"][b], 16)

                def emit(c, par):
                    if isinstance(c, int) and c == 0:
                        load_idx(0, 0)
                    if not (isinstance(c, int) and c == NC - 1):
                        load_idx(c + 1, 1 - par)
                    load_rows(c, par)
                chunks(sp, emit)
                for b in range(2):
                    sp.wait_ge(s["stored"][b], 16 * NPAIR // 2)

            edge_loads(L0)
            end_phase(sp, 2)

            def node1(k):
                for b in range(U):
                    w = k * U + b
                    wait(n1["x1"], w - U + 1)
                    sp.dma_start(nacc[b][:, 0:L0.AW], window(acc0_d, w)).then_inc(n1["load"][b], 16)
                    sp.dma_start(nxr[b][:, :], window(xr_d, w)).then_inc(n1["load"][b], 16)
                    sp.dma_start(nrow[b][:, :], node_rows(a["x"], w)).then_inc(n1["load"][b], 16)
                for b in range(U):
                    w = k * U + b
                    wait(n1["x1"], w + 1)
                    sp.dma_start(node_rows(x1_d, w), nres[b][:, 0:D]).then_inc(n1["store"][b], 16)
                    wait(n1["split"], w + 1)
                    sp.dma_start(window(q1_d, w).rearrange("p (k n) -> p k n", k=3), nq[b][:, :, :])\
                      .then_inc(n1["store"][b], 16)
            windows(sp, node1)
            for b in range(U):
                sp.wait_ge(n1["store"][b], 32 * (NW // U))
            end_phase(sp, 3)

            edge_loads(L1)
            end_phase(sp, 4)

            def node2(k):
                for b in range(U):
                    w = k * U + b
                    wait(n2["x2"], w - U + 1)
                    sp.dma_start(nacc[b][:, :], window(acc1_d, w)).then_inc(n2["load"][b], 16)
                    wait(n2["res"], w - U + 1)
                    sp.dma_start(nrow[b][:, :], node_rows(x1_d, w)).then_inc(n2["load"][b], 16)
                for b in range(U):
                    w = k * U + b
                    wait(n2["res"], w + 1)
                    sp.dma_start(node_rows(out, w), nres[b][:, 0:D]).then_inc(n2["store"][b], 16)
            windows(sp, node2)
            for b in range(U):
                sp.wait_ge(n2["store"][b], 16 * (NW // U))

        @block.gpsimd
        def _(pool):
            pool.iota(iota_row[:, :], [[1, P]], base=0, channel_multiplier=0, allow_small_or_imprecise_dtypes=True)
            pool.iota(iota_col[:, :], [[0, 1]], base=0, channel_multiplier=1, allow_small_or_imprecise_dtypes=True)
            pool.iota(pair_no[:, :], [[1, NPAIR]], base=0, channel_multiplier=0, allow_small_or_imprecise_dtypes=True)
            for h in (HEADS, 1):
                pool.memset(sel_j[h][:, :], 1.0)
                pool.memset(sel_h[h][:, :], 0.0)
                pool.memset(sel_ht[h][:, :], 0.0)
            pool.memset(minus_half[:, :], -0.5)
            pool.memset(pen_r[:, :], 0.0)
            pool.memset(runs[:, :, :], -BIG)
            for b in range(2):
                pool.memset(run_f[b][:, :], -BIG)
                pool.memset(acc[b][:, :], 0.0)
            pool.memset(run_b[:, :], -BIG)
            pool.memset(zero_rows[:, :], 0.0).then_inc(s_zero, 1)
            pool.drain()
            for h in (HEADS, 1):
                pool.affine_select(out=sel_j[h][:, :], in_=sel_j[h][:, :], compare_op=ALU.is_ge, fill=0.0, base=0,
                                   pattern=[[-h, NI]], channel_multiplier=1)
                for m in range(P // h):
                    pool.affine_select(out=sel_h[h][:, :], in_=sel_h[h][:, :], compare_op=ALU.not_equal, fill=1.0,
                                       base=-h * m, pattern=[[-1, h]], channel_multiplier=1) if h > 1 else None
                    pool.drain() if h > 1 else None
            pool.memset(sel_h[1][:, :], 1.0)
            pool.memset(sel_ht[1][:, :], 1.0)
            v = sel_ht[HEADS][:, :].rearrange("p (m c) -> p m c", c=HEADS)
            pool.affine_select(out=v, in_=v, compare_op=ALU.not_equal, fill=1.0, base=0,
                               pattern=[[0, P // HEADS], [-1, HEADS]], channel_multiplier=1)
            pool.drain()
            for h in (HEADS, 1):
                pool.affine_select(out=sel_j[h][:, :], in_=sel_j[h][:, :], compare_op=ALU.is_ge, fill=0.0, base=h - 1,
                                   pattern=[[h, NI]], channel_multiplier=-1)
            pool.drain().then_inc(s_iota, 1)
            for w in range(NW):
                pool.dma_start(acc0_d[w], zero_rows[:, 0:L0.AW]).then_inc(s_zst, 16)
                pool.dma_start(acc1_d[w], zero_rows[:, 0:L1.AW]).then_inc(s_zst, 16)
            end_phase(pool, 1)

            def gathers(L):
                s = L.s

                def emit(c, par):
                    for st in range(CH):
                        b, n = st % 2, CH // 2 * c + st // 2
                        pool.wait_ge(s["ld_idx"][b], 16 * (n + 1))
                        after(pool, s["agg"], CH * (c - 2) + st + 1)
                        after(pool, s["gathered"][b], 64 * n)
                        pool.sem_inc(s["go"], 1)
                        for j in range(JT):
                            pool.indirect_dma_start(
                                out=rows[par][:, st, j, :], out_offset=None, in_=L.table,
                                in_offset=bass.IndirectOffsetOnAxis(ap=idx[par][:, st, j:j + 1], axis=0))\
                                .then_inc(s["gathered"][b], 16)
                chunks(pool, emit)

            def root(n, k, count):
                for b in range(U):
                    pool.wait_ge(n["var"], count(k, b))
                    pool.tensor_tensor(nrs[b][:, :], nve[b][:, :], minus_half[:, :], ALU.pow).then_inc(n["rstd"], 1)

            gathers(L0)
            end_phase(pool, 2)
            windows(pool, lambda k: root(n1, k, lambda k, b: U * k + b + 1))
            end_phase(pool, 3)
            gathers(L1)
            end_phase(pool, 4)

            def roots(k):
                for r in range(3):
                    root(n2, k, lambda k, b: 3 * U * k + r * U + b + 1)
            windows(pool, roots)

        @block.scalar
        def _(act):
            gate = sem("act_gate")

            def wait(s, value):
                stand_by(act, gate, s, value)

            act.wait_ge(s_wcp, 1)
            act.activation(w_c[:, :], ps[0:DR, 7, 0:DM], ACT.Copy).then_inc(s_wc, 1)

            def node0(k):
                for b in range(U):
                    wait(n0["m"], U * k + b + 1)
                    wait(n0["big"], U * (k - 1) + b + 1)
                    act.activation(nT[b][:, 0, :], ps[:, 4 * b, 0:P], ACT.Copy).then_inc(n0["mT"], 1)
            windows(act, node0)
            end_phase(act, 1)

            def edge(L):
                s = L.s

                def emit(c, par):
                    wait(s["turned"], c + 1)
                    act.activation(pen_r[0:L.R, 0:P], turn_ps[0:L.R, P:2 * P], ACT.Copy).then_inc(s["pens"], 1)
                    wait(s["below"], c + 1)
                    wait(s["agg"], CH * (c - 1))
                    act.activation(prob[par][:, :, 0:L.H], below[:, 0:L.R].rearrange("p (n h) -> p n h", h=L.H), ACT.Exp)\
                       .then_inc(s["prob"], 1)
                    wait(s["shrink_in"], c + 1)
                    act.activation(shrink[0:L.H, :], shrink_in[0:L.H, :], ACT.Exp).then_inc(s["shrink"], 1)
                    act.drain()
                    for st in range(CH):
                        g, b = CH * c + st, st % 2
                        wait(s["agg"], g - 1)
                        pr = prob[par][:, st * JT:(st + 1) * JT, 0:L.H]
                        if L is L0:
                            act.activation(msg[b][:, :, 0:L.AW].rearrange("p j (h c) -> p j h c", h=HEADS)[:, :, :, OUTC],
                                           pr, ACT.Copy).then_inc(s["msgp"], 1)
                        else:
                            for j in range(JT):
                                act.activation(msg[b][:, j, 0:D], rows[par][:, st, j, :], ACT.Copy, scale=pr[:, j, :])
                            act.activation(msg[b][:, :, D:D + 1], pr, ACT.Copy).then_inc(s["msgp"], 1)
                        if st > 0:
                            store(c, st - 1)
                    store(c, CH - 1)

                def store(c, st):
                    g, b = CH * c + st, st % 2
                    w = act.value_load(tw_int[0:1, 1, bass.ds(g, 1)], min_val=0, max_val=NW - 1)
                    after(act, s["acc"], g + 1)
                    after(act, s["stored"][1 - b], 16 * (CH // 2 * c + (st + 1) // 2))
                    act.dma_start(window(L.acc_d, w), acc[b][:, 0:L.AW]).then_inc(s["stored"][b], 16)
                chunks(act, emit)

            edge(L0)
            end_phase(act, 2)

            def node1(k):
                for b in range(U):
                    wait(n1["z"], U * k + b + 1)
                    act.activation(nz[b][:, 3:4], nz[b][:, 2:3], ACT.Exp, scale=-1.0).then_inc(n1["en"], 1)
                for b in range(U):
                    wait(n1["tp"], U * k + b + 1)
                    act.activation(nT[b][:, 0, :], ps[:, 4 * b, 0:P], ACT.Copy).then_inc(n1["tc"], 1)
                for b in range(U):
                    wait(n1["xt"], U * k + b + 1)
                    act.activation(nT[b][:, 2:4, :], ps[:, 4 * b, 0:2 * P].rearrange("p (k n) -> p k n", k=2), ACT.Copy)\
                       .then_inc(n1["xc"], 1)
                for b in range(U):
                    wait(n1["q"], U * k + b + 1)
                    for m in range(2):
                        i = act.activation(nT2[b][:, m, :], ps[:, 4 * b + 2, m * P:(m + 1) * P], ACT.Identity,
                                           bias=b_q1[:, m:m + 1])
                    i.then_inc(n1["qc"], 1)
            windows(act, node1)
            end_phase(act, 3)
            edge(L1)
            end_phase(act, 4)

            def node2(k):
                for b in range(U):
                    wait(n2["tp"], U * k + b + 1)
                    act.activation(nT[b][:, :, :], ps[:, 4 * b, :].rearrange("p (k n) -> p k n", k=4), ACT.Copy)\
                       .then_inc(n2["tc"], 1)
                for b in range(U):
                    wait(n2["xt"], U * k + b + 1)
                    act.activation(nT[b][:, 0:2, :], ps[:, 4 * b, 0:2 * P].rearrange("p (k n) -> p k n", k=2), ACT.Copy)\
                       .then_inc(n2["xc"], 1)
                for b in range(U):
                    wait(n2["u"], U * k + b + 1)
                    for m in range(4):
                        i = act.activation(nT2[b][:, m, :], ps[:, 4 * b + 2, m * P:(m + 1) * P], ACT.Gelu_apprx_tanh,
                                           bias=b_f1[:, m:m + 1])
                    i.then_inc(n2["g"], 1)
            windows(act, node2)

        @block.vector
        def _(v):
            v.wait_ge(s_iota, 1)
            v.tensor_scalar(ident[:, :], iota_row[:, :], iota_col[:, 0:1], None, ALU.is_equal)
            v.tensor_scalar(tri[:, :], iota_row[:, :], iota_col[:, 0:1], None, ALU.is_gt)
            v.memset(ones[:, :], 1.0)
            v.drain().then_inc(s_cst, 1)
            v.wait_ge(s_sched, 16)
            v.tensor_scalar(sched_w[:, :, :], sched[:, :, :], 7, None, ALU.arith_shift_right)
            v.drain()
            v.tensor_copy(sched_f[:, :, :], sched_w[:, :, :])
            v.drain()
            v.tensor_tensor(n_win[:, :], sched_f[:, :, 1], sched_f[:, :, 0], ALU.subtract)
            v.tensor_tensor(d_win[:, :], sched_f[:, :, 0], sched_f[:, :, 2], ALU.subtract)
            v.drain()
            v.tensor_scalar(n_win[:, :], n_win[:, :], 1.0, None, ALU.add)
            v.tensor_scalar(d_win[:, :], d_win[:, :], -1.0, None, ALU.add)
            v.drain().then_inc(s_win, 1)
            v.wait_ge(s_start, 1)
            v.tensor_copy(start[:, :], ps[:, 0, 0:SG])
            v.drain()
            for gcol in range(SG):
                v.tensor_scalar(begun[:, gcol, :], pair_no[:, :], start[:, gcol:gcol + 1], None, ALU.is_ge)
                v.tensor_scalar(stepped[:, gcol, :], pair_no[:, :], start[:, gcol:gcol + 1], d_win[:, gcol:gcol + 1],
                                ALU.is_ge, ALU.mult)
            v.drain().then_inc(s_begun, 1)
            v.wait_ge(s_pairs, 1)
            v.tensor_scalar(t_of[:, :], ps[:, 1, 0:NPAIR], -1.0, float(NS - 1), ALU.add, ALU.min)
            v.tensor_tensor(w_of[:, :], pair_no[:, :], ps[:, 2, 0:NPAIR], ALU.add)
            v.drain()
            v.tensor_scalar(w_of[:, :], w_of[:, :], float(NW - 1), None, ALU.min)
            v.drain()
            v.tensor_copy(tw_int[0:1, 0, :], t_of[0:1, :])
            v.tensor_copy(tw_int[0:1, 1, :], w_of[0:1, :])
            v.tensor_scalar(base_tab[:, :], w_of[:, :], float(P), None, ALU.mult)
            v.tensor_scalar(node_tab[:, :], w_of[:, :], float(P), iota_col[:, 0:1], ALU.mult, ALU.add)
            v.memset(keep_tab[:, 0:1], 0.0)
            v.tensor_tensor(keep_tab[:, 1:NPAIR], w_of[:, 1:NPAIR], w_of[:, 0:NPAIR - 1], ALU.is_equal)
            v.drain().then_inc(s_tab, 1)

            def split(b, n, src, scale):
                v.tensor_scalar(nq[b][:, 0, 0:n], src, scale, None, ALU.mult)
                v.drain()
                v.scalar_tensor_tensor(nsum[b][:, 0:n], src, scale, nq[b][:, 0, 0:n], ALU.mult, ALU.subtract)
                v.drain()
                v.tensor_copy(nq[b][:, 1, 0:n], nsum[b][:, 0:n])
                v.drain()
                return v.tensor_tensor(nq[b][:, 2, 0:n], nsum[b][:, 0:n], nq[b][:, 1, 0:n], ALU.subtract)

            v.wait_ge(s_w, 16 * N_WEIGHTS)

            def node0(k):
                for b in range(U):
                    v.wait_ge(n0["big"], U * k + b + 1)
                    after(v, n0["store"][b], 48 * k)
                    v.tensor_tensor(nbig[b][:, :], ps[:, 4 * b + 1, :], b_qkvs[:, :], ALU.add)
                    v.drain()
                    v.tensor_copy(nres[b][:, 0:2 * DM], nbig[b][:, DM:3 * DM])
                    v.tensor_copy(nxr[b][:, :], nbig[b][:, 3 * DM:4 * DM])
                    split(b, DM, nbig[b][:, 0:DM], OUTC ** -0.5)
                    v.drain().then_inc(n0["res"], 1)
            windows(v, node0)
            end_phase(v, 1)

            def edge(L):
                s, H, R = L.s, L.H, L.R

                def front(c, par, st):
                    g, b, n = CH * c + st, st % 2, CH // 2 * c + st // 2
                    v.wait_ge(s["ld_row"][b], 16 * (n + 1))
                    after(v, s["q"], g - 1)
                    v.tensor_scalar(oht[b][:, :], dst_row[b][:, :], node_tab[:, bass.ds(g, 1)], None, ALU.is_equal)
                    if st == 0:
                        v.tensor_tensor(rel_first[par][0:H, :], dst_row[b][0:H, 0:1], base_tab[0:H, bass.ds(g, 1)],
                                        ALU.subtract)
                    v.drain().then_inc(s["oht"], 1)
                    v.wait_ge(s["gathered"][b], 64 * (n + 1))
                    if L is L0:
                        v.wait_ge(s["e"], g + 1)
                        for m in range(2):
                            kv = rows[par][:, st, :, m * DM:(m + 1) * DM]
                            v.tensor_tensor(kv, kv, e_ps(b).rearrange("p (j n) -> p j n", j=JT), ALU.add)
                        v.drain()
                        v.wait_ge(s["q"], g + 1)
                        v.tensor_tensor(prod[:, :, 0:DM], rows[par][:, st, :, 0:DM],
                                        q_ps(L, b).rearrange("p (j n) -> p j n", j=JT), ALU.mult)
                        v.drain()
                        v.tensor_reduce(score[par][:, st * JT:(st + 1) * JT, :],
                                        prod[:, :, 0:DM].rearrange("p j (h n) -> p j h n", h=HEADS), AX.X, ALU.add)\
                         .then_inc(s["score"], 1)
                    else:
                        v.wait_ge(s["q"], g + 1)
                        for j in range(JT):
                            i = v.tensor_tensor_reduce(
                                out=prod[:, j, :], in0=rows[par][:, st, j, :], in1=q_ps(L, b)[:, j * D:(j + 1) * D],
                                scale=1.0, scalar=qb_ps[b][:, j:j + 1], op0=ALU.mult, op1=ALU.add,
                                accum_out=score[par][:, st * JT + j, 0:1])
                        i.then_inc(s["score"], 1)

                def maxima(c, par):
                    for b in range(2):
                        v.wait_ge(s["ld_idx"][b], 16 * (CH // 2) * (c + 1))
                    dst = idx[par][:, :, JT:2 * JT]
                    before = idx[par][:, :, 2 * JT:3 * JT]
                    relc = rel[par][:, :, :]
                    flat = relc.rearrange("p s j -> p (s j)")
                    after(v, s["agg"], CH * (c - 1))
                    v.tensor_tensor(relc, dst, base_tab[:, bass.ds(CH * c, CH)].unsqueeze(2).to_broadcast([P, CH, JT]),
                                    ALU.subtract)
                    v.tensor_tensor(same[:, :].rearrange("p (s j) -> p s j", j=JT), dst, before, ALU.is_equal)
                    v.drain()
                    after(v, s["turned"], c)
                    v.tensor_scalar(pen[:, :, 0:H], same[:, :].unsqueeze(2).to_broadcast([P, NI, H]), -1.0, BIG,
                                    ALU.add, ALU.mult)
                    v.tensor_scalar(inside[:, :], flat, 0.0, None, ALU.is_ge)
                    v.drain()
                    v.scalar_tensor_tensor(inside[:, :], flat, float(P), inside[:, :], ALU.is_lt, ALU.mult)
                    v.drain()
                    v.tensor_scalar(outside[:, :], inside[:, :], -1.0, BIG, ALU.add, ALU.mult)
                    sc = score[par][:, :, 0:H]
                    if L is L1:
                        for b in range(2):
                            v.wait_ge(s["ld_ea"][b], 16 * (CH // 2) * (c + 1))
                        v.tensor_scalar(same[:, :], ew[par][:, :], we_be[:, 0:1], we_be[:, 1:2], ALU.mult, ALU.add)
                        v.drain()
                        v.tensor_tensor(outside[:, :], outside[:, :], same[:, :], ALU.add)
                    v.drain()
                    v.tensor_tensor(biased[:, :, 0:H], sc, outside[:, :].unsqueeze(2).to_broadcast([P, NI, H]), ALU.add)
                    v.drain().then_inc(s["masked"], 1)
                    v.wait_ge(s["turned"], c + 1)
                    v.wait_ge(s["pens"], c + 1)
                    sT = turn_ps[0:R, 0:P]
                    pf, pb = pen_r[0:R, 0:P], pen_r[0:R, 1:P + 1]
                    v.tensor_tensor_scan(fwd[0:R, :], pf, sT, -BIG, ALU.add, ALU.max)
                    v.tensor_tensor_scan(bwd[0:R, ::-1], pb[:, ::-1], sT[:, ::-1], -BIG, ALU.add, ALU.max)
                    v.tensor_reduce(carry_r[0:R, 0:1], pen_r[0:R, 1:P], AX.X, ALU.min)
                    v.drain()
                    ends = (fwd[0:R, P - 1:P], bwd[0:R, 0:1], pen_r[0:R, 0:1], carry_r[0:R, 0:1])
                    for m, col in enumerate(ends):
                        v.tensor_scalar(spread[0:R, m, :], sel_j[H][0:R, :], col, None, ALU.mult)
                    v.drain().then_inc(s["ends"], 1)
                    v.wait_ge(s["arranged"], c + 1)
                    v.tensor_copy(runs[0:H, :, 0:NI], arr_ps[0:H, :].rearrange("p (m n) -> p m n", m=4))
                    v.tensor_copy(run_f[par][0:H, 0:1], run_f[1 - par][0:H, NI:NI + 1])
                    v.drain()
                    v.tensor_tensor(pen_f[0:H, :], runs[0:H, 2, 0:NI], runs[0:H, 3, 0:NI], ALU.add)
                    v.tensor_tensor(pen_b[0:H, :], runs[0:H, 2, 1:NI + 1], runs[0:H, 3, 0:NI], ALU.add)
                    v.drain()
                    v.tensor_tensor_scan(run_f[par][0:H, 1:NI + 1], pen_f[0:H, :], runs[0:H, 0, 0:NI],
                                         run_f[par][0:H, 0:1], ALU.add, ALU.max)
                    v.tensor_tensor_scan(run_b[0:H, 0:NI][:, ::-1], pen_b[0:H, ::-1], runs[0:H, 1, 0:NI][:, ::-1],
                                         -BIG, ALU.add, ALU.max)
                    v.drain()
                    v.tensor_copy(carry[0:H, 0, :], run_f[par][0:H, 0:NI])
                    v.tensor_tensor(carry[0:H, 1, :], run_b[0:H, 1:NI + 1], runs[0:H, 2, 1:NI + 1], ALU.add)
                    v.drain().then_inc(s["carries"], 1)
                    v.wait_ge(s["spreadback"], c + 1)
                    v.tensor_tensor(carry_p[0:R, :, :], back_ps[0:R, :].rearrange("p (m n) -> p m n", m=2),
                                    sel_j[H][0:R, :].unsqueeze(1).to_broadcast([R, 2, NI]), ALU.mult)
                    v.drain()
                    v.tensor_reduce(carry_r[0:R, :], carry_p[0:R, :, :], AX.X, ALU.add)
                    v.drain()
                    v.tensor_tensor_scan(fwd[0:R, :], pf, sT, carry_r[0:R, 0:1], ALU.add, ALU.max)
                    v.drain()
                    v.tensor_tensor_scan(full[0:R, ::-1], pb[:, ::-1], fwd[0:R, ::-1], carry_r[0:R, 1:2],
                                         ALU.add, ALU.max)
                    v.drain().then_inc(s["full"], 1)
                    v.tensor_scalar(shrink_in[0:H, :], run_f[par][0:H, 0:1], full[0:H, 0:1], 0.0, ALU.subtract, ALU.min)\
                     .then_inc(s["shrink_in"], 1)
                    v.tensor_scalar(first_oh[0:H, :], iota_row[0:H, :], rel_first[par][0:H, 0:1], None, ALU.is_equal)
                    v.wait_ge(s["fullT"], c + 1)
                    v.tensor_tensor(below[:, 0:R], biased[:, :, 0:H].rearrange("p n h -> p (n h)") if H == HEADS else
                                    biased[:, :, 0], turn_ps[:, 2 * P:2 * P + R], ALU.subtract).then_inc(s["below"], 1)
                    v.wait_ge(s["shrink"], c + 1)
                    v.scalar_tensor_tensor(shrink_d[0:H, 0:H], ident[0:H, 0:H], shrink[0:H, 0:1], ident[0:H, 0:H],
                                           ALU.mult, ALU.subtract)
                    v.drain().then_inc(s["so_in"], 1)

                def back(c, par, st):
                    g, b = CH * c + st, st % 2
                    after(v, s["agg"], g - 1)
                    for j in range(JT):
                        v.tensor_scalar(oh[b][:, j, :], iota_row[:, :], rel[par][:, st, j:j + 1], None, ALU.is_equal)
                    if L is L0:
                        v.wait_ge(s["prob"], c + 1)
                        m = msg[b][:, :, 0:L.AW].rearrange("p j (h c) -> p j h c", h=HEADS)[:, :, :, 0:OUTC]
                        v.tensor_tensor(m, rows[par][:, st, :, DM:2 * DM].rearrange("p j (h c) -> p j h c", h=HEADS),
                                        prob[par][:, st * JT:(st + 1) * JT, :].unsqueeze(3)
                                        .to_broadcast([P, JT, HEADS, OUTC]), ALU.mult)
                    v.drain().then_inc(s["msg"], 1)
                    old = acc[1 - b]
                    if st == 0:
                        v.wait_ge(s["so"], c + 1)
                        v.tensor_scalar(rescale[:, 0:H], so_ps[:, 0:H], 1.0, None, ALU.add)
                        v.drain()
                        v.tensor_tensor(acc_scaled[:, 0:L.AW].rearrange("p (h c) -> p h c", h=H),
                                        acc[1 - b][:, 0:L.AW].rearrange("p (h c) -> p h c", h=H),
                                        rescale[:, 0:H].unsqueeze(2).to_broadcast([P, H, L.AW // H]), ALU.mult)
                        v.drain()
                        old = acc_scaled
                    v.wait_ge(s["agg"], g + 1)
                    after(v, s["stored"][b], 16 * (CH // 2 * c + st // 2))
                    v.scalar_tensor_tensor(acc[b][:, 0:L.AW], old[:, 0:L.AW], keep_tab[:, bass.ds(g, 1)], agg_ps(L, b),
                                           ALU.mult, ALU.add)
                    v.drain().then_inc(s["acc"], 1)

                def emit(c, par):
                    for st in range(CH):
                        front(c, par, st)
                    v.drain()
                    maxima(c, par)
                    for st in range(CH):
                        back(c, par, st)
                chunks(v, emit)

            edge(L0)
            end_phase(v, 2)

            def moments(n, b):
                v.bn_stats(nst[b][:, :], nh[b][:, :])
                v.drain()
                v.bn_aggr(nmv[b][:, :], nst[b][:, :])
                v.drain()
                v.tensor_scalar(nve[b][:, :], nmv[b][:, 1:2], EPS, None, ALU.add).then_inc(n["var"], 1)

            def normal(out_, b):
                return v.tensor_scalar(out_, nh[b][:, :], nmv[b][:, 0:1], nrs[b][:, 0:1], ALU.subtract, ALU.mult)

            def node1(k):
                for b in range(U):
                    w = U * k + b
                    v.wait_ge(n1["load"][b], 48 * (k + 1))
                    sums = nacc[b][:, 0:L0.AW].rearrange("p (h c) -> p h c", h=HEADS)
                    v.tensor_scalar(nden[b][:, :], sums[:, :, OUTC], 1e-16, None, ALU.add)
                    v.drain()
                    v.reciprocal(nden[b][:, :], nden[b][:, :])
                    v.drain()
                    o, t = nsum[b][:, 0:DM], nbig[b][:, 0:DM]
                    v.tensor_tensor(o.rearrange("p (h c) -> p h c", h=HEADS), sums[:, :, 0:OUTC],
                                    nden[b][:, :].unsqueeze(2).to_broadcast([P, HEADS, OUTC]), ALU.mult)
                    v.drain()
                    v.tensor_tensor(t, o, nxr[b][:, :], ALU.subtract)
                    v.drain()
                    z = 0.0
                    for m, part in enumerate((o, nxr[b][:, :], t)):
                        v.tensor_tensor_reduce(out=nbig[b][:, DM:2 * DM], in0=part, in1=w_beta[:, m, :], scale=1.0,
                                               scalar=z, op0=ALU.mult, op1=ALU.add, accum_out=nz[b][:, m:m + 1])
                        v.drain()
                        z = nz[b][:, m:m + 1]
                    v.drain().then_inc(n1["z"], 1)
                for b in range(U):
                    v.wait_ge(n1["en"], U * k + b + 1)
                    v.tensor_scalar(nz[b][:, 4:5], nz[b][:, 3:4], 1.0, None, ALU.add)
                    v.drain()
                    v.reciprocal(nz[b][:, 5:6], nz[b][:, 4:5])
                    v.drain()
                    v.tensor_scalar(nz[b][:, 6:7], nz[b][:, 5:6], -1.0, None, ALU.mult)
                    v.drain()
                    v.scalar_tensor_tensor(nbig[b][:, DM:2 * DM], nbig[b][:, 0:DM], nz[b][:, 6:7], nsum[b][:, 0:DM],
                                           ALU.mult, ALU.add).then_inc(n1["mix"], 1)
                for b in range(U):
                    v.wait_ge(n1["y"], U * k + b + 1)
                    v.tensor_tensor(nh[b][:, :], nrow[b][:, :], ps[:, 4 * b + 1, 0:D], ALU.add)
                    v.drain()
                    moments(n1, b)
                for b in range(U):
                    v.wait_ge(n1["rstd"], U * k + b + 1)
                    after(v, n1["store"][b], 32 * k)
                    normal(nres[b][:, 0:D], b)
                    v.drain().then_inc(n1["x1"], 1)
                for b in range(U):
                    v.wait_ge(n1["qk"], U * k + b + 1)
                    split(b, D + 1, ps[:, 4 * b + 3, 0:D + 1], D ** -0.5)
                    v.drain().then_inc(n1["split"], 1)
            windows(v, node1)
            end_phase(v, 3)

            edge(L1)
            end_phase(v, 4)

            def node2(k):
                for b in range(U):
                    v.wait_ge(n2["load"][b], 32 * (k + 1))
                    v.tensor_scalar(nden[b][:, 0:1], nacc[b][:, D:D + 1], 1e-12, None, ALU.max)
                    v.drain()
                    v.reciprocal(nden[b][:, 1:2], nden[b][:, 0:1])
                    v.drain()
                    v.tensor_scalar(nsum[b][:, :], nacc[b][:, :], nden[b][:, 1:2], None, ALU.mult)
                    v.drain().then_inc(n2["mean"], 1)
                    v.tensor_tensor(nh2[b][:, :], nrow[b][:, :], rows1[:, BS, :], ALU.add)
                    v.drain()
                    v.scalar_tensor_tensor(nh2[b][:, :], rows1[:, BV, :], nsum[b][:, D:D + 1], nh2[b][:, :],
                                           ALU.mult, ALU.add)
                v.drain()

                def affine(out_, b, g, beta):
                    normal(out_, b)
                    v.drain()
                    v.tensor_tensor(out_, out_, rows1[:, g, :], ALU.mult)
                    v.drain()
                    v.tensor_tensor(out_, out_, rows1[:, beta, :], ALU.add)
                    v.drain()

                for b in range(U):
                    v.wait_ge(n2["lin"], U * k + b + 1)
                    v.tensor_tensor(nh[b][:, :], nh2[b][:, :], ps[:, 4 * b + 1, 0:D], ALU.add)
                    v.drain()
                    moments(n2, b)
                for b in range(U):
                    v.wait_ge(n2["rstd"], 3 * U * k + b + 1)
                    affine(nh2[b][:, :], b, G1, B1)
                    v.drain().then_inc(n2["x2"], 1)
                    v.tensor_tensor(nbig[b][:, 0:D], nh2[b][:, :], rows1[:, BF2, :], ALU.add)
                v.drain()
                for b in range(U):
                    v.wait_ge(n2["f"], U * k + b + 1)
                    v.tensor_tensor(nh[b][:, :], nbig[b][:, 0:D], ps[:, 4 * b + 3, 0:D], ALU.add)
                    v.drain()
                    moments(n2, b)
                for b in range(U):
                    v.wait_ge(n2["rstd"], 3 * U * k + U + b + 1)
                    affine(nh2[b][:, :], b, G2, B2)
                    v.tensor_tensor(nh[b][:, :], nh2[b][:, :], nrow[b][:, :], ALU.add)
                    v.drain()
                    moments(n2, b)
                for b in range(U):
                    v.wait_ge(n2["rstd"], 3 * U * k + 2 * U + b + 1)
                    after(v, n2["store"][b], 16 * k)
                    normal(nres[b][:, 0:D], b)
                    v.drain().then_inc(n2["res"], 1)
            windows(v, node2)

        @block.tensor
        def _(pe):
            gate = sem("pe_gate")

            def mm(out_, lhsT, rhs, first=True, last=True):
                return pe.matmul(out_, lhsT=lhsT, rhs=rhs, start=first, stop=last)

            pe.wait_ge(s_cst, 1)
            pe.wait_ge(s_win, 1)
            for gcol in range(SG):
                for m in range(gcol + 1):
                    i = mm(ps[:, 0, gcol:gcol + 1], tri[:, :] if m == gcol else ones[:, :], n_win[:, m:m + 1],
                           m == 0, m == gcol)
            i.then_inc(s_start, 1)
            pe.wait_ge(s_begun, 1)
            for bank, part in ((1, begun), (2, stepped)):
                for gcol in range(SG):
                    i = mm(ps[:, bank, 0:NPAIR], ones[:, :], part[:, gcol, :], gcol == 0, gcol == SG - 1)
            i.then_inc(s_pairs, 1)
            pe.wait_ge(s_w, 16 * N_WEIGHTS)
            mm(ps[0:DR, 7, 0:DM], w_edge[:, :], w_et[:, :]).then_inc(s_wcp, 1)
            pe.wait_ge(s_tab, 1)
            pe.wait_ge(s_wc, 1)

            def node0(k):
                for b in range(U):
                    pe.wait_ge(n0["load"][b], 16 * (k + 1))
                    after(pe, n0["mT"], U * (k - 1) + b + 1)
                    for m in range(2):
                        i = mm(ps[:, 4 * b, 0:P], w_n2m[:, m, :], nx[b][:, m, :], m == 0, m == 1)
                    i.then_inc(n0["m"], 1)
                for b in range(U):
                    pe.wait_ge(n0["mT"], U * k + b + 1)
                    after(pe, n0["res"], U * (k - 1) + b + 1)
                    mm(ps[:, 4 * b + 1, :], nT[b][:, 0, :], w_qkvs[:, :]).then_inc(n0["big"], 1)
            windows(pe, node0)
            end_phase(pe, 1)

            def edge(L):
                s, H, R = L.s, L.H, L.R

                def front(c, par, st):
                    g, b, n = CH * c + st, st % 2, CH // 2 * c + st // 2
                    after(pe, s["score"], g - 1)
                    if L is L0:
                        pe.wait_ge(s["ld_ea"][b], 16 * (n + 1))
                        for j in range(JT):
                            i = mm(e_ps(b)[:, j * DM:(j + 1) * DM], ea[b][:, j * P:(j + 1) * P], w_c[:, :])
                        i.then_inc(s["e"], 1)
                    pe.wait_ge(s["ld_q"][b], 16 * (n + 1))
                    pe.wait_ge(s["oht"], g + 1)
                    for j in range(JT):
                        for m in range(3):
                            i = mm(q_ps(L, b)[:, j * L.D:(j + 1) * L.D], oht[b][:, j * P:(j + 1) * P],
                                   qw[b][:, m, 0:L.D], m == 0, m == 2)
                        if L is L1:
                            for m in range(3):
                                i = mm(qb_ps[b][:, j:j + 1], oht[b][:, j * P:(j + 1) * P], qw[b][:, m, D:D + 1],
                                       m == 0, m == 2)
                    i.then_inc(s["q"], 1)

                def maxima(c, par):
                    stand_by(pe, gate, s["masked"], c + 1)
                    sc = biased[:, :, 0:H].rearrange("p n h -> p (n h)") if H == HEADS else biased[:, :, 0]
                    pn = pen[:, :, 0:H].rearrange("p n h -> p (n h)") if H == HEADS else pen[:, :, 0]
                    pe.transpose(turn_ps[0:R, 0:P], sc, ident[:, :])
                    pe.transpose(turn_ps[0:R, P:2 * P], pn, ident[:, :]).then_inc(s["turned"], 1)
                    stand_by(pe, gate, s["ends"], c + 1)
                    mm(arr_ps[0:H, :], sel_h[H][0:R, :], spread[0:R, :, :].rearrange("p m n -> p (m n)"))\
                        .then_inc(s["arranged"], 1)
                    stand_by(pe, gate, s["carries"], c + 1)
                    mm(back_ps[0:R, :], sel_ht[H][0:H, 0:R], carry[0:H, :, :].rearrange("p m n -> p (m n)"))\
                        .then_inc(s["spreadback"], 1)
                    stand_by(pe, gate, s["full"], c + 1)
                    pe.transpose(turn_ps[:, 2 * P:2 * P + R], full[0:R, :], ident[0:R, 0:R]).then_inc(s["fullT"], 1)
                    stand_by(pe, gate, s["so_in"], c + 1)
                    mm(so_ps[:, 0:H], first_oh[0:H, :], shrink_d[0:H, 0:H]).then_inc(s["so"], 1)

                def back(c, par, st):
                    g, b = CH * c + st, st % 2
                    pe.wait_ge(s["msg"], g + 1)
                    pe.wait_ge(s["msgp"], g + 1)
                    after(pe, s["acc"], g - 1)
                    for j in range(JT):
                        i = mm(agg_ps(L, b), oh[b][:, j, :], msg[b][:, j, 0:L.AW], j == 0, j == JT - 1)
                    i.then_inc(s["agg"], 1)

                def emit(c, par):
                    for st in range(CH):
                        front(c, par, st)
                    maxima(c, par)
                    for st in range(CH):
                        back(c, par, st)
                chunks(pe, emit)

            edge(L0)
            end_phase(pe, 2)

            def node1(k):
                for b in range(U):
                    pe.wait_ge(n1["mix"], U * k + b + 1)
                    pe.transpose(ps[:, 4 * b, 0:P], nbig[b][:, DM:2 * DM], ident[:, :]).then_inc(n1["tp"], 1)
                for b in range(U):
                    pe.wait_ge(n1["tc"], U * k + b + 1)
                    mm(ps[:, 4 * b + 1, 0:D], nT[b][:, 0, :], w_m2n[:, :]).then_inc(n1["y"], 1)
                for b in range(U):
                    pe.wait_ge(n1["x1"], U * k + b + 1)
                    for m in range(2):
                        i = pe.transpose(ps[:, 4 * b, m * P:(m + 1) * P], nres[b][:, m * P:(m + 1) * P], ident[:, :])
                    i.then_inc(n1["xt"], 1)
                for b in range(U):
                    pe.wait_ge(n1["xc"], U * k + b + 1)
                    for f in range(2):
                        for m in range(2):
                            i = mm(ps[:, 4 * b + 2, f * P:(f + 1) * P], w_q1[:, m, f * P:(f + 1) * P], nT[b][:, 2 + m, :],
                                   m == 0, m == 1)
                    i.then_inc(n1["q"], 1)
                for b in range(U):
                    pe.wait_ge(n1["qc"], U * k + b + 1)
                    after(pe, n1["split"], U * (k - 1) + b + 1)
                    for m in range(2):
                        i = mm(ps[:, 4 * b + 3, 0:D + 1], nT2[b][:, m, :], w_k1t[:, m, :], m == 0, m == 1)
                    i.then_inc(n1["qk"], 1)
            windows(pe, node1)
            end_phase(pe, 3)
            edge(L1)
            end_phase(pe, 4)

            def node2(k):
                for b in range(U):
                    pe.wait_ge(n2["mean"], U * k + b + 1)
                    for m in range(4):
                        src = nsum[b] if m < 2 else nrow[b]
                        i = pe.transpose(ps[:, 4 * b, m * P:(m + 1) * P], src[:, m % 2 * P:(m % 2 + 1) * P], ident[:, :])
                    i.then_inc(n2["tp"], 1)
                for b in range(U):
                    pe.wait_ge(n2["tc"], U * k + b + 1)
                    for m in range(4):
                        i = mm(ps[:, 4 * b + 1, 0:D], nT[b][:, m, :], (w_v1 if m < 2 else w_s1)[:, m % 2, :], m == 0, m == 3)
                    i.then_inc(n2["lin"], 1)
                for b in range(U):
                    pe.wait_ge(n2["x2"], U * k + b + 1)
                    for m in range(2):
                        i = pe.transpose(ps[:, 4 * b, m * P:(m + 1) * P], nh2[b][:, m * P:(m + 1) * P], ident[:, :])
                    i.then_inc(n2["xt"], 1)
                for b in range(U):
                    pe.wait_ge(n2["xc"], U * k + b + 1)
                    for f in range(4):
                        for m in range(2):
                            i = mm(ps[:, 4 * b + 2, f * P:(f + 1) * P], w_f1[:, m, f * P:(f + 1) * P], nT[b][:, m, :],
                                   m == 0, m == 1)
                    i.then_inc(n2["u"], 1)
                for b in range(U):
                    pe.wait_ge(n2["g"], U * k + b + 1)
                    for m in range(4):
                        i = mm(ps[:, 4 * b + 3, 0:D], nT2[b][:, m, :], w_f2[:, m, :], m == 0, m == 3)
                    i.then_inc(n2["f"], 1)
            windows(pe, node2)


N_WEIGHTS = 17


def kernel(x, src, dst, edge_attr_64, edge_weight, **w):
    import concourse.bacc as bacc
    from concourse.bass_utils import run_bass_kernel_spmd

    def arr(v):
        return np.asarray(v)

    def halves(m):
        m = arr(m)
        return m.reshape(-1, P, m.shape[1]).transpose(1, 0, 2)

    x, src, dst = arr(x), arr(src), arr(dst)
    xp = np.zeros((NP, D), x.dtype)
    xp[:N] = x

    def padded(v, fill):
        p = np.full((EP,) + v.shape[1:], fill, v.dtype)
        p[:E] = v
        return p

    def tiles(v):
        return v.reshape(NS, JT, P).transpose(0, 2, 1)

    dstp = padded(dst, NO_NODE)
    before = np.full(EP, -1, dst.dtype)
    before[1:] = dstp[:-1]
    behind = np.full(EP, -1, dst.dtype)
    behind[:-1] = dstp[1:]
    idx = np.concatenate([tiles(v) for v in (padded(src, 0), dstp, before, behind)], axis=2)
    sched = np.zeros((SG * P, 3), dst.dtype)
    sched[:, 1] = -P
    sched[:, 2] = -1
    lasts = [min(SUPER * (t + 1), E) - 1 for t in range(NS)]
    sched[:NS, 0] = dst[::SUPER]
    sched[:NS, 1] = dst[lasts]
    sched[1:NS, 2] = dst[lasts[:-1]]
    sched = sched.reshape(SG, P, 3).transpose(1, 0, 2)
    k1t = np.concatenate([arr(w["L1_gnn_wk"]).T, arr(w["L1_gnn_bk"])[:, None]], axis=1)

    arrays = {
        "xT": xp.T.reshape(2, P, NP).transpose(1, 0, 2), "x": xp, "idx": idx, "dst_row": dstp.reshape(NS, SUPER),
        "eaT": padded(arr(edge_attr_64), 0).T, "ew": tiles(padded(arr(edge_weight), 0)), "sched": sched,
        "w_n2m": halves(arr(w["L0_gnn_W_n2m"]).T),
        "w_qkvs": np.concatenate([arr(w["L0_gnn_" + n]).T for n in ("Wq", "Wk", "Wv", "Wskip")], axis=1),
        "b_qkvs": np.concatenate([arr(w["L0_gnn_" + n]) for n in ("bq", "bk", "bv", "bskip")])[None],
        "w_edge": arr(w["L0_gnn_W_edge"]), "w_et": arr(w["L0_gnn_We"]).T, "w_beta": arr(w["L0_gnn_Wbeta"]),
        "w_m2n": arr(w["L0_gnn_W_m2n"]).T, "w_q1": halves(w["L1_gnn_wq"]),
        "b_q1": arr(w["L1_gnn_bq"]).reshape(2, P).T, "w_k1t": halves(k1t), "w_v1": halves(w["L1_gnn_wv"]),
        "w_s1": halves(w["L1_gnn_ws"]), "w_f1": halves(w["L1_gnn_w_ff1"]), "b_f1": arr(w["L1_gnn_b_ff1"]).reshape(4, P).T,
        "w_f2": halves(w["L1_gnn_w_ff2"]),
        "rows1": np.concatenate([arr(w["L1_gnn_" + n]) for n in ("bv", "bs", "g1", "b1", "g2", "b2", "b_ff2")])[None],
        "we_be": np.concatenate([arr(w["L1_gnn_we"]).reshape(-1), arr(w["L1_gnn_be"])])[None],
    }
    arrays = {n: np.ascontiguousarray(v) for n, v in arrays.items()}
    nc = bacc.Bacc("TRN2", target_bir_lowering=False, num_devices=1)
    aps = {n: nc.dram_tensor("in_" + n, v.shape, mybir.dt.from_np(v.dtype), kind="ExternalInput").ap()
           for n, v in arrays.items()}
    out = nc.dram_tensor("out", (NP, D), F32, kind="ExternalOutput").ap()
    build(nc, aps, out)
    r = run_bass_kernel_spmd(nc, [{"in_" + n: v for n, v in arrays.items()}], core_ids=[0])
    return r.results[0]["out"][:N]
```

```python
from contextlib import ExitStack

import numpy as np
import concourse.bass as bass
from concourse import mybir

F32, BF16, I32 = mybir.dt.float32, mybir.dt.bfloat16, mybir.dt.int32
ALU = mybir.AluOpType
ACT = mybir.ActivationFunctionType
AX = mybir.AxisListType

P = 128
N, E, D = 6250, 200000, 256
DM, DR, HEADS = 128, 64, 4
OUTC = DM // HEADS
NW = 50
NP = NW * P
JT = 4
SUPER = JT * P
NS = -(-E // SUPER)
EP = NS * SUPER
REAL_W = -(-N // P)
CH = 8
NI = CH * JT
NC = -(-(NS + REAL_W - 1) // CH)
NPAIR = NC * CH
SG = -(-NS // P)
BIG = 1e30
SUMMED = ((), (), (0, 1), (2, 3), (4,), (5,), (6,), (7,))
NO_NODE = 1 << 20
U = 2
EPS = 1e-5


def after(eng, sem, value):
    if not (isinstance(value, int) and value <= 0):
        eng.wait_ge(sem, value)


def stand_by(eng, gate, sem, value):
    if isinstance(value, int):
        after(eng, sem, value)
    else:
        eng.wait_ge(sem, value)
        eng.sem_inc(gate, 1)


def build(nc, a, out):
    ctx = ExitStack()
    with ctx:
        def sb(name, shape, dt=F32):
            return ctx.enter_context(nc.sbuf_tensor(name, shape, dt))

        def sem(name):
            return ctx.enter_context(nc.semaphore(name))

        def dram(name, shape, dt=F32):
            return nc.dram_tensor(name, shape, dt, kind="Internal").ap()

        kv_d = dram("kv_d", (NP, 2 * DM))
        q0_d = dram("q0_d", (NW, P, 3 * DM), BF16)
        xr_d = dram("xr_d", (NW, P, DM))
        acc0_d = dram("acc0_d", (NW + NPAIR, P, DM + HEADS))
        x1_d = dram("x1_d", (NP, D))
        q1_d = dram("q1_d", (NW, P, 3 * (D + 1)), BF16)
        acc1_d = dram("acc1_d", (NW + NPAIR, P, D + 1))

        ident = sb("ident", [P, P])
        iota_row = sb("iota_row", [P, P])
        iota_col = sb("iota_col", [P, 1])
        ones = sb("ones", [P, P])
        tri = sb("tri", [P, P])
        sel_j = {4: sb("sel_j4", [P, NI]), 1: sb("sel_j1", [P, NI])}
        sel_h = {4: sb("sel_h4", [P, 4]), 1: sb("sel_h1", [P, 1])}
        sel_ht = {4: sb("sel_ht4", [4, P]), 1: sb("sel_ht1", [1, P])}
        minus_half = sb("minus_half", [P, 1])
        zero_rows = sb("zero_rows", [P, D + 1])
        w_n2m = sb("w_n2m", [P, 2, DM])
        w_qkvs = sb("w_qkvs", [P, 4 * DM])
        b_qkvs = sb("b_qkvs", [P, 4 * DM])
        w_edge = sb("w_edge", [DR, DR])
        w_et = sb("w_et", [DR, DM])
        w_c = sb("w_c", [P, DM])
        w_beta = sb("w_beta", [P, 3, DM])
        w_m2n = sb("w_m2n", [P, D])
        w_q1 = sb("w_q1", [P, 2, D])
        b_q1 = sb("b_q1", [P, 2])
        w_k1t = sb("w_k1t", [P, 2, D + 1])
        w_v1 = sb("w_v1", [P, 2, D])
        w_s1 = sb("w_s1", [P, 2, D])
        w_f1 = sb("w_f1", [P, 2, 2 * D])
        b_f1 = sb("b_f1", [P, 4])
        w_f2 = sb("w_f2", [P, 4, D])
        rows1 = sb("vecs1", [P, 7, D])
        we_be = sb("we_be", [P, 2])
        BV, BS, G1, B1, G2, B2, BF2 = range(7)
        sched = sb("sched", [P, SG, 3], I32)
        sched_w = sb("sched_w", [P, SG, 3], I32)
        sched_f = sb("sched_f", [P, SG, 3])
        n_win = sb("n_win", [P, SG])
        d_win = sb("d_win", [P, SG])
        start = sb("start", [P, SG])
        pair_no = sb("pair_no", [P, NPAIR])
        begun = sb("begun", [P, SG, NPAIR])
        stepped = sb("stepped", [P, SG, NPAIR])
        t_of = sb("t_of", [P, NPAIR])
        w_of = sb("w_of", [P, NPAIR])
        base_tab = sb("base_tab", [P, NPAIR])
        node_tab = sb("node_tab", [P, NPAIR])
        keep_tab = sb("keep_tab", [P, NPAIR])
        save_of = sb("save_of", [P, NPAIR])
        tw_int = sb("tw_int", [1, 3, NPAIR], I32)

        ps = ctx.enter_context(nc.psum_tensor("ps", [P, 8, 512], F32))

        idx = [sb(f"idx{b}", [P, CH, 4 * JT], I32) for b in range(2)]
        dst_row = [sb(f"dst_row{b}", [P, SUPER], I32) for b in range(2)]
        qw = [sb(f"qw{b}", [P, 3, D + 1], BF16) for b in range(2)]
        ea = [sb(f"ea{b}", [P, SUPER]) for b in range(2)]
        ew = [sb(f"ew{b}", [P, NI]) for b in range(2)]
        rows = [sb(f"rows{b}", [P, CH, JT, D]) for b in range(2)]
        oht = [sb(f"oht{b}", [P, SUPER], BF16) for b in range(2)]
        oh = [sb(f"oh{b}", [P, JT, P]) for b in range(2)]
        prod = sb("prod", [P, JT, D])
        score = [sb(f"score{b}", [P, NI, HEADS]) for b in range(2)]
        rel_first = [sb(f"rel_first{b}", [HEADS, 1]) for b in range(2)]
        rel = [sb(f"rel{b}", [P, CH, JT]) for b in range(2)]
        same = sb("same", [P, NI])
        qb = sb("qb", [P, NI])
        inside = sb("inside", [P, NI])
        outside = sb("outside", [P, NI])
        biased = sb("biased", [P, NI, HEADS])
        pen = sb("pen", [P, NI, HEADS])
        pen_r = sb("pen_r", [P, P + 1])
        fwd = sb("fwd", [P, P])
        bwd = sb("bwd", [P, P])
        full = sb("full", [P, P])
        spread = sb("spread", [P, 4, NI])
        runs = sb("runs", [HEADS, 4, NI + 1])
        pen_f = sb("pen_f", [HEADS, NI])
        pen_b = sb("pen_b", [HEADS, NI])
        run_f = [sb(f"run_f{b}", [HEADS, NI + 1]) for b in range(2)]
        run_b = sb("run_b", [HEADS, NI + 1])
        carry = sb("carry", [HEADS, 2, NI])
        carry_p = sb("carry_p", [P, 2, NI])
        carry_r = sb("carry_r", [P, 2])
        below = sb("below", [P, NI * HEADS])
        prob = [sb(f"prob{b}", [P, NI, HEADS]) for b in range(2)]
        shrink_in = sb("shrink_in", [HEADS, 1])
        shrink = sb("shrink", [HEADS, 1])
        shrink_d = sb("shrink_d", [HEADS, HEADS])
        first_oh = sb("first_oh", [HEADS, P])
        rescale = sb("rescale", [P, HEADS])
        msg = [sb(f"msg{b}", [P, JT, D + 1]) for b in range(2)]
        acc = [sb(f"acc{b}", [P, D + 1]) for b in range(2)]
        acc_scaled = sb("acc_scaled", [P, D + 1])

        nx = [sb(f"nx{b}", [P, 2, P]) for b in range(U)]
        nrow = [sb(f"nrow{b}", [P, D]) for b in range(U)]
        nT = [sb(f"nT{b}", [P, 4, P]) for b in range(U)]
        nT2 = [sb(f"nT2{b}", [P, 4, P]) for b in range(U)]
        nbig = [sb(f"nbig{b}", [P, 4 * DM]) for b in range(U)]
        nacc = [sb(f"nacc{b}", [P, D + 1]) for b in range(U)]
        nsum = [sb(f"nsum{b}", [P, D + 1]) for b in range(U)]
        nh = [sb(f"nh{b}", [P, D]) for b in range(U)]
        nh2 = [sb(f"nh2{b}", [P, D]) for b in range(U)]
        nres = [sb(f"nres{b}", [P, D + 1]) for b in range(U)]
        nq = [sb(f"nq{b}", [P, 3, D + 1], BF16) for b in range(U)]
        nxr = [sb(f"nxr{b}", [P, DM]) for b in range(U)]
        nden = [sb(f"nden{b}", [P, HEADS]) for b in range(U)]
        nz = [sb(f"nz{b}", [P, 8]) for b in range(U)]
        nst = [sb(f"nst{b}", [P, 6]) for b in range(U)]
        nmv = [sb(f"nmv{b}", [P, 2]) for b in range(U)]
        nve = [sb(f"nve{b}", [P, 1]) for b in range(U)]
        nrs = [sb(f"nrs{b}", [P, 1]) for b in range(U)]

        s_w = sem("weights_loaded")
        s_sched = sem("sched_loaded")
        s_iota = sem("iotas_ready")
        s_zero = sem("zero_rows_ready")
        s_zst = sem("zeros_stored")
        s_cst = sem("constants_ready")
        s_win = sem("windows_ready")
        s_start = sem("starts_ready")
        s_stp = sem("starts_copied")
        s_begun = sem("begun_ready")
        s_pairs = sem("pairs_ready")
        s_tab = sem("tables_ready")
        s_wcp, s_wc = sem("edge_weight_product"), sem("edge_weight_ready")
        s_phase = sem("phase_done")
        phases = [0]

        def end_phase(eng, n):
            eng.drain().then_inc(s_phase, 1)
            eng.wait_ge(s_phase, 5 * n)

        def window(ap, w):
            return ap[bass.ds(w, 1)].rearrange("o p c -> (o p) c")

        def node_rows(ap, w):
            return ap[bass.ds(w * P, P), :]

        def slots(name):
            return [sem(f"{name}{b}") for b in range(U)]

        n0 = dict(load=slots("n0_loaded"), store=slots("n0_stored"), m=sem("n0_m"), mT=sem("n0_mT"),
                  big=sem("n0_projected"), res=sem("n0_biased"))
        n1 = dict(load=slots("n1_loaded"), store=slots("n1_stored"), z=sem("n1_gate_sum"), en=sem("n1_gate_exp"),
                  mix=sem("n1_mixed"), tp=sem("n1_mixedT"), tc=sem("n1_mixedT_copied"), y=sem("n1_out"),
                  var=sem("n1_var"), rstd=sem("n1_rstd"), x1=sem("n1_x1"), xt=sem("n1_x1T"), xc=sem("n1_x1T_copied"),
                  q=sem("n1_qT"), qc=sem("n1_qT_copied"), qk=sem("n1_qk"), split=sem("n1_split"))
        n2 = dict(load=slots("n2_loaded"), store=slots("n2_stored"), mean=sem("n2_attention"), tp=sem("n2_T"),
                  tc=sem("n2_T_copied"), lin=sem("n2_linear"), var=sem("n2_var"), rstd=sem("n2_rstd"), x2=sem("n2_x2"),
                  xt=sem("n2_x2T"), xc=sem("n2_x2T_copied"), u=sem("n2_up"), g=sem("n2_gelu"), f=sem("n2_ffn"),
                  res=sem("n2_result"))

        def edge_sems(n):
            names = ("oht", "e", "q", "score", "masked", "turned", "pens", "ends", "arranged", "carries", "spreadback",
                     "full", "fullT", "below", "prob", "shrink_in", "shrink", "so_in", "so", "msg", "msgp", "agg",
                     "acc", "go", "first")
            s = {x: sem(f"l{n}_{x}") for x in names}
            for x in ("ld_row", "ld_q", "ld_ea", "gathered", "stored"):
                s[x] = [sem(f"l{n}_{x}{b}") for b in range(2)]
            s["ld_idx"] = [sem(f"l{n}_ld_idx{st}") for st in range(CH)]
            return s

        s_l = [edge_sems(0), edge_sems(1)]

        block = ctx.enter_context(nc.Block())

        class Layer:
            pass

        L0, L1 = Layer(), Layer()
        L0.s, L0.H, L0.D, L0.table, L0.q_d, L0.acc_d, L0.AW = s_l[0], HEADS, DM, kv_d, q0_d, acc0_d, DM + HEADS
        L1.s, L1.H, L1.D, L1.table, L1.q_d, L1.acc_d, L1.AW = s_l[1], 1, D, x1_d, q1_d, acc1_d, D + 1
        L0.QD, L1.QD = DM, D + 1
        for L in (L0, L1):
            L.R = NI * L.H

        def chunks(eng, emit):
            emit(0, 0, True, False)
            for c in range(1, 4):
                emit(c, c % 2, True, True)
            with eng.Fori(2, NC // 2) as k:
                emit(2 * k, 0, True, True)
                emit(2 * k + 1, 1, True, True)
            if NC % 2:
                emit(NC - 1, 0, True, True)
            emit(NC, NC % 2, False, True)

        def windows(eng, emit):
            emit(0)
            with eng.Fori(1, NW // U) as k:
                emit(k)

        def q_ps(L, b):
            if L.H == HEADS:
                return ps[:, 2 * b, :]
            return ps[:, 2 * b:2 * b + 2, :].rearrange("p k n -> p (k n)")

        def e_ps(b):
            return ps[:, 2 * b + 1, :]

        def agg_ps(L, b):
            return ps[:, 4 + b, 0:L.AW]

        turn_ps = ps[:, 6, :]
        arr_ps, back_ps, so_ps = ps[:, 7, 0:P], ps[:, 7, P:P + 2 * NI], ps[:, 6, 3 * P:3 * P + HEADS]
        qb_ps = [ps[:, 7, 208 + 3 * NI * b:208 + 3 * NI * (b + 1)] for b in range(2)]

        @block.sync
        def _(sp):
            gate = sem("sp_gate")

            def wait(s, value):
                stand_by(sp, gate, s, value)

            sp.dma_start(sched[:, :, :], a["sched"]).then_inc(s_sched, 16)
            loads = [
                (w_n2m[:, :, :], a["w_n2m"]), (w_qkvs[:, :], a["w_qkvs"]), (w_edge[:, :], a["w_edge"]),
                (w_et[:, :], a["w_et"]), (w_m2n[:, :], a["w_m2n"]), (w_q1[:, :, :], a["w_q1"]), (b_q1[:, :], a["b_q1"]),
                (w_k1t[:, :, :], a["w_k1t"]), (w_v1[:, :, :], a["w_v1"]), (w_s1[:, :, :], a["w_s1"]),
                (w_f1[:, :, :], a["w_f1"]), (b_f1[:, :], a["b_f1"]), (w_f2[:, :, :], a["w_f2"]),
                (b_qkvs[:, :], a["b_qkvs"].partition_broadcast(P)),
                (w_beta[:, :, :].rearrange("p k n -> p (k n)"), a["w_beta"].partition_broadcast(P)),
                (rows1[:, :, :].rearrange("p k n -> p (k n)"), a["rows1"].partition_broadcast(P)),
                (we_be[:, :], a["we_be"].partition_broadcast(P)),
            ]
            for dst, src in loads:
                sp.dma_start(dst, src).then_inc(s_w, 16)
            assert len(loads) == N_WEIGHTS

            def node0(k):
                for b in range(U):
                    w = k * U + b
                    wait(n0["m"], w - U + 1)
                    sp.dma_start(nx[b][:, :, :], a["xT"][:, :, bass.ds(w * P, P)]).then_inc(n0["load"][b], 16)
                for b in range(U):
                    w = k * U + b
                    wait(n0["res"], w + 1)
                    sp.dma_start(node_rows(kv_d, w), nres[b][:, 0:2 * DM]).then_inc(n0["store"][b], 16)
                    sp.dma_start(window(q0_d, w), nq[b][:, :, 0:DM]).then_inc(n0["store"][b], 16)
                    sp.dma_start(window(xr_d, w), nxr[b][:, :]).then_inc(n0["store"][b], 16)
            windows(sp, node0)
            for b in range(U):
                sp.wait_ge(n0["store"][b], 48 * (NW // U))
            for n in range(2):
                sp.wait_ge(s_zst, 16 * 2 * NW)
            sp.wait_ge(s_tab, 1)
            end_phase(sp, 1)

            def edge_loads(L):
                s = L.s

                def load_idx(c, par):
                    wait(s["masked"], c - 1)
                    wait(s["go"], CH * (c - 1))
                    wait(s["gathered"][0], 64 * (CH // 2) * (c - 1))
                    wait(s["gathered"][1], 64 * (CH // 2) * (c - 1))
                    for st in range(CH):
                        t = sp.value_load(tw_int[0:1, 0, bass.ds(CH * c + st, 1)], min_val=0, max_val=NS - 1)
                        sp.dma_start(idx[par][:, st, :], a["idx"][bass.ds(t, 1)].rearrange("o p c -> (o p) c"))\
                          .then_inc(s["ld_idx"][st], 16)

                def load_rows(c, par, st):
                    g, b = CH * c + st, st % 2
                    t = sp.value_load(tw_int[0:1, 0, bass.ds(g, 1)], min_val=0, max_val=NS - 1)
                    w = sp.value_load(tw_int[0:1, 1, bass.ds(g, 1)], min_val=0, max_val=NW - 1)
                    wait(s["oht"], g - 1)
                    if st == 2:
                        wait(s["first"], c + 1)
                    sp.dma_start(dst_row[b][:, :], a["dst_row"][bass.ds(t, 1), :].partition_broadcast(P))\
                      .then_inc(s["ld_row"][b], 16)
                    wait(s["q"], g - 1)
                    sp.dma_start(qw[b][:, :, 0:L.QD], window(L.q_d, w).rearrange("p (k n) -> p k n", k=3))\
                      .then_inc(s["ld_q"][b], 16)
                    if L is L0:
                        wait(s["e"], g - 1)
                        sp.dma_start(ea[b][0:DR, :], a["eaT"][:, bass.ds(t * SUPER, SUPER)])\
                          .then_inc(s["ld_ea"][b], 16)
                    else:
                        if st == 0:
                            wait(s["masked"], c - 1)
                        wait(s["ld_ea"][b], 16 * (CH // 2 * c + st // 2))
                        sp.dma_start(ew[par][:, st * JT:(st + 1) * JT],
                                     a["ew"][bass.ds(t, 1)].rearrange("o p c -> (o p) c"))\
                          .then_inc(s["ld_ea"][b], 16)

                def emit(c, par, scores, sums):
                    if not scores:
                        return
                    if not sums:
                        load_idx(0, 0)
                    for st in range(CH):
                        load_rows(c, par, st)
                        if st == 2 and not (isinstance(c, int) and c == NC - 1):
                            load_idx(c + 1, 1 - par)
                chunks(sp, emit)
                for b in range(2):
                    sp.wait_ge(s["stored"][b], 16 * NPAIR // 2)

            edge_loads(L0)
            end_phase(sp, 2)

            def node1(k):
                for b in range(U):
                    w = k * U + b
                    wait(n1["x1"], w - U + 1)
                    sp.dma_start(nacc[b][:, 0:L0.AW], window(acc0_d, w)).then_inc(n1["load"][b], 16)
                    sp.dma_start(nxr[b][:, :], window(xr_d, w)).then_inc(n1["load"][b], 16)
                    sp.dma_start(nrow[b][:, :], node_rows(a["x"], w)).then_inc(n1["load"][b], 16)
                for b in range(U):
                    w = k * U + b
                    wait(n1["x1"], w + 1)
                    sp.dma_start(node_rows(x1_d, w), nres[b][:, 0:D]).then_inc(n1["store"][b], 16)
                    wait(n1["split"], w + 1)
                    sp.dma_start(window(q1_d, w).rearrange("p (k n) -> p k n", k=3), nq[b][:, :, :])\
                      .then_inc(n1["store"][b], 16)
            windows(sp, node1)
            for b in range(U):
                sp.wait_ge(n1["store"][b], 32 * (NW // U))
            end_phase(sp, 3)

            edge_loads(L1)
            end_phase(sp, 4)

            def node2(k):
                for b in range(U):
                    w = k * U + b
                    wait(n2["x2"], w - U + 1)
                    sp.dma_start(nacc[b][:, :], window(acc1_d, w)).then_inc(n2["load"][b], 16)
                    wait(n2["res"], w - U + 1)
                    sp.dma_start(nrow[b][:, :], node_rows(x1_d, w)).then_inc(n2["load"][b], 16)
                for b in range(U):
                    w = k * U + b
                    wait(n2["res"], w + 1)
                    sp.dma_start(node_rows(out, w), nres[b][:, 0:D]).then_inc(n2["store"][b], 16)
            windows(sp, node2)
            for b in range(U):
                sp.wait_ge(n2["store"][b], 16 * (NW // U))

        @block.gpsimd
        def _(pool):
            pool.iota(iota_row[:, :], [[1, P]], base=0, channel_multiplier=0, allow_small_or_imprecise_dtypes=True)
            pool.iota(iota_col[:, :], [[0, 1]], base=0, channel_multiplier=1, allow_small_or_imprecise_dtypes=True)
            pool.iota(pair_no[:, :], [[1, NPAIR]], base=0, channel_multiplier=0, allow_small_or_imprecise_dtypes=True)
            for h in (HEADS, 1):
                pool.memset(sel_j[h][:, :], 1.0)
                pool.memset(sel_h[h][:, :], 0.0)
                pool.memset(sel_ht[h][:, :], 0.0)
            pool.memset(minus_half[:, :], -0.5)
            pool.memset(pen_r[:, :], 0.0)
            pool.memset(runs[:, :, :], -BIG)
            for b in range(2):
                pool.memset(run_f[b][:, :], -BIG)
                pool.memset(acc[b][:, :], 0.0)
                pool.memset(ea[b][:, :], 0.0)
            pool.memset(run_b[:, :], -BIG)
            pool.memset(w_c[:, :], 0.0)
            pool.memset(zero_rows[:, :], 0.0).then_inc(s_zero, 1)
            pool.drain()
            for h in (HEADS, 1):
                pool.affine_select(out=sel_j[h][:, :], in_=sel_j[h][:, :], compare_op=ALU.is_ge, fill=0.0, base=0,
                                   pattern=[[-h, NI]], channel_multiplier=1)
                for m in range(P // h):
                    pool.affine_select(out=sel_h[h][:, :], in_=sel_h[h][:, :], compare_op=ALU.not_equal, fill=1.0,
                                       base=-h * m, pattern=[[-1, h]], channel_multiplier=1) if h > 1 else None
                    pool.drain() if h > 1 else None
            pool.memset(sel_h[1][:, :], 1.0)
            pool.memset(sel_ht[1][:, :], 1.0)
            v = sel_ht[HEADS][:, :].rearrange("p (m c) -> p m c", c=HEADS)
            pool.affine_select(out=v, in_=v, compare_op=ALU.not_equal, fill=1.0, base=0,
                               pattern=[[0, P // HEADS], [-1, HEADS]], channel_multiplier=1)
            pool.drain()
            for h in (HEADS, 1):
                pool.affine_select(out=sel_j[h][:, :], in_=sel_j[h][:, :], compare_op=ALU.is_ge, fill=0.0, base=h - 1,
                                   pattern=[[h, NI]], channel_multiplier=-1)
            pool.drain().then_inc(s_iota, 1)
            for w in range(NW):
                pool.dma_start(acc0_d[w], zero_rows[:, 0:L0.AW]).then_inc(s_zst, 16)
                pool.dma_start(acc1_d[w], zero_rows[:, 0:L1.AW]).then_inc(s_zst, 16)
            end_phase(pool, 1)

            def gathers(L):
                s = L.s

                def emit(c, par, scores, sums):
                    for st in range(CH if scores else 0):
                        b, n = st % 2, CH // 2 * c + st // 2
                        pool.wait_ge(s["ld_idx"][st], 16 * (c + 1))
                        after(pool, s["agg"], CH * (c - 2) + st + 1)
                        after(pool, s["gathered"][b], 64 * n)
                        pool.sem_inc(s["go"], 1)
                        for j in range(JT):
                            pool.indirect_dma_start(
                                out=rows[par][:, st, j, :], out_offset=None, in_=L.table,
                                in_offset=bass.IndirectOffsetOnAxis(ap=idx[par][:, st, j:j + 1], axis=0))\
                                .then_inc(s["gathered"][b], 16)
                chunks(pool, emit)

            def root(n, k, count):
                for b in range(U):
                    pool.wait_ge(n["var"], count(k, b))
                    pool.tensor_tensor(nrs[b][:, :], nve[b][:, :], minus_half[:, :], ALU.pow).then_inc(n["rstd"], 1)

            gathers(L0)
            end_phase(pool, 2)
            windows(pool, lambda k: root(n1, k, lambda k, b: U * k + b + 1))
            end_phase(pool, 3)
            gathers(L1)
            end_phase(pool, 4)

            def roots(k):
                for r in range(3):
                    root(n2, k, lambda k, b: 3 * U * k + r * U + b + 1)
            windows(pool, roots)

        @block.scalar
        def _(act):
            gate = sem("act_gate")

            def wait(s, value):
                stand_by(act, gate, s, value)

            act.wait_ge(s_wcp, 1)
            act.activation(w_c[0:DR, :], ps[0:DR, 7, 0:DM], ACT.Copy).then_inc(s_wc, 1)

            def node0(k):
                for b in range(U):
                    wait(n0["m"], U * k + b + 1)
                    wait(n0["big"], U * (k - 1) + b + 1)
                    act.activation(nT[b][:, 0, :], ps[:, 4 * b, 0:P], ACT.Copy).then_inc(n0["mT"], 1)
            windows(act, node0)
            end_phase(act, 1)

            def edge(L):
                s = L.s

                def spread_nodes(c, st):
                    g, b = CH * c + st, st % 2
                    wait(s["ld_row"][b], 16 * (CH // 2 * c + st // 2 + 1))
                    wait(s["q"], g - 1)
                    act.activation(oht[b][:, :], dst_row[b][:, :], ACT.Abs, scale=-1.0, bias=node_tab[:, bass.ds(g, 1)])

                def spread_nodes_end(st):
                    b = st % 2
                    act.activation(oht[b][:, :], oht[b][:, :], ACT.Relu, scale=-1.0, bias=ones[:, 0:1])\
                       .then_inc(s["oht"], 1)

                def edge_nodes(c, par, st):
                    b = st % 2
                    wait(s["agg"], CH * c + st - 1)
                    for j in range(JT):
                        act.activation(oh[b][:, j, :], iota_row[:, :], ACT.Abs, scale=-1.0, bias=rel[par][:, st, j:j + 1])

                def messages(c, par, st):
                    b = st % 2
                    pr = prob[par][:, st * JT:(st + 1) * JT, 0:L.H]
                    if L is L0:
                        act.activation(oh[b][:, :, :], oh[b][:, :, :], ACT.Relu, scale=-1.0, bias=ones[:, 0:1])
                        act.activation(msg[b][:, :, 0:L.AW].rearrange("p j (h c) -> p j h c", h=HEADS)[:, :, :, OUTC],
                                       pr, ACT.Copy).then_inc(s["msgp"], 1)
                    else:
                        wait(s["agg"], CH * c + st - 1)
                        for j in range(JT):
                            act.activation(msg[b][:, j, 0:D], rows[par][:, st, j, :], ACT.Copy, scale=pr[:, j, :])
                        act.activation(msg[b][:, :, D:D + 1], pr, ACT.Copy).then_inc(s["msgp"], 1)

                def store(c, st):
                    g, b = CH * c + st, st % 2
                    w = act.value_load(tw_int[0:1, 2, bass.ds(g, 1)], min_val=0, max_val=NW + NPAIR - 1)
                    after(act, s["acc"], g + 1)
                    act.dma_start(window(L.acc_d, w), acc[b][:, 0:L.AW]).then_inc(s["stored"][b], 16)

                def emit(c, par, scores, sums):
                    past, pp = c - 1, 1 - par
                    one_hot = scores and L is L0
                    if one_hot:
                        for st in range(2):
                            spread_nodes(c, st)
                        act.drain()
                        for st in range(2):
                            spread_nodes_end(st)
                    if sums:
                        wait(s["turned"], past + 1)
                        act.activation(pen_r[0:L.R, 0:P], turn_ps[0:L.R, P:2 * P], ACT.Copy).then_inc(s["pens"], 1)
                    if one_hot:
                        spread_nodes(c, 2)
                        act.drain()
                        spread_nodes_end(2)
                    if sums:
                        wait(s["shrink_in"], past + 1)
                        act.activation(shrink[0:L.H, :], shrink_in[0:L.H, :], ACT.Exp).then_inc(s["shrink"], 1)
                        wait(s["below"], past + 1)
                        wait(s["agg"], CH * (past - 1))
                        act.activation(prob[pp][:, :, 0:L.H], below[:, 0:L.R].rearrange("p (n h) -> p n h", h=L.H),
                                       ACT.Exp).then_inc(s["prob"], 1)
                        act.drain()
                    for st in range(2, CH):
                        if one_hot and st + 1 < CH:
                            spread_nodes(c, st + 1)
                        if L is L1:
                            for r in SUMMED[st] if sums else ():
                                messages(past, pp, r)
                        else:
                            if one_hot and st + 1 < CH and not (sums and SUMMED[st]):
                                act.drain()
                                spread_nodes_end(st + 1)
                            for m, r in enumerate(SUMMED[st] if sums else ()):
                                edge_nodes(past, pp, r)
                                act.drain()
                                if one_hot and st + 1 < CH and m == 0:
                                    spread_nodes_end(st + 1)
                                messages(past, pp, r)
                        for r in SUMMED[st - 1] if sums else ():
                            store(past, r)
                    if sums:
                        for r in SUMMED[CH - 1]:
                            store(past, r)
                chunks(act, emit)

            edge(L0)
            end_phase(act, 2)

            def node1(k):
                for b in range(U):
                    wait(n1["z"], U * k + b + 1)
                    act.activation(nz[b][:, 3:4], nz[b][:, 2:3], ACT.Exp, scale=-1.0).then_inc(n1["en"], 1)
                for b in range(U):
                    wait(n1["tp"], U * k + b + 1)
                    act.activation(nT[b][:, 0, :], ps[:, 4 * b, 0:P], ACT.Copy).then_inc(n1["tc"], 1)
                for b in range(U):
                    wait(n1["xt"], U * k + b + 1)
                    act.activation(nT[b][:, 2:4, :], ps[:, 4 * b, 0:2 * P].rearrange("p (k n) -> p k n", k=2), ACT.Copy)\
                       .then_inc(n1["xc"], 1)
                for b in range(U):
                    wait(n1["q"], U * k + b + 1)
                    for m in range(2):
                        i = act.activation(nT2[b][:, m, :], ps[:, 4 * b + 2, m * P:(m + 1) * P], ACT.Identity,
                                           bias=b_q1[:, m:m + 1])
                    i.then_inc(n1["qc"], 1)
            windows(act, node1)
            end_phase(act, 3)
            edge(L1)
            end_phase(act, 4)

            def node2(k):
                for b in range(U):
                    wait(n2["tp"], U * k + b + 1)
                    act.activation(nT[b][:, :, :], ps[:, 4 * b, :].rearrange("p (k n) -> p k n", k=4), ACT.Copy)\
                       .then_inc(n2["tc"], 1)
                for b in range(U):
                    wait(n2["xt"], U * k + b + 1)
                    act.activation(nT[b][:, 0:2, :], ps[:, 4 * b, 0:2 * P].rearrange("p (k n) -> p k n", k=2), ACT.Copy)\
                       .then_inc(n2["xc"], 1)
                for b in range(U):
                    wait(n2["u"], U * k + b + 1)
                    for m in range(4):
                        i = act.activation(nT2[b][:, m, :], ps[:, 4 * b + 2, m * P:(m + 1) * P], ACT.Gelu_apprx_tanh,
                                           bias=b_f1[:, m:m + 1])
                    i.then_inc(n2["g"], 1)
            windows(act, node2)

        @block.vector
        def _(v):
            v.wait_ge(s_iota, 1)
            v.tensor_scalar(ident[:, :], iota_row[:, :], iota_col[:, 0:1], None, ALU.is_equal)
            v.tensor_scalar(tri[:, :], iota_row[:, :], iota_col[:, 0:1], None, ALU.is_gt)
            v.memset(ones[:, :], 1.0)
            v.drain().then_inc(s_cst, 1)
            v.wait_ge(s_sched, 16)
            v.tensor_scalar(sched_w[:, :, :], sched[:, :, :], 7, None, ALU.arith_shift_right)
            v.drain()
            v.tensor_copy(sched_f[:, :, :], sched_w[:, :, :])
            v.drain()
            v.tensor_tensor(n_win[:, :], sched_f[:, :, 1], sched_f[:, :, 0], ALU.subtract)
            v.tensor_tensor(d_win[:, :], sched_f[:, :, 0], sched_f[:, :, 2], ALU.subtract)
            v.drain()
            v.tensor_scalar(n_win[:, :], n_win[:, :], 1.0, None, ALU.add)
            v.tensor_scalar(d_win[:, :], d_win[:, :], -1.0, None, ALU.add)
            v.drain().then_inc(s_win, 1)
            v.wait_ge(s_start, 1)
            v.tensor_copy(start[:, :], ps[:, 0, 0:SG])
            v.drain()
            for gcol in range(SG):
                v.tensor_scalar(begun[:, gcol, :], pair_no[:, :], start[:, gcol:gcol + 1], None, ALU.is_ge)
                v.tensor_scalar(stepped[:, gcol, :], pair_no[:, :], start[:, gcol:gcol + 1], d_win[:, gcol:gcol + 1],
                                ALU.is_ge, ALU.mult)
            v.drain().then_inc(s_begun, 1)
            v.wait_ge(s_pairs, 1)
            v.tensor_scalar(t_of[:, :], ps[:, 1, 0:NPAIR], -1.0, float(NS - 1), ALU.add, ALU.min)
            v.tensor_tensor(w_of[:, :], pair_no[:, :], ps[:, 2, 0:NPAIR], ALU.add)
            v.drain()
            v.tensor_scalar(w_of[:, :], w_of[:, :], float(NW - 1), None, ALU.min)
            v.drain()
            v.tensor_copy(tw_int[0:1, 0, :], t_of[0:1, :])
            v.tensor_copy(tw_int[0:1, 1, :], w_of[0:1, :])
            v.tensor_scalar(base_tab[:, :], w_of[:, :], float(P), None, ALU.mult)
            v.tensor_scalar(node_tab[:, :], w_of[:, :], float(P), iota_col[:, 0:1], ALU.mult, ALU.add)
            v.memset(keep_tab[:, 0:1], 0.0)
            v.tensor_tensor(keep_tab[:, 1:NPAIR], w_of[:, 1:NPAIR], w_of[:, 0:NPAIR - 1], ALU.is_equal)
            v.scalar_tensor_tensor(save_of[:, :], pair_no[:, :], float(NW), w_of[:, :], ALU.add, ALU.subtract)
            v.drain()
            v.memset(save_of[:, NPAIR - 1:NPAIR], 0.0)
            v.drain()
            v.tensor_tensor(save_of[:, 0:NPAIR - 1], save_of[:, 0:NPAIR - 1], keep_tab[:, 1:NPAIR], ALU.mult)
            v.drain()
            v.tensor_tensor(save_of[:, :], save_of[:, :], w_of[:, :], ALU.add)
            v.drain()
            v.tensor_copy(tw_int[0:1, 2, :], save_of[0:1, :])
            v.drain().then_inc(s_tab, 1)

            def split(b, n, src, scale):
                v.tensor_scalar(nq[b][:, 0, 0:n], src, scale, None, ALU.mult)
                v.drain()
                v.scalar_tensor_tensor(nsum[b][:, 0:n], src, scale, nq[b][:, 0, 0:n], ALU.mult, ALU.subtract)
                v.drain()
                v.tensor_copy(nq[b][:, 1, 0:n], nsum[b][:, 0:n])
                v.drain()
                return v.tensor_tensor(nq[b][:, 2, 0:n], nsum[b][:, 0:n], nq[b][:, 1, 0:n], ALU.subtract)

            v.wait_ge(s_w, 16 * N_WEIGHTS)

            def node0(k):
                for b in range(U):
                    v.wait_ge(n0["big"], U * k + b + 1)
                    after(v, n0["store"][b], 48 * k)
                    v.tensor_tensor(nbig[b][:, :], ps[:, 4 * b + 1, :], b_qkvs[:, :], ALU.add)
                    v.drain()
                    v.tensor_copy(nres[b][:, 0:2 * DM], nbig[b][:, DM:3 * DM])
                    v.tensor_copy(nxr[b][:, :], nbig[b][:, 3 * DM:4 * DM])
                    split(b, DM, nbig[b][:, 0:DM], OUTC ** -0.5)
                    v.drain().then_inc(n0["res"], 1)
            windows(v, node0)
            end_phase(v, 1)

            def edge(L):
                s, H, R = L.s, L.H, L.R

                def first_node(c, par):
                    v.wait_ge(s["ld_row"][0], 16 * (CH // 2 * c + 1))
                    v.tensor_tensor(rel_first[par][0:H, :], dst_row[0][0:H, 0:1], base_tab[0:H, bass.ds(CH * c, 1)],
                                    ALU.subtract).then_inc(s["first"], 1)

                def spread_nodes(c, st):
                    g, b, n = CH * c + st, st % 2, CH // 2 * c + st // 2
                    v.wait_ge(s["ld_row"][b], 16 * (n + 1))
                    after(v, s["q"], g - 1)
                    v.tensor_scalar(oht[b][:, :], dst_row[b][:, :], node_tab[:, bass.ds(g, 1)], None, ALU.is_equal)\
                     .then_inc(s["oht"], 1)

                def add_edges(c, par, st):
                    b, n = st % 2, CH // 2 * c + st // 2
                    v.wait_ge(s["gathered"][b], 64 * (n + 1))
                    v.wait_ge(s["e"], CH * c + st + 1)
                    kv = rows[par][:, st, :, :].rearrange("p j (m n) -> p j m n", m=2)
                    v.tensor_tensor(kv, kv, e_ps(b).rearrange("p (j n) -> p j n", j=JT).unsqueeze(2)
                                    .to_broadcast([P, JT, 2, DM]), ALU.add)

                def products(c, par, st):
                    v.wait_ge(s["q"], CH * c + st + 1)
                    v.tensor_tensor(prod[:, :, 0:DM], rows[par][:, st, :, 0:DM],
                                    q_ps(L, st % 2).rearrange("p (j n) -> p j n", j=JT), ALU.mult)

                def scores_of(c, par, st):
                    v.tensor_reduce(score[par][:, st * JT:(st + 1) * JT, :],
                                    prod[:, :, 0:DM].rearrange("p j (h n) -> p j h n", h=HEADS), AX.X, ALU.add)\
                     .then_inc(s["score"], 1)

                def dots(c, par, st):
                    g, b, n = CH * c + st, st % 2, CH // 2 * c + st // 2
                    v.wait_ge(s["gathered"][b], 64 * (n + 1))
                    v.wait_ge(s["q"], g + 1)
                    for j in range(JT):
                        i = v.tensor_tensor_reduce(
                            out=prod[:, j, :], in0=rows[par][:, st, j, :], in1=q_ps(L, b)[:, j * D:(j + 1) * D],
                            scale=1.0, scalar=0.0, op0=ALU.mult, op1=ALU.add,
                            accum_out=score[par][:, st * JT + j, 0:1])
                    i.then_inc(s["score"], 1)

                def mask(c, par):
                    for st in range(CH):
                        v.wait_ge(s["ld_idx"][st], 16 * (c + 1))
                    dst = idx[par][:, :, JT:2 * JT]
                    before = idx[par][:, :, 2 * JT:3 * JT]
                    relc = rel[par][:, :, :]
                    flat = relc.rearrange("p s j -> p (s j)")
                    after(v, s["agg"], CH * (c - 1))
                    v.tensor_tensor(relc, dst, base_tab[:, bass.ds(CH * c, CH)].unsqueeze(2).to_broadcast([P, CH, JT]),
                                    ALU.subtract)
                    v.tensor_tensor(same[:, :].rearrange("p (s j) -> p s j", j=JT), dst, before, ALU.is_equal)
                    v.drain()
                    after(v, s["turned"], c)
                    v.tensor_scalar(pen[:, :, 0:H], same[:, :].unsqueeze(2).to_broadcast([P, NI, H]), -1.0, BIG,
                                    ALU.add, ALU.mult)
                    v.tensor_scalar(inside[:, :], flat, 0.0, None, ALU.is_ge)
                    v.drain()
                    v.scalar_tensor_tensor(inside[:, :], flat, float(P), inside[:, :], ALU.is_lt, ALU.mult)
                    v.drain()
                    v.tensor_scalar(outside[:, :], inside[:, :], -1.0, BIG, ALU.add, ALU.mult)
                    sc = score[par][:, :, 0:H]
                    if L is L1:
                        for b in range(2):
                            v.wait_ge(s["ld_ea"][b], 16 * (CH // 2) * (c + 1))
                        v.tensor_scalar(same[:, :], ew[par][:, :], we_be[:, 0:1], we_be[:, 1:2], ALU.mult, ALU.add)
                        v.tensor_reduce(qb[:, :], qb_ps[par].rearrange("p (n m) -> p n m", m=3), AX.X, ALU.add)
                        v.drain()
                        v.tensor_tensor(sc[:, :, 0], sc[:, :, 0], same[:, :], ALU.add)
                        v.tensor_tensor(outside[:, :], outside[:, :], qb[:, :], ALU.add)
                    v.drain()
                    v.tensor_tensor(biased[:, :, 0:H], sc, outside[:, :].unsqueeze(2).to_broadcast([P, NI, H]), ALU.add)
                    v.drain().then_inc(s["masked"], 1)

                sT = turn_ps[0:R, 0:P]
                pf, pb = pen_r[0:R, 0:P], pen_r[0:R, 1:P + 1]

                def scan_tiles(c, par):
                    v.wait_ge(s["turned"], c + 1)
                    v.wait_ge(s["pens"], c + 1)
                    v.tensor_tensor_scan(fwd[0:R, :], pf, sT, -BIG, ALU.add, ALU.max)
                    v.tensor_tensor_scan(bwd[0:R, ::-1], pb[:, ::-1], sT[:, ::-1], -BIG, ALU.add, ALU.max)
                    v.tensor_reduce(carry_r[0:R, 0:1], pen_r[0:R, 1:P], AX.X, ALU.min)
                    v.drain()
                    ends = (fwd[0:R, P - 1:P], bwd[0:R, 0:1], pen_r[0:R, 0:1], carry_r[0:R, 0:1])
                    for m, col in enumerate(ends):
                        v.tensor_scalar(spread[0:R, m, :], sel_j[H][0:R, :], col, None, ALU.mult)
                    v.drain().then_inc(s["ends"], 1)

                def scan_ends(c, par):
                    v.wait_ge(s["arranged"], c + 1)
                    v.tensor_copy(runs[0:H, :, 0:NI], arr_ps[0:H, :].rearrange("p (m n) -> p m n", m=4))
                    v.tensor_copy(run_f[par][0:H, 0:1], run_f[1 - par][0:H, NI:NI + 1])
                    v.drain()
                    v.tensor_tensor(pen_f[0:H, :], runs[0:H, 2, 0:NI], runs[0:H, 3, 0:NI], ALU.add)
                    v.tensor_tensor(pen_b[0:H, :], runs[0:H, 2, 1:NI + 1], runs[0:H, 3, 0:NI], ALU.add)
                    v.drain()
                    v.tensor_tensor_scan(run_f[par][0:H, 1:NI + 1], pen_f[0:H, :], runs[0:H, 0, 0:NI],
                                         run_f[par][0:H, 0:1], ALU.add, ALU.max)
                    v.tensor_tensor_scan(run_b[0:H, 0:NI][:, ::-1], pen_b[0:H, ::-1], runs[0:H, 1, 0:NI][:, ::-1],
                                         -BIG, ALU.add, ALU.max)
                    v.drain()
                    v.tensor_copy(carry[0:H, 0, :], run_f[par][0:H, 0:NI])
                    v.tensor_tensor(carry[0:H, 1, :], run_b[0:H, 1:NI + 1], runs[0:H, 2, 1:NI + 1], ALU.add)
                    v.drain().then_inc(s["carries"], 1)

                def scan_carried(c, par):
                    v.wait_ge(s["spreadback"], c + 1)
                    v.tensor_tensor(carry_p[0:R, :, :], back_ps[0:R, :].rearrange("p (m n) -> p m n", m=2),
                                    sel_j[H][0:R, :].unsqueeze(1).to_broadcast([R, 2, NI]), ALU.mult)
                    v.drain()
                    v.tensor_reduce(carry_r[0:R, :], carry_p[0:R, :, :], AX.X, ALU.add)
                    v.drain()
                    v.tensor_tensor_scan(fwd[0:R, :], pf, sT, carry_r[0:R, 0:1], ALU.add, ALU.max)
                    v.drain()
                    v.tensor_tensor_scan(full[0:R, ::-1], pb[:, ::-1], fwd[0:R, ::-1], carry_r[0:R, 1:2],
                                         ALU.add, ALU.max)
                    v.drain().then_inc(s["full"], 1)

                def subtract(c, par):
                    v.tensor_scalar(shrink_in[0:H, :], run_f[par][0:H, 0:1], full[0:H, 0:1], 0.0, ALU.subtract, ALU.min)\
                     .then_inc(s["shrink_in"], 1)
                    v.tensor_scalar(first_oh[0:H, :], iota_row[0:H, :], rel_first[par][0:H, 0:1], None, ALU.is_equal)
                    v.wait_ge(s["fullT"], c + 1)
                    v.tensor_tensor(below[:, 0:R], biased[:, :, 0:H].rearrange("p n h -> p (n h)") if H == HEADS else
                                    biased[:, :, 0], turn_ps[:, 2 * P:2 * P + R], ALU.subtract).then_inc(s["below"], 1)
                    v.wait_ge(s["shrink"], c + 1)
                    v.scalar_tensor_tensor(shrink_d[0:H, 0:H], ident[0:H, 0:H], shrink[0:H, 0:1], ident[0:H, 0:H],
                                           ALU.mult, ALU.subtract)
                    v.drain().then_inc(s["so_in"], 1)

                def weigh(c, par, st):
                    g, b = CH * c + st, st % 2
                    after(v, s["agg"], g - 1)
                    if L is L0:
                        v.wait_ge(s["prob"], c + 1)
                        m = msg[b][:, :, 0:L.AW].rearrange("p j (h c) -> p j h c", h=HEADS)[:, :, :, 0:OUTC]
                        v.tensor_tensor(m, rows[par][:, st, :, DM:2 * DM].rearrange("p j (h c) -> p j h c", h=HEADS),
                                        prob[par][:, st * JT:(st + 1) * JT, :].unsqueeze(3)
                                        .to_broadcast([P, JT, HEADS, OUTC]), ALU.mult).then_inc(s["msg"], 1)
                    else:
                        v.tensor_tensor(oh[b][:, :, :], iota_row[:, :].unsqueeze(1).to_broadcast([P, JT, P]),
                                        rel[par][:, st, :].unsqueeze(2).to_broadcast([P, JT, P]), ALU.is_equal)\
                         .then_inc(s["msg"], 1)

                def shrink_sums(c):
                    v.wait_ge(s["so"], c + 1)
                    v.tensor_scalar(rescale[:, 0:H], so_ps[:, 0:H], 1.0, None, ALU.add)
                    v.drain()
                    v.tensor_tensor(acc_scaled[:, 0:L.AW].rearrange("p (h c) -> p h c", h=H),
                                    acc[1][:, 0:L.AW].rearrange("p (h c) -> p h c", h=H),
                                    rescale[:, 0:H].unsqueeze(2).to_broadcast([P, H, L.AW // H]), ALU.mult)

                def accumulate(c, st):
                    g, b = CH * c + st, st % 2
                    old = acc_scaled if st == 0 else acc[1 - b]
                    v.wait_ge(s["agg"], g + 1)
                    after(v, s["stored"][b], 16 * (CH // 2 * c + st // 2))
                    v.scalar_tensor_tensor(acc[b][:, 0:L.AW], old[:, 0:L.AW], keep_tab[:, bass.ds(g, 1)], agg_ps(L, b),
                                           ALU.mult, ALU.add).then_inc(s["acc"], 1)

                def emit(c, par, scores, sums):
                    past, pp = c - 1, 1 - par
                    if scores:
                        first_node(c, par)
                        if L is L1:
                            spread_nodes(c, 0)
                            spread_nodes(c, 1)
                    if sums:
                        mask(past, pp)
                    parts = iter((scan_tiles, scan_ends, scan_carried, subtract))
                    for st in range(CH):
                        if sums and st == 0 and L is L1:
                            next(parts)(past, pp)
                        if scores:
                            if L is L0:
                                add_edges(c, par, st)
                                if st > 0:
                                    scores_of(c, par, st - 1)
                            else:
                                dots(c, par, st)
                                if 0 < st < CH - 1:
                                    spread_nodes(c, st + 1)
                        if sums and st < 2 and not (st == 0 and L is L1):
                            next(parts)(past, pp)
                        for r in SUMMED[st] if sums else ():
                            weigh(past, pp, r)
                        v.drain()
                        if scores and L is L0:
                            products(c, par, st)
                        if sums and st < 2:
                            next(parts)(past, pp)
                        if sums and st == 2:
                            shrink_sums(past)
                        for m, r in enumerate(SUMMED[st - 1] if sums and st else ()):
                            if m:
                                v.drain()
                            accumulate(past, r)
                        v.drain()
                    if scores and L is L0:
                        scores_of(c, par, CH - 1)
                    if sums:
                        for r in SUMMED[CH - 1]:
                            accumulate(past, r)
                    v.drain()
                chunks(v, emit)

            edge(L0)
            end_phase(v, 2)

            def moments(n, b):
                v.bn_stats(nst[b][:, :], nh[b][:, :])
                v.drain()
                v.bn_aggr(nmv[b][:, :], nst[b][:, :])
                v.drain()
                v.tensor_scalar(nve[b][:, :], nmv[b][:, 1:2], EPS, None, ALU.add).then_inc(n["var"], 1)

            def normal(out_, b):
                return v.tensor_scalar(out_, nh[b][:, :], nmv[b][:, 0:1], nrs[b][:, 0:1], ALU.subtract, ALU.mult)

            def node1(k):
                for b in range(U):
                    w = U * k + b
                    v.wait_ge(n1["load"][b], 48 * (k + 1))
                    sums = nacc[b][:, 0:L0.AW].rearrange("p (h c) -> p h c", h=HEADS)
                    v.tensor_scalar(nden[b][:, :], sums[:, :, OUTC], 1e-16, None, ALU.add)
                    v.drain()
                    v.reciprocal(nden[b][:, :], nden[b][:, :])
                    v.drain()
                    o, t = nsum[b][:, 0:DM], nbig[b][:, 0:DM]
                    v.tensor_tensor(o.rearrange("p (h c) -> p h c", h=HEADS), sums[:, :, 0:OUTC],
                                    nden[b][:, :].unsqueeze(2).to_broadcast([P, HEADS, OUTC]), ALU.mult)
                    v.drain()
                    v.tensor_tensor(t, o, nxr[b][:, :], ALU.subtract)
                    v.drain()
                    z = 0.0
                    for m, part in enumerate((o, nxr[b][:, :], t)):
                        v.tensor_tensor_reduce(out=nbig[b][:, DM:2 * DM], in0=part, in1=w_beta[:, m, :], scale=1.0,
                                               scalar=z, op0=ALU.mult, op1=ALU.add, accum_out=nz[b][:, m:m + 1])
                        v.drain()
                        z = nz[b][:, m:m + 1]
                    v.drain().then_inc(n1["z"], 1)
                for b in range(U):
                    v.wait_ge(n1["en"], U * k + b + 1)
                    v.tensor_scalar(nz[b][:, 4:5], nz[b][:, 3:4], 1.0, None, ALU.add)
                    v.drain()
                    v.reciprocal(nz[b][:, 5:6], nz[b][:, 4:5])
                    v.drain()
                    v.tensor_scalar(nz[b][:, 6:7], nz[b][:, 5:6], -1.0, None, ALU.mult)
                    v.drain()
                    v.scalar_tensor_tensor(nbig[b][:, DM:2 * DM], nbig[b][:, 0:DM], nz[b][:, 6:7], nsum[b][:, 0:DM],
                                           ALU.mult, ALU.add).then_inc(n1["mix"], 1)
                for b in range(U):
                    v.wait_ge(n1["y"], U * k + b + 1)
                    v.tensor_tensor(nh[b][:, :], nrow[b][:, :], ps[:, 4 * b + 1, 0:D], ALU.add)
                    v.drain()
                    moments(n1, b)
                for b in range(U):
                    v.wait_ge(n1["rstd"], U * k + b + 1)
                    after(v, n1["store"][b], 32 * k)
                    normal(nres[b][:, 0:D], b)
                    v.drain().then_inc(n1["x1"], 1)
                for b in range(U):
                    v.wait_ge(n1["qk"], U * k + b + 1)
                    split(b, D + 1, ps[:, 4 * b + 3, 0:D + 1], D ** -0.5)
                    v.drain().then_inc(n1["split"], 1)
            windows(v, node1)
            end_phase(v, 3)

            edge(L1)
            end_phase(v, 4)

            def node2(k):
                for b in range(U):
                    v.wait_ge(n2["load"][b], 32 * (k + 1))
                    v.tensor_scalar(nden[b][:, 0:1], nacc[b][:, D:D + 1], 1e-12, None, ALU.max)
                    v.drain()
                    v.reciprocal(nden[b][:, 1:2], nden[b][:, 0:1])
                    v.drain()
                    v.tensor_scalar(nsum[b][:, :], nacc[b][:, :], nden[b][:, 1:2], None, ALU.mult)
                    v.drain().then_inc(n2["mean"], 1)
                    v.tensor_tensor(nh2[b][:, :], nrow[b][:, :], rows1[:, BS, :], ALU.add)
                    v.drain()
                    v.scalar_tensor_tensor(nh2[b][:, :], rows1[:, BV, :], nsum[b][:, D:D + 1], nh2[b][:, :],
                                           ALU.mult, ALU.add)
                v.drain()

                def affine(out_, b, g, beta):
                    normal(out_, b)
                    v.drain()
                    v.tensor_tensor(out_, out_, rows1[:, g, :], ALU.mult)
                    v.drain()
                    v.tensor_tensor(out_, out_, rows1[:, beta, :], ALU.add)
                    v.drain()

                for b in range(U):
                    v.wait_ge(n2["lin"], U * k + b + 1)
                    v.tensor_tensor(nh[b][:, :], nh2[b][:, :], ps[:, 4 * b + 1, 0:D], ALU.add)
                    v.drain()
                    moments(n2, b)
                for b in range(U):
                    v.wait_ge(n2["rstd"], 3 * U * k + b + 1)
                    affine(nh2[b][:, :], b, G1, B1)
                    v.drain().then_inc(n2["x2"], 1)
                    v.tensor_tensor(nbig[b][:, 0:D], nh2[b][:, :], rows1[:, BF2, :], ALU.add)
                v.drain()
                for b in range(U):
                    v.wait_ge(n2["f"], U * k + b + 1)
                    v.tensor_tensor(nh[b][:, :], nbig[b][:, 0:D], ps[:, 4 * b + 3, 0:D], ALU.add)
                    v.drain()
                    moments(n2, b)
                for b in range(U):
                    v.wait_ge(n2["rstd"], 3 * U * k + U + b + 1)
                    affine(nh2[b][:, :], b, G2, B2)
                    v.tensor_tensor(nh[b][:, :], nh2[b][:, :], nrow[b][:, :], ALU.add)
                    v.drain()
                    moments(n2, b)
                for b in range(U):
                    v.wait_ge(n2["rstd"], 3 * U * k + 2 * U + b + 1)
                    after(v, n2["store"][b], 16 * k)
                    normal(nres[b][:, 0:D], b)
                    v.drain().then_inc(n2["res"], 1)
            windows(v, node2)

        @block.tensor
        def _(pe):
            gate = sem("pe_gate")

            def mm(out_, lhsT, rhs, first=True, last=True):
                return pe.matmul(out_, lhsT=lhsT, rhs=rhs, start=first, stop=last)

            pe.wait_ge(s_cst, 1)
            pe.wait_ge(s_win, 1)
            for gcol in range(SG):
                for m in range(gcol + 1):
                    i = mm(ps[:, 0, gcol:gcol + 1], tri[:, :] if m == gcol else ones[:, :], n_win[:, m:m + 1],
                           m == 0, m == gcol)
            i.then_inc(s_start, 1)
            pe.wait_ge(s_begun, 1)
            for bank, part in ((1, begun), (2, stepped)):
                for gcol in range(SG):
                    i = mm(ps[:, bank, 0:NPAIR], ones[:, :], part[:, gcol, :], gcol == 0, gcol == SG - 1)
            i.then_inc(s_pairs, 1)
            pe.wait_ge(s_w, 16 * N_WEIGHTS)
            mm(ps[0:DR, 7, 0:DM], w_edge[:, :], w_et[:, :]).then_inc(s_wcp, 1)
            pe.wait_ge(s_tab, 1)
            pe.wait_ge(s_wc, 1)

            def node0(k):
                for b in range(U):
                    pe.wait_ge(n0["load"][b], 16 * (k + 1))
                    after(pe, n0["mT"], U * (k - 1) + b + 1)
                    for m in range(2):
                        i = mm(ps[:, 4 * b, 0:P], w_n2m[:, m, :], nx[b][:, m, :], m == 0, m == 1)
                    i.then_inc(n0["m"], 1)
                for b in range(U):
                    pe.wait_ge(n0["mT"], U * k + b + 1)
                    after(pe, n0["res"], U * (k - 1) + b + 1)
                    mm(ps[:, 4 * b + 1, :], nT[b][:, 0, :], w_qkvs[:, :]).then_inc(n0["big"], 1)
            windows(pe, node0)
            end_phase(pe, 1)

            def edge(L):
                s, H, R = L.s, L.H, L.R

                def front(c, par, st):
                    g, b, n = CH * c + st, st % 2, CH // 2 * c + st // 2
                    after(pe, s["score"], g - 1)
                    if L is L0:
                        pe.wait_ge(s["ld_ea"][b], 16 * (n + 1))
                        for j in range(JT):
                            i = mm(e_ps(b)[:, j * DM:(j + 1) * DM], ea[b][:, j * P:(j + 1) * P], w_c[:, :])
                        i.then_inc(s["e"], 1)
                    pe.wait_ge(s["ld_q"][b], 16 * (n + 1))
                    pe.wait_ge(s["oht"], g + 1)
                    for j in range(JT):
                        for m in range(3):
                            i = mm(q_ps(L, b)[:, j * L.D:(j + 1) * L.D], oht[b][:, j * P:(j + 1) * P],
                                   qw[b][:, m, 0:L.D], m == 0, m == 2)
                        if L is L1:
                            n = st * JT + j
                            i = mm(qb_ps[par][:, 3 * n:3 * (n + 1)], oht[b][:, j * P:(j + 1) * P], qw[b][:, :, D])
                    i.then_inc(s["q"], 1)

                def turn(c):
                    stand_by(pe, gate, s["masked"], c + 1)
                    sc = biased[:, :, 0:H].rearrange("p n h -> p (n h)") if H == HEADS else biased[:, :, 0]
                    pn = pen[:, :, 0:H].rearrange("p n h -> p (n h)") if H == HEADS else pen[:, :, 0]
                    pe.transpose(turn_ps[0:R, 0:P], sc, ident[:, :])
                    pe.transpose(turn_ps[0:R, P:2 * P], pn, ident[:, :]).then_inc(s["turned"], 1)

                def arrange(c):
                    stand_by(pe, gate, s["ends"], c + 1)
                    mm(arr_ps[0:H, :], sel_h[H][0:R, :], spread[0:R, :, :].rearrange("p m n -> p (m n)"))\
                        .then_inc(s["arranged"], 1)

                def carry_back(c):
                    stand_by(pe, gate, s["carries"], c + 1)
                    mm(back_ps[0:R, :], sel_ht[H][0:H, 0:R], carry[0:H, :, :].rearrange("p m n -> p (m n)"))\
                        .then_inc(s["spreadback"], 1)

                def turn_back(c):
                    stand_by(pe, gate, s["full"], c + 1)
                    pe.transpose(turn_ps[:, 2 * P:2 * P + R], full[0:R, :], ident[0:R, 0:R]).then_inc(s["fullT"], 1)
                    stand_by(pe, gate, s["so_in"], c + 1)
                    mm(so_ps[:, 0:H], first_oh[0:H, :], shrink_d[0:H, 0:H]).then_inc(s["so"], 1)

                def back(c, par, st):
                    g, b = CH * c + st, st % 2
                    pe.wait_ge(s["msg"], g + 1)
                    pe.wait_ge(s["msgp"], g + 1)
                    after(pe, s["acc"], g - 1)
                    for j in range(JT):
                        i = mm(agg_ps(L, b), oh[b][:, j, :], msg[b][:, j, 0:L.AW], j == 0, j == JT - 1)
                    i.then_inc(s["agg"], 1)

                def emit(c, par, scores, sums):
                    past, pp = c - 1, 1 - par
                    if scores and L is L0:
                        front(c, par, 0)
                    if sums:
                        turn(past)
                    if scores and L is L1:
                        front(c, par, 0)
                    if scores:
                        front(c, par, 1)
                    if sums:
                        arrange(past)
                        carry_back(past)
                    if scores and L is L0:
                        front(c, par, 2)
                    if sums:
                        turn_back(past)
                    if scores and L is L1:
                        front(c, par, 2)
                    for st in range(2, CH):
                        if scores and st + 1 < CH:
                            front(c, par, st + 1)
                        for r in SUMMED[st] if sums else ():
                            back(past, pp, r)
                chunks(pe, emit)

            edge(L0)
            end_phase(pe, 2)

            def node1(k):
                for b in range(U):
                    pe.wait_ge(n1["mix"], U * k + b + 1)
                    pe.transpose(ps[:, 4 * b, 0:P], nbig[b][:, DM:2 * DM], ident[:, :]).then_inc(n1["tp"], 1)
                for b in range(U):
                    pe.wait_ge(n1["tc"], U * k + b + 1)
                    mm(ps[:, 4 * b + 1, 0:D], nT[b][:, 0, :], w_m2n[:, :]).then_inc(n1["y"], 1)
                for b in range(U):
                    pe.wait_ge(n1["x1"], U * k + b + 1)
                    for m in range(2):
                        i = pe.transpose(ps[:, 4 * b, m * P:(m + 1) * P], nres[b][:, m * P:(m + 1) * P], ident[:, :])
                    i.then_inc(n1["xt"], 1)
                for b in range(U):
                    pe.wait_ge(n1["xc"], U * k + b + 1)
                    for f in range(2):
                        for m in range(2):
                            i = mm(ps[:, 4 * b + 2, f * P:(f + 1) * P], w_q1[:, m, f * P:(f + 1) * P], nT[b][:, 2 + m, :],
                                   m == 0, m == 1)
                    i.then_inc(n1["q"], 1)
                for b in range(U):
                    pe.wait_ge(n1["qc"], U * k + b + 1)
                    after(pe, n1["split"], U * (k - 1) + b + 1)
                    for m in range(2):
                        i = mm(ps[:, 4 * b + 3, 0:D + 1], nT2[b][:, m, :], w_k1t[:, m, :], m == 0, m == 1)
                    i.then_inc(n1["qk"], 1)
            windows(pe, node1)
            end_phase(pe, 3)
            edge(L1)
            end_phase(pe, 4)

            def node2(k):
                for b in range(U):
                    pe.wait_ge(n2["mean"], U * k + b + 1)
                    for m in range(4):
                        src = nsum[b] if m < 2 else nrow[b]
                        i = pe.transpose(ps[:, 4 * b, m * P:(m + 1) * P], src[:, m % 2 * P:(m % 2 + 1) * P], ident[:, :])
                    i.then_inc(n2["tp"], 1)
                for b in range(U):
                    pe.wait_ge(n2["tc"], U * k + b + 1)
                    for m in range(4):
                        i = mm(ps[:, 4 * b + 1, 0:D], nT[b][:, m, :], (w_v1 if m < 2 else w_s1)[:, m % 2, :], m == 0, m == 3)
                    i.then_inc(n2["lin"], 1)
                for b in range(U):
                    pe.wait_ge(n2["x2"], U * k + b + 1)
                    for m in range(2):
                        i = pe.transpose(ps[:, 4 * b, m * P:(m + 1) * P], nh2[b][:, m * P:(m + 1) * P], ident[:, :])
                    i.then_inc(n2["xt"], 1)
                for b in range(U):
                    pe.wait_ge(n2["xc"], U * k + b + 1)
                    for f in range(4):
                        for m in range(2):
                            i = mm(ps[:, 4 * b + 2, f * P:(f + 1) * P], w_f1[:, m, f * P:(f + 1) * P], nT[b][:, m, :],
                                   m == 0, m == 1)
                    i.then_inc(n2["u"], 1)
                for b in range(U):
                    pe.wait_ge(n2["g"], U * k + b + 1)
                    for m in range(4):
                        i = mm(ps[:, 4 * b + 3, 0:D], nT2[b][:, m, :], w_f2[:, m, :], m == 0, m == 3)
                    i.then_inc(n2["f"], 1)
            windows(pe, node2)


N_WEIGHTS = 17


def kernel(x, src, dst, edge_attr_64, edge_weight, **w):
    import concourse.bacc as bacc
    from concourse.bass_utils import run_bass_kernel_spmd

    def arr(v):
        return np.asarray(v)

    def halves(m):
        m = arr(m)
        return m.reshape(-1, P, m.shape[1]).transpose(1, 0, 2)

    x, src, dst = arr(x), arr(src), arr(dst)
    xp = np.zeros((NP, D), x.dtype)
    xp[:N] = x

    def padded(v, fill):
        p = np.full((EP,) + v.shape[1:], fill, v.dtype)
        p[:E] = v
        return p

    def tiles(v):
        return v.reshape(NS, JT, P).transpose(0, 2, 1)

    dstp = padded(dst, NO_NODE)
    before = np.full(EP, -1, dst.dtype)
    before[1:] = dstp[:-1]
    behind = np.full(EP, -1, dst.dtype)
    behind[:-1] = dstp[1:]
    idx = np.concatenate([tiles(v) for v in (padded(src, 0), dstp, before, behind)], axis=2)
    sched = np.zeros((SG * P, 3), dst.dtype)
    sched[:, 1] = -P
    sched[:, 2] = -1
    lasts = [min(SUPER * (t + 1), E) - 1 for t in range(NS)]
    sched[:NS, 0] = dst[::SUPER]
    sched[:NS, 1] = dst[lasts]
    sched[1:NS, 2] = dst[lasts[:-1]]
    sched = sched.reshape(SG, P, 3).transpose(1, 0, 2)
    k1t = np.concatenate([arr(w["L1_gnn_wk"]).T, arr(w["L1_gnn_bk"])[:, None]], axis=1)

    arrays = {
        "xT": xp.T.reshape(2, P, NP).transpose(1, 0, 2), "x": xp, "idx": idx, "dst_row": dstp.reshape(NS, SUPER),
        "eaT": padded(arr(edge_attr_64), 0).T, "ew": tiles(padded(arr(edge_weight), 0)), "sched": sched,
        "w_n2m": halves(arr(w["L0_gnn_W_n2m"]).T),
        "w_qkvs": np.concatenate([arr(w["L0_gnn_" + n]).T for n in ("Wq", "Wk", "Wv", "Wskip")], axis=1),
        "b_qkvs": np.concatenate([arr(w["L0_gnn_" + n]) for n in ("bq", "bk", "bv", "bskip")])[None],
        "w_edge": arr(w["L0_gnn_W_edge"]), "w_et": arr(w["L0_gnn_We"]).T, "w_beta": arr(w["L0_gnn_Wbeta"]),
        "w_m2n": arr(w["L0_gnn_W_m2n"]).T, "w_q1": halves(w["L1_gnn_wq"]),
        "b_q1": arr(w["L1_gnn_bq"]).reshape(2, P).T, "w_k1t": halves(k1t), "w_v1": halves(w["L1_gnn_wv"]),
        "w_s1": halves(w["L1_gnn_ws"]), "w_f1": halves(w["L1_gnn_w_ff1"]), "b_f1": arr(w["L1_gnn_b_ff1"]).reshape(4, P).T,
        "w_f2": halves(w["L1_gnn_w_ff2"]),
        "rows1": np.concatenate([arr(w["L1_gnn_" + n]) for n in ("bv", "bs", "g1", "b1", "g2", "b2", "b_ff2")])[None],
        "we_be": np.concatenate([arr(w["L1_gnn_we"]).reshape(-1), arr(w["L1_gnn_be"])])[None],
    }
    arrays = {n: np.ascontiguousarray(v) for n, v in arrays.items()}
    nc = bacc.Bacc("TRN2", target_bir_lowering=False, num_devices=1)
    aps = {n: nc.dram_tensor("in_" + n, v.shape, mybir.dt.from_np(v.dtype), kind="ExternalInput").ap()
           for n, v in arrays.items()}
    out = nc.dram_tensor("out", (NP, D), F32, kind="ExternalOutput").ap()
    build(nc, aps, out)
    r = run_bass_kernel_spmd(nc, [{"in_" + n: v for n, v in arrays.items()}], core_ids=[0])
    return r.results[0]["out"][:N]
```

```python
from contextlib import ExitStack

import numpy as np
import concourse.bass as bass
from concourse import mybir

F32, BF16, I32 = mybir.dt.float32, mybir.dt.bfloat16, mybir.dt.int32
ALU = mybir.AluOpType
ACT = mybir.ActivationFunctionType
AX = mybir.AxisListType

P = 128
N, E, D = 6250, 200000, 256
DM, DR, HEADS = 128, 64, 4
OUTC = DM // HEADS
NW = 52
NP = NW * P
JT = 4
SUPER = JT * P
NS = -(-E // SUPER)
EP = NS * SUPER
REAL_W = -(-N // P)
CH = 8
NI = CH * JT
NC = -(-(NS + REAL_W - 1) // CH)
NPAIR = NC * CH
SG = -(-NS // P)
BIG = 1e30
PLACES = 4
ACCS = 4
OHS = 4
SUMMED = (((), (), (0,), (1, 2), (3,), (4, 5), (6,), (7,)),
          ((), (), (0,), (1,), (2, 3), (4,), (5, 6), (7,)))
ONE_HOTS = ((), (), (2, 3), (4,), (5, 6), (7,), (), ())
NO_NODE = 1 << 20
U = 4
EPS = 1e-5


def after(eng, sem, value):
    if not (isinstance(value, int) and value <= 0):
        eng.wait_ge(sem, value)


def stand_by(eng, gate, sem, value):
    if isinstance(value, int):
        after(eng, sem, value)
    else:
        eng.wait_ge(sem, value)
        eng.sem_inc(gate, 1)


def build(nc, a, out):
    ctx = ExitStack()
    with ctx:
        def sb(name, shape, dt=F32):
            return ctx.enter_context(nc.sbuf_tensor(name, shape, dt))

        def sem(name):
            return ctx.enter_context(nc.semaphore(name))

        def dram(name, shape, dt=F32):
            return nc.dram_tensor(name, shape, dt, kind="Internal").ap()

        kv_d = dram("kv_d", (NP, 2 * DM))
        q0_d = dram("q0_d", (NW, P, 3 * DM), BF16)
        xr_d = dram("xr_d", (NW, P, DM))
        acc0_d = dram("acc0_d", (NPAIR + 1, P, DM + HEADS))
        x1_d = dram("x1_d", (NP, D))
        q1_d = dram("q1_d", (NW, P, 3 * (D + 1)), BF16)
        idx_d = dram("idx_d", (NC, P, CH * 3 * JT), I32)
        acc1_d = dram("acc1_d", (NPAIR + 1, P, D + 1))

        ident = sb("ident", [P, P])
        iota_row = sb("iota_row", [P, P])
        iota_col = sb("iota_col", [P, 1])
        ones = sb("ones", [P, P])
        tri = sb("tri", [P, P])
        sel_j = {4: sb("sel_j4", [P, NI]), 1: sb("sel_j1", [P, NI])}
        sel_h = {4: sb("sel_h4", [P, 4]), 1: sb("sel_h1", [P, 1])}
        sel_ht = {4: sb("sel_ht4", [4, P]), 1: sb("sel_ht1", [1, P])}
        minus_half = sb("minus_half", [P, 1])
        zero_rows = sb("zero_rows", [P, D + 1])
        w_n2m = sb("w_n2m", [P, 2, DM])
        w_qkvs = sb("w_qkvs", [P, 4 * DM])
        b_qkvs = sb("b_qkvs", [P, 4 * DM])
        w_edge = sb("w_edge", [DR, DR])
        w_et = sb("w_et", [DR, DM])
        w_c = sb("w_c", [P, DM])
        w_beta = sb("w_beta", [P, 3, DM])
        w_m2n = sb("w_m2n", [P, D])
        w_q1 = sb("w_q1", [P, 2, D])
        b_q1 = sb("b_q1", [P, 2])
        w_k1t = sb("w_k1t", [P, 2, D + 1])
        w_v1 = sb("w_v1", [P, 2, D])
        w_s1 = sb("w_s1", [P, 2, D])
        w_f1 = sb("w_f1", [P, 2, 2 * D])
        b_f1 = sb("b_f1", [P, 4])
        w_f2 = sb("w_f2", [P, 4, D])
        rows1 = sb("vecs1", [P, 7, D])
        we_be = sb("we_be", [P, 2])
        BV, BS, G1, B1, G2, B2, BF2 = range(7)
        sched = sb("sched", [P, SG, 3], I32)
        sched_w = sb("sched_w", [P, SG, 3], I32)
        sched_f = sb("sched_f", [P, SG, 3])
        n_win = sb("n_win", [P, SG])
        d_win = sb("d_win", [P, SG])
        start = sb("start", [P, SG])
        pair_no = sb("pair_no", [P, NPAIR])
        begun = sb("begun", [P, SG, NPAIR])
        stepped = sb("stepped", [P, SG, NPAIR])
        t_of = sb("t_of", [P, NPAIR])
        w_of = sb("w_of", [P, NPAIR])
        base_tab = sb("base_tab", [P, NPAIR])
        node_tab = sb("node_tab", [P, NPAIR])
        keep_tab = sb("keep_tab", [P, NPAIR])
        tw_int = sb("tw_int", [1, 2, NPAIR], I32)
        last_pair = sb("last_pair", [P, 4])
        last_int = sb("last_int", [1, P], I32)

        ps = ctx.enter_context(nc.psum_tensor("ps", [P, 8, 512], F32))

        idx = [sb(f"idx{b}", [P, CH, 3 * JT], I32) for b in range(2)]
        dst_row = [sb(f"dst_row{b}", [P, SUPER], I32) for b in range(PLACES)]
        qw = [sb(f"qw{b}", [P, 3 * (D + 1)], BF16) for b in range(PLACES)]
        ea = [sb(f"ea{b}", [P, SUPER]) for b in range(PLACES)]
        ew = [sb(f"ew{b}", [P, NI]) for b in range(2)]
        rows = [sb(f"rows{b}", [P, CH, JT, D]) for b in range(2)]
        oht = [sb(f"oht{b}", [P, SUPER], BF16) for b in range(PLACES)]
        oh = sb("oh", [P, OHS, JT, P])
        prod = sb("prod", [P, JT, D])
        score = [sb(f"score{b}", [P, NI, HEADS]) for b in range(2)]
        rel_first = [sb(f"rel_first{b}", [HEADS, 1]) for b in range(2)]
        rel = [sb(f"rel{b}", [P, CH, JT]) for b in range(2)]
        same = sb("same", [P, NI])
        qb = sb("qb", [P, NI])
        weighed = sb("weighed", [P, NI])
        inside = sb("inside", [P, NI])
        outside = sb("outside", [P, NI])
        biased = sb("biased", [P, NI, HEADS])
        pen = sb("pen", [P, NI, HEADS])
        pen_r = sb("pen_r", [P, P + 1])
        fwd = sb("fwd", [P, P])
        bwd = sb("bwd", [P, P])
        full = sb("full", [P, P])
        spread = sb("spread", [P, 4, NI])
        runs = sb("runs", [HEADS, 4, NI + 1])
        pen_f = sb("pen_f", [HEADS, NI])
        pen_b = sb("pen_b", [HEADS, NI])
        run_f = [sb(f"run_f{b}", [HEADS, NI + 1]) for b in range(2)]
        run_b = sb("run_b", [HEADS, NI + 1])
        carry = sb("carry", [HEADS, 2, NI])
        carry_p = sb("carry_p", [P, 2, NI])
        carry_r = sb("carry_r", [P, 2])
        below = sb("below", [P, NI * HEADS])
        prob = [sb(f"prob{b}", [P, NI, HEADS]) for b in range(2)]
        shrink_in = sb("shrink_in", [HEADS, 1])
        shrink = sb("shrink", [HEADS, 1])
        shrink_d = sb("shrink_d", [HEADS, HEADS])
        first_oh = sb("first_oh", [HEADS, P])
        rescale = sb("rescale", [P, HEADS])
        msg = [sb(f"msg{b}", [P, JT, D + 1]) for b in range(OHS)]
        acc = [sb(f"acc{b}", [P, D + 1]) for b in range(ACCS)]
        acc_scaled = sb("acc_scaled", [P, D + 1])

        space = [r[:, :, :, :].rearrange("p s j n -> p (s j n)") for r in rows]
        used = [0] * len(rows)

        def slot_buffers(*shape):
            bufs = []
            for b in range(U):
                size, half = int(np.prod(shape)), b % len(rows)
                buf = space[half][:, used[half]:used[half] + size]
                used[half] += size
                bufs.append(buf.rearrange("p (k n) -> p k n", n=shape[1]) if len(shape) == 2 else buf)
            return bufs

        def norm_buffers():
            return [slot_buffers(n) for n in (6, 2, 1, 1)]

        nrow, nacc, nsum, nres = slot_buffers(D), slot_buffers(D + 1), slot_buffers(D + 1), slot_buffers(D + 1)
        nT, nT2, nden = slot_buffers(4, P), slot_buffers(4, P), slot_buffers(HEADS)
        shared = list(used)
        nx, nh, nbig, nxr, nlow, nz = (slot_buffers(2, P), slot_buffers(D), slot_buffers(4 * DM), slot_buffers(DM),
                                       slot_buffers(D + 1), slot_buffers(8))
        norm_x1 = norm_buffers()
        nq = [sb(f"nq{b}", [P, 3, D + 1], BF16) for b in range(U)]
        used[:] = shared
        nskip, natt, nx2, nup, nffn, nagain, nend = [slot_buffers(D) for _ in range(7)]
        norm_att, norm_ffn, norm_end = norm_buffers(), norm_buffers(), norm_buffers()

        s_w = sem("weights_loaded")
        s_sched = sem("sched_loaded")
        s_iota = sem("iotas_ready")
        s_zst = sem("zeros_stored")
        s_cst = sem("constants_ready")
        s_win = sem("windows_ready")
        s_start = sem("starts_ready")
        s_stp = sem("starts_copied")
        s_begun = sem("begun_and_last_ready")
        s_pairs = sem("pairs_and_last_ready")
        s_tab = sem("tables_ready")
        s_wcp, s_wc = sem("edge_weight_product"), sem("edge_weight_ready")
        s_phase = sem("phase_done")
        phases = [0]

        def end_phase(eng, n):
            eng.drain().then_inc(s_phase, 1)
            eng.wait_ge(s_phase, 5 * n)

        def window(ap, w):
            return ap[bass.ds(w, 1)].rearrange("o p c -> (o p) c")

        def node_rows(ap, w):
            return ap[bass.ds(w * P, P), :]

        def slots(name):
            return [sem(f"{name}{b}") for b in range(U)]

        n0 = dict(load=slots("n0_loaded"), store=slots("n0_stored"), m=sem("n0_m"), mT=sem("n0_mT"),
                  big=sem("n0_projected"), kv=sem("n0_biased"), res=sem("n0_split"))
        loaded = slots("n_loaded")
        n1 = dict(load=loaded, store=slots("n1_stored"), z=sem("n1_gate_sum"), en=sem("n1_gate_exp"),
                  mix=sem("n1_mixed"), tp=sem("n1_mixedT"), tc=sem("n1_mixedT_copied"), y=sem("n1_out"),
                  x1=sem("n1_x1"), xt=sem("n1_x1T"), xc=sem("n1_x1T_copied"),
                  q=sem("n1_qT"), qc=sem("n1_qT_copied"), qk=sem("n1_qk"), split=sem("n1_split"))
        LOADED1 = 48 * (NW // U)
        n2 = dict(load=loaded, store=slots("n2_stored"), mean=sem("n2_attention"), tp=sem("n2_T"),
                  tc=sem("n2_T_copied"), lin=sem("n2_linear"), x2=sem("n2_x2"),
                  xt=sem("n2_x2T"), xc=sem("n2_x2T_copied"), u=sem("n2_up"), g=sem("n2_gelu"), f=sem("n2_ffn"),
                  skip=sem("n2_skip"), up=sem("n2_x2_bias"), end=sem("n2_x1_bias"), res=sem("n2_result"))

        roots1 = [(sem("n1_var"), sem("n1_rstd")) + tuple(norm_x1)]
        roots2 = [(sem(f"n2_var{r}"), sem(f"n2_rstd{r}")) + tuple(bufs) for r, bufs in enumerate((norm_att, norm_ffn, norm_end))]

        def edge_sems(n):
            names = ("oht", "e", "q", "score", "masked", "turned", "pens", "ends", "arranged", "carries", "spreadback",
                     "full", "fullT", "below", "prob", "shrink_in", "shrink", "so_in", "so", "msg", "msgp", "agg",
                     "acc", "first", "added")
            s = {x: sem(f"l{n}_{x}") for x in names if n == 0 or x not in ("e", "added")}
            for x in ("ld_row", "ld_q", "ld_ea", "gathered", "stored"):
                s[x] = [sem(f"l{n}_{x}{b}") for b in range(2)]
            return s

        s_l = [edge_sems(0), edge_sems(1)]
        s_kept = sem("indices_kept")
        s_idx = [sem(f"ld_idx{st}") for st in range(CH)]

        block = ctx.enter_context(nc.Block())

        class Layer:
            pass

        L0, L1 = Layer(), Layer()
        L0.s, L0.H, L0.D, L0.table, L0.q_d, L0.acc_d, L0.AW = s_l[0], HEADS, DM, kv_d, q0_d, acc0_d, DM + HEADS
        L1.s, L1.H, L1.D, L1.table, L1.q_d, L1.acc_d, L1.AW = s_l[1], 1, D, x1_d, q1_d, acc1_d, D + 1
        L0.QD, L1.QD = DM, D + 1
        L0.summed, L1.summed = SUMMED
        L0.idx_before, L1.idx_before = 0, 16 * NC
        L0.idx_sem, L1.idx_sem = s_idx, [s_idx[0]] * CH
        for L in (L0, L1):
            L.R = NI * L.H

        def chunks(eng, emit):
            emit(0, 0, True, False)
            for c in range(1, 4):
                emit(c, c % 2, True, True)
            with eng.Fori(2, NC // 2) as k:
                emit(2 * k, 0, True, True)
                emit(2 * k + 1, 1, True, True)
            if NC % 2:
                emit(NC - 1, 0, True, True)
            emit(NC, NC % 2, False, True)

        def more(c, st):
            return not (isinstance(c, int) and CH * c + st >= NPAIR)

        def pipeline(eng, *items):
            def step(n, k, i):
                for item in items:
                    at = []
                    for stage, lag in item if isinstance(item, list) else [item]:
                        turn, slot = divmod(i - lag, U)
                        if not isinstance(n, int) or 0 <= n - lag < NW:
                            at.append(stage(n - lag, slot, k + turn))
                    while isinstance(item, list) and at:
                        at = [stage for stage in at if next(stage, "ended") != "ended"]
                        eng.drain()

            lags = [lag for item in items for stage, lag in (item if isinstance(item, list) else [item])]
            for n in range(min(0, *lags), 2 * U):
                step(n, 0, n)
            with eng.Fori(2, NW // U - 1) as k:
                for i in range(U):
                    step(U * k + i, k, i)
            for n in range(NW - U, NW + max(lags)):
                step(n, 0, n)

        def q_ps(L, b):
            if L.H == HEADS:
                return ps[:, 2 * b, :]
            return ps[:, 2 * b:2 * b + 2, :].rearrange("p k n -> p (k n)")

        def e_ps(b):
            return ps[:, 2 * b + 1, :]

        def agg_ps(L, b):
            return ps[:, 4 + b, 0:L.AW]

        turn_ps = ps[:, 6, :]
        arr_ps, back_ps, so_ps = ps[:, 7, 0:P], ps[:, 7, P:P + 2 * NI], ps[:, 6, 3 * P:3 * P + HEADS]
        qb_ps = [ps[:, 7, 208 + 3 * NI * b:208 + 3 * NI * (b + 1)] for b in range(2)]

        @block.sync
        def _(sp):
            gate = sem("sp_gate")

            def wait(s, value):
                stand_by(sp, gate, s, value)

            sp.dma_start(sched[:, :, :], a["sched"]).then_inc(s_sched, 16)
            loads = [
                (w_n2m[:, :, :], a["w_n2m"]), (w_qkvs[:, :], a["w_qkvs"]), (w_edge[:, :], a["w_edge"]),
                (w_et[:, :], a["w_et"]), (w_m2n[:, :], a["w_m2n"]), (w_q1[:, :, :], a["w_q1"]), (b_q1[:, :], a["b_q1"]),
                (w_k1t[:, :, :], a["w_k1t"]), (w_v1[:, :, :], a["w_v1"]), (w_s1[:, :, :], a["w_s1"]),
                (w_f1[:, :, :], a["w_f1"]), (b_f1[:, :], a["b_f1"]), (w_f2[:, :, :], a["w_f2"]),
                (b_qkvs[:, :], a["b_qkvs"].partition_broadcast(P)),
                (w_beta[:, :, :].rearrange("p k n -> p (k n)"), a["w_beta"].partition_broadcast(P)),
                (rows1[:, :, :].rearrange("p k n -> p (k n)"), a["rows1"].partition_broadcast(P)),
                (we_be[:, :], a["we_be"].partition_broadcast(P)),
            ]
            for dst, src in loads:
                sp.dma_start(dst, src).then_inc(s_w, 16)
            assert len(loads) == N_WEIGHTS

            def n0_load(w, b, k):
                wait(n0["m"], w - U + 1)
                sp.dma_start(nx[b][:, :, :], a["xT"][:, :, bass.ds(w * P, P)]).then_inc(n0["load"][b], 16)

            def n0_store_q(w, b, k):
                wait(n0["res"], w + 1)
                sp.dma_start(window(q0_d, w), nq[b][:, :, 0:DM]).then_inc(n0["store"][b], 16)
            pipeline(sp, (n0_load, -3), (n0_store_q, 2))
            for b in range(U):
                sp.wait_ge(n0["store"][b], 48 * (NW // U))
            sp.wait_ge(s_zst, 32)
            sp.wait_ge(s_tab, 1)
            end_phase(sp, 1)

            def edge_loads(L):
                s = L.s

                def free_idx(c):
                    wait(s["masked"], c - 1)
                    wait(s["gathered"][0], 64 * (CH // 2) * (c - 1))
                    wait(s["gathered"][1], 64 * (CH // 2) * (c - 1))

                def load_idx(c, par, steps):
                    for st in steps:
                        t = sp.value_load(tw_int[0:1, 0, bass.ds(CH * c + st, 1)])
                        sp.dma_start(idx[par][:, st, :], a["idx"][bass.ds(t, 1)].rearrange("o p c -> (o p) c"))\
                          .then_inc(s_idx[st], 16)

                def keep_idx(c, par):
                    for st in range(CH):
                        wait(s_idx[st], 16 * (c + 1))
                    sp.dma_start(window(idx_d, c), idx[par][:, :, :].rearrange("p s j -> p (s j)")).then_inc(s_kept, 16)

                def load_idx_chunk(c, par):
                    wait(s_idx[0], L.idx_before + 16 * c)
                    sp.dma_start(idx[par][:, :, :].rearrange("p s j -> p (s j)"), window(idx_d, c)).then_inc(s_idx[0], 16)

                def load_pair(g, par, st):
                    place = st % PLACES
                    t = sp.value_load(tw_int[0:1, 0, bass.ds(g, 1)])
                    w = sp.value_load(tw_int[0:1, 1, bass.ds(g, 1)])
                    b = place % 2
                    sp.dma_start(dst_row[place][:, :], a["dst_row"][bass.ds(t, 1), :].partition_broadcast(P))\
                      .then_inc(s["ld_row"][b], 16)
                    sp.dma_start(qw[place][:, 0:3 * L.QD], window(L.q_d, w))\
                      .then_inc(s["ld_q"][b], 16)
                    if L is L0:
                        sp.dma_start(ea[place][0:DR, :], a["eaT"][:, bass.ds(t * SUPER, SUPER)])\
                          .then_inc(s["ld_ea"][b], 16)
                    else:
                        sp.dma_start(ew[par][:, st * JT:(st + 1) * JT], a["ew"][bass.ds(t, 1)].rearrange("o p c -> (o p) c"))\
                          .then_inc(s["ld_ea"][b], 16)

                def load_ahead(c, par, st):
                    g, b, n = CH * c + st, st % 2, CH // 2 * c + st // 2
                    wait(s["oht"], g - 1)
                    if st == 2:
                        wait(s["first"], c + 1)
                    wait(s["q"], g - 1)
                    wait(s["ld_row"][b], 16 * (n + 1))
                    wait(s["ld_q"][b], 16 * (n + 1))
                    wait(s["ld_ea"][b], 16 * (n + 1))
                    if L is L0:
                        wait(s["e"], g - 1)
                    elif st == CH - 2:
                        wait(s["masked"], c)
                    load_pair(g + 2, (par + (st + 2) // CH) % 2, (st + 2) % CH)

                def emit(c, par, scores, sums):
                    if not scores:
                        return
                    last = isinstance(c, int) and c == NC - 1
                    if not sums:
                        if L is L0:
                            load_idx(0, 0, range(CH))
                        else:
                            load_idx_chunk(0, 0)
                        for st in range(2):
                            load_pair(st, 0, st)
                    for st in range(CH):
                        if more(c, st + 2):
                            load_ahead(c, par, st)
                        if st == (1 if L is L0 else 2) and not last:
                            free_idx(c + 1)
                            if L is L0:
                                wait(s_kept, 16 * c)
                            else:
                                load_idx_chunk(c + 1, 1 - par)
                        if L is L0 and st > 0 and not last:
                            load_idx(c + 1, 1 - par, (st - 1,) if st < CH - 1 else (st - 1, st))
                    if L is L0:
                        keep_idx(c, par)
                chunks(sp, emit)
                for b in range(2):
                    sp.wait_ge(s["stored"][b], 16 * NPAIR // 2)
                sp.wait_ge(s_kept, 16 * NC)

            edge_loads(L0)
            end_phase(sp, 2)

            def n1_load(w, b, k):
                wait(n1["x1"], w - U + 1)
                sp.dma_start(nacc[b][:, 0:L0.AW], window(acc0_d, sp.value_load(last_int[0:1, bass.ds(w, 1)]))).then_inc(n1["load"][b], 16)
                sp.dma_start(nxr[b][:, :], window(xr_d, w)).then_inc(n1["load"][b], 16)
                sp.dma_start(nrow[b][:, :], node_rows(a["x"], w)).then_inc(n1["load"][b], 16)

            def n1_store_x1(w, b, k):
                wait(n1["x1"], w + 1)
                sp.dma_start(node_rows(x1_d, w), nres[b][:, 0:D]).then_inc(n1["store"][b], 16)

            def n1_store_q(w, b, k):
                wait(n1["split"], w + 1)
                sp.dma_start(window(q1_d, w).rearrange("p (k n) -> p k n", k=3), nq[b][:, :, :])\
                  .then_inc(n1["store"][b], 16)
            pipeline(sp, (n1_load, -1), (n1_store_x1, 3), (n1_store_q, 4))
            for b in range(U):
                sp.wait_ge(n1["store"][b], 32 * (NW // U))
            end_phase(sp, 3)

            edge_loads(L1)
            end_phase(sp, 4)

            def n2_load(w, b, k):
                wait(n2["tp"], w - U + 1)
                wait(n2["skip"], w - U + 1)
                wait(n2["load"][b], LOADED1 + 48 * k)
                sp.dma_start(nacc[b][:, :], window(acc1_d, sp.value_load(last_int[0:1, bass.ds(w, 1)]))).then_inc(n2["load"][b], 16)
                sp.dma_start(nrow[b][:, :], node_rows(x1_d, w)).then_inc(n2["load"][b], 16)

            def n2_load_again(w, b, k):
                wait(roots2[2][0], w - U + 1)
                wait(n2["load"][b], LOADED1 + 48 * k + 32)
                sp.dma_start(nagain[b][:, :], node_rows(x1_d, w)).then_inc(n2["load"][b], 16)

            def n2_store(w, b, k):
                wait(n2["res"], w + 1)
                sp.dma_start(node_rows(out, w), nres[b][:, 0:D]).then_inc(n2["store"][b], 16)
            pipeline(sp, (n2_load, -2), (n2_load_again, 1), (n2_store, 6))
            for b in range(U):
                sp.wait_ge(n2["store"][b], 16 * (NW // U))

        @block.gpsimd
        def _(pool):
            pool.iota(iota_row[:, :], [[1, P]], base=0, channel_multiplier=0, allow_small_or_imprecise_dtypes=True)
            pool.iota(iota_col[:, :], [[0, 1]], base=0, channel_multiplier=1, allow_small_or_imprecise_dtypes=True)
            pool.iota(pair_no[:, :], [[1, NPAIR]], base=0, channel_multiplier=0, allow_small_or_imprecise_dtypes=True)
            for h in (HEADS, 1):
                pool.memset(sel_j[h][:, :], 1.0)
                pool.memset(sel_h[h][:, :], 0.0)
                pool.memset(sel_ht[h][:, :], 0.0)
            pool.memset(minus_half[:, :], -0.5)
            pool.memset(pen_r[:, :], 0.0)
            pool.memset(runs[:, :, :], -BIG)
            for b in range(2):
                pool.memset(run_f[b][:, :], -BIG)
            pool.memset(run_b[:, :], -BIG)
            pool.memset(w_c[:, :], 0.0)
            pool.memset(acc[(CH - 1) % ACCS][:, :], 0.0)
            for place in range(PLACES):
                pool.memset(ea[place][:, :], 0.0)
            pool.memset(zero_rows[:, :], 0.0)
            pool.drain()
            for h in (HEADS, 1):
                pool.affine_select(out=sel_j[h][:, :], in_=sel_j[h][:, :], compare_op=ALU.is_ge, fill=0.0, base=0,
                                   pattern=[[-h, NI]], channel_multiplier=1)
                for m in range(P // h):
                    pool.affine_select(out=sel_h[h][:, :], in_=sel_h[h][:, :], compare_op=ALU.not_equal, fill=1.0,
                                       base=-h * m, pattern=[[-1, h]], channel_multiplier=1) if h > 1 else None
                    pool.drain() if h > 1 else None
            pool.memset(sel_h[1][:, :], 1.0)
            pool.memset(sel_ht[1][:, :], 1.0)
            v = sel_ht[HEADS][:, :].rearrange("p (m c) -> p m c", c=HEADS)
            pool.affine_select(out=v, in_=v, compare_op=ALU.not_equal, fill=1.0, base=0,
                               pattern=[[0, P // HEADS], [-1, HEADS]], channel_multiplier=1)
            pool.drain()
            for h in (HEADS, 1):
                pool.affine_select(out=sel_j[h][:, :], in_=sel_j[h][:, :], compare_op=ALU.is_ge, fill=0.0, base=h - 1,
                                   pattern=[[h, NI]], channel_multiplier=-1)
            pool.drain().then_inc(s_iota, 1)
            pool.dma_start(acc0_d[NPAIR], zero_rows[:, 0:L0.AW]).then_inc(s_zst, 16)
            pool.dma_start(acc1_d[NPAIR], zero_rows[:, 0:L1.AW]).then_inc(s_zst, 16)
            end_phase(pool, 1)

            pool_gate = sem("pool_gate")

            def gathers(L):
                s = L.s

                def emit(c, par, scores, sums):
                    for st in range(CH if scores else 0):
                        b, n = st % 2, CH // 2 * c + st // 2
                        pool.wait_ge(L.idx_sem[st], L.idx_before + 16 * (c + 1))
                        after(pool, s["msg" if L is L0 else "msgp"], CH * (c - 2) + st + 1)
                        after(pool, s["gathered"][b], 64 * n)
                        pool.sem_inc(pool_gate, 1)
                        for j in range(JT):
                            pool.indirect_dma_start(
                                out=rows[par][:, st, j, :], out_offset=None, in_=L.table,
                                in_offset=bass.IndirectOffsetOnAxis(ap=idx[par][:, st, j:j + 1], axis=0))\
                                .then_inc(s["gathered"][b], 16)
                chunks(pool, emit)

            def root(norm):
                var_ready, rstd_ready, _, _, ve, rstd = norm

                def stage(w, b, k):
                    pool.wait_ge(var_ready, w + 1)
                    pool.tensor_tensor(rstd[b][:, :], ve[b][:, :], minus_half[:, :], ALU.pow).then_inc(rstd_ready, 1)
                return stage

            gathers(L0)
            end_phase(pool, 2)
            pipeline(pool, (root(roots1[0]), 2))
            end_phase(pool, 3)
            gathers(L1)
            end_phase(pool, 4)

            def n2_skip(w, b, k):
                pool.wait_ge(n2["load"][b], LOADED1 + 48 * k + 32)
                after(pool, roots2[0][0], w - U + 1)
                pool.tensor_tensor(nskip[b][:, :], nrow[b][:, :], rows1[:, BS, :], ALU.add).then_inc(n2["skip"], 1)

            def n2_x2_bias(w, b, k):
                pool.wait_ge(n2["x2"], w + 1)
                after(pool, roots2[1][0], w - U + 1)
                pool.tensor_tensor(nup[b][:, :], nx2[b][:, :], rows1[:, BF2, :], ALU.add).then_inc(n2["up"], 1)

            def n2_x1_bias(w, b, k):
                pool.wait_ge(n2["load"][b], LOADED1 + 48 * (k + 1))
                pool.tensor_tensor(nagain[b][:, :], nagain[b][:, :], rows1[:, B2, :], ALU.add).then_inc(n2["end"], 1)
            pipeline(pool, (n2_skip, -1), (n2_x1_bias, 4), (n2_x2_bias, 2), (root(roots2[1]), 4), (root(roots2[0]), 1),
                     (root(roots2[2]), 5))

        @block.scalar
        def _(act):
            gate = sem("act_gate")

            def wait(s, value):
                stand_by(act, gate, s, value)

            act.wait_ge(s_wcp, 1)
            act.activation(w_c[0:DR, :], ps[0:DR, 7, 0:DM], ACT.Copy).then_inc(s_wc, 1)

            def n0_messagesT(w, b, k):
                wait(n0["m"], w + 1)
                wait(n0["big"], w - U + 1)
                act.activation(nT[b][:, 0, :], ps[:, 2 * b, 0:P], ACT.Copy).then_inc(n0["mT"], 1)
            def n0_store_kv(w, b, k):
                wait(n0["kv"], w + 1)
                act.dma_start(node_rows(kv_d, w), nres[b][:, 0:2 * DM]).then_inc(n0["store"][b], 16)
                act.dma_start(window(xr_d, w), nxr[b][:, :]).then_inc(n0["store"][b], 16)
            pipeline(act, (n0_messagesT, 0), (n0_store_kv, 1))
            end_phase(act, 1)

            def edge(L):
                s = L.s

                def spread_nodes(c, st):
                    c, st = c + st // CH, st % CH
                    g, b = CH * c + st, st % 2
                    wait(s["ld_row"][b], 16 * (CH // 2 * c + st // 2 + 1))
                    wait(s["q"], g - PLACES + 1)
                    act.activation(oht[st % PLACES][:, :], dst_row[st % PLACES][:, :], ACT.Abs, scale=-1.0,
                                   bias=node_tab[:, bass.ds(g, 1)])

                def spread_nodes_end(st):
                    act.activation(oht[st % PLACES][:, :], oht[st % PLACES][:, :], ACT.Relu, scale=-1.0, bias=ones[:, 0:1])\
                       .then_inc(s["oht"], 1)

                def edge_nodes(c, par, st):
                    for j in range(JT):
                        act.activation(oh[:, st % OHS, j, :], iota_row[:, :], ACT.Abs, scale=-1.0,
                                       bias=rel[par][:, st, j:j + 1])

                def edge_nodes_end(first, count):
                    o = oh[:, first % OHS:first % OHS + count, :, :]
                    act.activation(o, o, ACT.Relu, scale=-1.0, bias=ones[:, 0:1])

                def messages(c, par, st):
                    pr = prob[par][:, st * JT:(st + 1) * JT, 0:L.H]
                    wait(s["agg"], CH * c + st - OHS + 1)
                    if L is L0:
                        act.activation(msg[st % OHS][:, :, 0:L.AW].rearrange("p j (h c) -> p j h c", h=HEADS)[:, :, :, OUTC],
                                       pr, ACT.Copy).then_inc(s["msgp"], 1)
                    else:
                        for j in range(JT):
                            act.activation(msg[st % OHS][:, j, 0:D], rows[par][:, st, j, :], ACT.Copy, scale=pr[:, j, :])
                        act.activation(msg[st % OHS][:, :, D:D + 1], pr, ACT.Copy).then_inc(s["msgp"], 1)

                def store(c, st):
                    g, b = CH * c + st, st % 2
                    after(act, s["acc"], g + 1)
                    after(act, s["stored"][b], 16 * (CH // 2 * c + st // 2))
                    act.dma_start(window(L.acc_d, g), acc[st % ACCS][:, 0:L.AW]).then_inc(s["stored"][b], 16)

                def emit(c, par, scores, sums):
                    past, pp = c - 1, 1 - par
                    one_hot = scores and L is L0
                    if one_hot and not sums:
                        for st in range(2):
                            spread_nodes(c, st)
                        act.drain()
                        for st in range(2):
                            spread_nodes_end(st)
                    if sums:
                        wait(s["turned"], past + 1)
                        act.activation(pen_r[0:L.R, 0:P], turn_ps[0:L.R, P:2 * P], ACT.Copy).then_inc(s["pens"], 1)
                        if not (isinstance(past, int) and past == 0):
                            for r in L.summed[CH - 2] + L.summed[CH - 1]:
                                store(past - 1, r)
                    if one_hot:
                        for st in (2, 3):
                            spread_nodes(c, st)
                        act.drain()
                        for st in (2, 3):
                            spread_nodes_end(st)
                    if sums and L is L0:
                        wait(s["agg"], CH * past - OHS + 2)
                        edge_nodes(past, pp, 0)
                        edge_nodes(past, pp, 1)
                        act.drain()
                        edge_nodes_end(0, 2)
                    if sums:
                        wait(s["shrink_in"], past + 1)
                        act.activation(shrink[0:L.H, :], shrink_in[0:L.H, :], ACT.Exp).then_inc(s["shrink"], 1)
                        wait(s["below"], past + 1)
                        wait(s["agg"], CH * (past - 1))
                        act.activation(prob[pp][:, :, 0:L.H], below[:, 0:L.R].rearrange("p (n h) -> p n h", h=L.H),
                                       ACT.Exp).then_inc(s["prob"], 1)
                        act.drain()
                    for st in range(2, CH):
                        for r in L.summed[st] if sums else ():
                            messages(past, pp, r)
                        if one_hot and more(c, st + 2):
                            spread_nodes(c, st + 2)
                            act.drain()
                            spread_nodes_end((st + 2) % CH)
                        ahead = ONE_HOTS[st] if sums and L is L0 else ()
                        for r in ahead:
                            wait(s["agg"], CH * past + r - OHS + 1)
                            edge_nodes(past, pp, r)
                        if ahead:
                            act.drain()
                            edge_nodes_end(ahead[0], len(ahead))
                        for r in L.summed[st - 2] if sums else ():
                            store(past, r)
                    if not scores:
                        for r in L.summed[CH - 2] + L.summed[CH - 1]:
                            store(past, r)
                chunks(act, emit)

            edge(L0)
            end_phase(act, 2)

            def n1_gate(w, b, k):
                wait(n1["z"], w + 1)
                act.activation(nz[b][:, 3:4], nz[b][:, 2:3], ACT.Exp, scale=-1.0).then_inc(n1["en"], 1)

            def n1_mixedT(w, b, k):
                wait(n1["tp"], w + 1)
                act.activation(nT[b][:, 0, :], ps[:, 2 * b, 0:P], ACT.Copy).then_inc(n1["tc"], 1)

            def n1_x1T(w, b, k):
                wait(n1["xt"], w + 1)
                act.activation(nT[b][:, 2:4, :], ps[:, 2 * b, 0:2 * P].rearrange("p (k n) -> p k n", k=2), ACT.Copy)\
                   .then_inc(n1["xc"], 1)

            def n1_qT(w, b, k):
                wait(n1["q"], w + 1)
                for m in range(2):
                    i = act.activation(nT2[b][:, m, :], ps[:, 2 * b + 1, m * P:(m + 1) * P], ACT.Identity,
                                       bias=b_q1[:, m:m + 1])
                i.then_inc(n1["qc"], 1)
            pipeline(act, (n1_x1T, 3), (n1_qT, 3), (n1_mixedT, 1), (n1_gate, 0))
            end_phase(act, 3)
            edge(L1)
            end_phase(act, 4)

            def n2_T(w, b, k):
                wait(n2["tp"], w + 1)
                act.activation(nT[b][:, :, :], ps[:, 2 * b, :].rearrange("p (k n) -> p k n", k=4), ACT.Copy)\
                   .then_inc(n2["tc"], 1)

            def n2_x2T(w, b, k):
                wait(n2["xt"], w + 1)
                act.activation(nT[b][:, 0:2, :], ps[:, 2 * b, 0:2 * P].rearrange("p (k n) -> p k n", k=2), ACT.Copy)\
                   .then_inc(n2["xc"], 1)

            def n2_gelu(w, b, k):
                wait(n2["u"], w + 1)
                for m in range(4):
                    i = act.activation(nT2[b][:, m, :], ps[:, 2 * b + 1, m * P:(m + 1) * P], ACT.Gelu_apprx_tanh,
                                       bias=b_f1[:, m:m + 1])
                i.then_inc(n2["g"], 1)
            pipeline(act, (n2_T, 0), (n2_gelu, 3), (n2_x2T, 2))

        @block.vector
        def _(v):
            v.wait_ge(s_iota, 1)
            v.tensor_scalar(ident[:, :], iota_row[:, :], iota_col[:, 0:1], None, ALU.is_equal)
            v.tensor_scalar(tri[:, :], iota_row[:, :], iota_col[:, 0:1], None, ALU.is_gt)
            v.memset(ones[:, :], 1.0)
            v.drain().then_inc(s_cst, 1)
            v.wait_ge(s_sched, 16)
            v.tensor_scalar(sched_w[:, :, :], sched[:, :, :], 7, None, ALU.arith_shift_right)
            v.drain()
            v.tensor_copy(sched_f[:, :, :], sched_w[:, :, :])
            v.drain()
            v.tensor_tensor(n_win[:, :], sched_f[:, :, 1], sched_f[:, :, 0], ALU.subtract)
            v.tensor_tensor(d_win[:, :], sched_f[:, :, 0], sched_f[:, :, 2], ALU.subtract)
            v.drain()
            v.tensor_scalar(n_win[:, :], n_win[:, :], 1.0, None, ALU.add)
            v.tensor_scalar(d_win[:, :], d_win[:, :], -1.0, None, ALU.add)
            v.drain().then_inc(s_win, 1)
            v.wait_ge(s_start, 1)
            v.tensor_copy(start[:, :], ps[:, 0, 0:SG])
            v.drain()
            for gcol in range(SG):
                v.tensor_scalar(begun[:, gcol, :], pair_no[:, :], start[:, gcol:gcol + 1], None, ALU.is_ge)
                v.tensor_scalar(stepped[:, gcol, :], pair_no[:, :], start[:, gcol:gcol + 1], d_win[:, gcol:gcol + 1],
                                ALU.is_ge, ALU.mult)
            v.drain().then_inc(s_begun, 1)
            v.wait_ge(s_pairs, 1)
            v.tensor_scalar(t_of[:, :], ps[:, 1, 0:NPAIR], -1.0, float(NS - 1), ALU.add, ALU.min)
            v.tensor_tensor(w_of[:, :], pair_no[:, :], ps[:, 2, 0:NPAIR], ALU.add)
            v.drain()
            v.tensor_scalar(w_of[:, :], w_of[:, :], float(NW - 1), None, ALU.min)
            v.drain()
            v.tensor_copy(tw_int[0:1, 0, :], t_of[0:1, :])
            v.tensor_copy(tw_int[0:1, 1, :], w_of[0:1, :])
            v.tensor_scalar(base_tab[:, :], w_of[:, :], float(P), None, ALU.mult)
            v.tensor_scalar(node_tab[:, :], w_of[:, :], float(P), iota_col[:, 0:1], ALU.mult, ALU.add)
            v.memset(keep_tab[:, 0:1], 0.0)
            v.tensor_tensor(keep_tab[:, 1:NPAIR], w_of[:, 1:NPAIR], w_of[:, 0:NPAIR - 1], ALU.is_equal)
            v.tensor_scalar(begun[:, 0, :], w_of[:, :], iota_col[:, 0:1], None, ALU.is_le)
            v.tensor_scalar(begun[:, 1, :], w_of[:, :], iota_col[:, 0:1], None, ALU.is_equal)
            v.drain()
            v.tensor_reduce(last_pair[:, 0:2], begun[:, 0:2, :], AX.X, ALU.add)
            v.drain()
            v.tensor_scalar(last_pair[:, 2:3], last_pair[:, 0:1], float(-1 - NPAIR), None, ALU.add)
            v.tensor_scalar(last_pair[:, 1:2], last_pair[:, 1:2], 1.0, None, ALU.min)
            v.drain()
            v.tensor_tensor(last_pair[:, 3:4], last_pair[:, 2:3], last_pair[:, 1:2], ALU.mult)
            v.drain()
            v.tensor_scalar(last_pair[:, 0:1], last_pair[:, 3:4], float(NPAIR), None, ALU.add)
            v.drain().then_inc(s_begun, 1)
            v.wait_ge(s_pairs, 2)
            v.tensor_copy(last_int[:, :], ps[0:1, 3, 0:P])
            v.drain().then_inc(s_tab, 1)

            def split(b, n, src, scale, done):
                v.tensor_scalar(nq[b][:, 0, 0:n], src, scale, None, ALU.mult)
                yield
                v.scalar_tensor_tensor(nlow[b][:, 0:n], src, scale, nq[b][:, 0, 0:n], ALU.mult, ALU.subtract)
                yield
                v.tensor_copy(nq[b][:, 1, 0:n], nlow[b][:, 0:n])
                yield
                v.tensor_tensor(nq[b][:, 2, 0:n], nlow[b][:, 0:n], nq[b][:, 1, 0:n], ALU.subtract).then_inc(done, 1)

            v.wait_ge(s_w, 16 * N_WEIGHTS)

            def n0_bias(w, b, k):
                v.wait_ge(n0["big"], w + 1)
                after(v, n0["store"][b], 48 * k)
                proj = ps[:, 2 * b + 1, :]
                v.tensor_tensor(nbig[b][:, 0:DM], proj[:, 0:DM], b_qkvs[:, 0:DM], ALU.add)
                v.tensor_tensor(nres[b][:, 0:2 * DM], proj[:, DM:3 * DM], b_qkvs[:, DM:3 * DM], ALU.add)
                v.tensor_tensor(nxr[b][:, :], proj[:, 3 * DM:4 * DM], b_qkvs[:, 3 * DM:4 * DM], ALU.add)\
                 .then_inc(n0["kv"], 1)
                yield

            def n0_split(w, b, k):
                return split(b, DM, nbig[b][:, 0:DM], OUTC ** -0.5, n0["res"])
            pipeline(v, [(n0_bias, 1), (n0_split, 2)])
            end_phase(v, 1)

            def edge(L):
                s, H, R = L.s, L.H, L.R

                def first_node(c, par):
                    v.wait_ge(s["ld_row"][0], 16 * (CH // 2 * c + 1))
                    v.tensor_tensor(rel_first[par][0:H, :], dst_row[0][0:H, 0:1], base_tab[0:H, bass.ds(CH * c, 1)],
                                    ALU.subtract).then_inc(s["first"], 1)

                def spread_nodes(c, st):
                    c, st = c + st // CH, st % CH
                    g, b, n = CH * c + st, st % 2, CH // 2 * c + st // 2
                    v.wait_ge(s["ld_row"][b], 16 * (n + 1))
                    after(v, s["q"], g - PLACES + 1)
                    v.tensor_scalar(oht[st % PLACES][:, :], dst_row[st % PLACES][:, :], node_tab[:, bass.ds(g, 1)], None,
                                    ALU.is_equal).then_inc(s["oht"], 1)

                def add_edges(c, par, st):
                    b, n = st % 2, CH // 2 * c + st // 2
                    v.wait_ge(s["gathered"][b], 64 * (n + 1))
                    v.wait_ge(s["e"], CH * c + st + 1)
                    kv = rows[par][:, st, :, :].rearrange("p j (m n) -> p j m n", m=2)
                    v.tensor_tensor(kv, kv, e_ps(b).rearrange("p (j n) -> p j n", j=JT).unsqueeze(2)
                                    .to_broadcast([P, JT, 2, DM]), ALU.add).then_inc(s["added"], 1)

                def products(c, par, st):
                    v.wait_ge(s["q"], CH * c + st + 1)
                    half = prod[:, :, st % 2 * DM:(st % 2 + 1) * DM]
                    v.tensor_tensor(half, rows[par][:, st, :, 0:DM],
                                    q_ps(L, st % 2).rearrange("p (j n) -> p j n", j=JT), ALU.mult)

                def scores_of(c, par, st):
                    v.tensor_reduce(score[par][:, st * JT:(st + 1) * JT, :],
                                    prod[:, :, st % 2 * DM:(st % 2 + 1) * DM]
                                    .rearrange("p j (h n) -> p j h n", h=HEADS), AX.X, ALU.add)\
                     .then_inc(s["score"], 1)

                def dots(c, par, st):
                    g, b, n = CH * c + st, st % 2, CH // 2 * c + st // 2
                    v.wait_ge(s["gathered"][b], 64 * (n + 1))
                    v.wait_ge(s["q"], g + 1)
                    for j in range(JT):
                        i = v.tensor_tensor_reduce(
                            out=prod[:, j, :], in0=rows[par][:, st, j, :], in1=q_ps(L, b)[:, j * D:(j + 1) * D],
                            scale=1.0, scalar=0.0, op0=ALU.mult, op1=ALU.add,
                            accum_out=score[par][:, st * JT + j, 0:1])
                    i.then_inc(s["score"], 1)

                def mask(c, par):
                    for st in range(CH if L is L0 else 1):
                        v.wait_ge(L.idx_sem[st], L.idx_before + 16 * (c + 1))
                    dst = idx[par][:, :, JT:2 * JT]
                    before = idx[par][:, :, 2 * JT:3 * JT]
                    relc = rel[par][:, :, :]
                    flat = relc.rearrange("p s j -> p (s j)")
                    after(v, s["agg"], CH * (c - 1))
                    v.tensor_tensor(relc, dst, base_tab[:, bass.ds(CH * c, CH)].unsqueeze(2).to_broadcast([P, CH, JT]),
                                    ALU.subtract)
                    v.tensor_tensor(same[:, :].rearrange("p (s j) -> p s j", j=JT), dst, before, ALU.is_equal)
                    yield
                    after(v, s["turned"], c)
                    v.tensor_scalar(pen[:, :, 0:H], same[:, :].unsqueeze(2).to_broadcast([P, NI, H]), -1.0, BIG,
                                    ALU.add, ALU.mult)
                    v.tensor_scalar(inside[:, :], flat, 0.0, None, ALU.is_ge)
                    yield
                    v.scalar_tensor_tensor(inside[:, :], flat, float(P), inside[:, :], ALU.is_lt, ALU.mult)
                    yield
                    v.tensor_scalar(outside[:, :], inside[:, :], -1.0, BIG, ALU.add, ALU.mult)

                def mask_scores(c, par):
                    sc = score[par][:, :, 0:H]
                    if L is L1:
                        for b in range(2):
                            v.wait_ge(s["ld_ea"][b], 16 * (CH // 2) * (c + 1))
                        v.tensor_scalar(weighed[:, :], ew[par][:, :], we_be[:, 0:1], we_be[:, 1:2], ALU.mult, ALU.add)
                        v.tensor_reduce(qb[:, :], qb_ps[par].rearrange("p (n m) -> p n m", m=3), AX.X, ALU.add)
                        v.drain()
                        v.tensor_tensor(sc[:, :, 0], sc[:, :, 0], weighed[:, :], ALU.add)
                        v.tensor_tensor(outside[:, :], outside[:, :], qb[:, :], ALU.add)
                    v.drain()
                    v.tensor_tensor(biased[:, :, 0:H], sc, outside[:, :].unsqueeze(2).to_broadcast([P, NI, H]), ALU.add)
                    v.drain().then_inc(s["masked"], 1)

                sT = turn_ps[0:R, 0:P]
                pf, pb = pen_r[0:R, 0:P], pen_r[0:R, 1:P + 1]

                def scan_tiles(c, par):
                    v.wait_ge(s["turned"], c + 1)
                    v.wait_ge(s["pens"], c + 1)
                    v.tensor_tensor_scan(fwd[0:R, :], pf, sT, -BIG, ALU.add, ALU.max)
                    v.tensor_tensor_scan(bwd[0:R, ::-1], pb[:, ::-1], sT[:, ::-1], -BIG, ALU.add, ALU.max)
                    v.tensor_reduce(carry_r[0:R, 0:1], pen_r[0:R, 1:P], AX.X, ALU.min)
                    v.drain()
                    ends = (fwd[0:R, P - 1:P], bwd[0:R, 0:1], pen_r[0:R, 0:1], carry_r[0:R, 0:1])
                    for m, col in enumerate(ends):
                        v.tensor_scalar(spread[0:R, m, :], sel_j[H][0:R, :], col, None, ALU.mult)
                    v.drain().then_inc(s["ends"], 1)

                def scan_ends(c, par):
                    v.wait_ge(s["arranged"], c + 1)
                    v.tensor_copy(runs[0:H, :, 0:NI], arr_ps[0:H, :].rearrange("p (m n) -> p m n", m=4))
                    v.tensor_copy(run_f[par][0:H, 0:1], run_f[1 - par][0:H, NI:NI + 1])
                    v.drain()
                    v.tensor_tensor(pen_f[0:H, :], runs[0:H, 2, 0:NI], runs[0:H, 3, 0:NI], ALU.add)
                    v.tensor_tensor(pen_b[0:H, :], runs[0:H, 2, 1:NI + 1], runs[0:H, 3, 0:NI], ALU.add)
                    v.drain()
                    v.tensor_tensor_scan(run_f[par][0:H, 1:NI + 1], pen_f[0:H, :], runs[0:H, 0, 0:NI],
                                         run_f[par][0:H, 0:1], ALU.add, ALU.max)
                    v.tensor_tensor_scan(run_b[0:H, 0:NI][:, ::-1], pen_b[0:H, ::-1], runs[0:H, 1, 0:NI][:, ::-1],
                                         -BIG, ALU.add, ALU.max)
                    v.drain()
                    v.tensor_copy(carry[0:H, 0, :], run_f[par][0:H, 0:NI])
                    v.tensor_tensor(carry[0:H, 1, :], run_b[0:H, 1:NI + 1], runs[0:H, 2, 1:NI + 1], ALU.add)
                    v.drain().then_inc(s["carries"], 1)

                def scan_carried(c, par):
                    v.wait_ge(s["spreadback"], c + 1)
                    v.tensor_tensor(carry_p[0:R, :, :], back_ps[0:R, :].rearrange("p (m n) -> p m n", m=2),
                                    sel_j[H][0:R, :].unsqueeze(1).to_broadcast([R, 2, NI]), ALU.mult)
                    v.drain()
                    v.tensor_reduce(carry_r[0:R, :], carry_p[0:R, :, :], AX.X, ALU.add)
                    v.drain()
                    v.tensor_tensor_scan(fwd[0:R, :], pf, sT, carry_r[0:R, 0:1], ALU.add, ALU.max)
                    v.drain()
                    v.tensor_tensor_scan(full[0:R, ::-1], pb[:, ::-1], fwd[0:R, ::-1], carry_r[0:R, 1:2],
                                         ALU.add, ALU.max)
                    v.drain().then_inc(s["full"], 1)

                def subtract(c, par):
                    v.tensor_scalar(shrink_in[0:H, :], run_f[par][0:H, 0:1], full[0:H, 0:1], 0.0, ALU.subtract, ALU.min)\
                     .then_inc(s["shrink_in"], 1)
                    v.tensor_scalar(first_oh[0:H, :], iota_row[0:H, :], rel_first[par][0:H, 0:1], None, ALU.is_equal)
                    v.wait_ge(s["fullT"], c + 1)
                    v.tensor_tensor(below[:, 0:R], biased[:, :, 0:H].rearrange("p n h -> p (n h)") if H == HEADS else
                                    biased[:, :, 0], turn_ps[:, 2 * P:2 * P + R], ALU.subtract).then_inc(s["below"], 1)

                def shrink_first(c):
                    v.wait_ge(s["shrink"], c + 1)
                    v.scalar_tensor_tensor(shrink_d[0:H, 0:H], ident[0:H, 0:H], shrink[0:H, 0:1], ident[0:H, 0:H],
                                           ALU.mult, ALU.subtract).then_inc(s["so_in"], 1)

                def weigh(c, par, st):
                    g, b = CH * c + st, st % 2
                    after(v, s["agg"], g - OHS + 1)
                    if L is L0:
                        v.wait_ge(s["prob"], c + 1)
                        m = msg[st % OHS][:, :, 0:L.AW].rearrange("p j (h c) -> p j h c", h=HEADS)[:, :, :, 0:OUTC]
                        v.tensor_tensor(m, rows[par][:, st, :, DM:2 * DM].rearrange("p j (h c) -> p j h c", h=HEADS),
                                        prob[par][:, st * JT:(st + 1) * JT, :].unsqueeze(3)
                                        .to_broadcast([P, JT, HEADS, OUTC]), ALU.mult).then_inc(s["msg"], 1)
                    else:
                        v.tensor_tensor(oh[:, st % OHS, :, :], iota_row[:, :].unsqueeze(1).to_broadcast([P, JT, P]),
                                        rel[par][:, st, :].unsqueeze(2).to_broadcast([P, JT, P]), ALU.is_equal)\
                         .then_inc(s["msg"], 1)

                def shrink_sums(c):
                    v.wait_ge(s["so"], c + 1)
                    v.tensor_scalar(rescale[:, 0:H], so_ps[:, 0:H], 1.0, None, ALU.add)
                    v.drain()
                    v.tensor_tensor(acc_scaled[:, 0:L.AW].rearrange("p (h c) -> p h c", h=H),
                                    acc[(CH - 1) % ACCS][:, 0:L.AW].rearrange("p (h c) -> p h c", h=H),
                                    rescale[:, 0:H].unsqueeze(2).to_broadcast([P, H, L.AW // H]), ALU.mult)

                def accumulate(c, st):
                    g, b = CH * c + st, st % 2
                    old = acc_scaled if st == 0 else acc[(st - 1) % ACCS]
                    v.wait_ge(s["agg"], g + 1)
                    after(v, s["stored"][b], 16 * (CH // 2 * c + st // 2 - ACCS // 2 + 1))
                    v.scalar_tensor_tensor(acc[st % ACCS][:, 0:L.AW], old[:, 0:L.AW], keep_tab[:, bass.ds(g, 1)], agg_ps(L, b),
                                           ALU.mult, ALU.add).then_inc(s["acc"], 1)

                def emit(c, par, scores, sums):
                    past, pp = c - 1, 1 - par
                    if scores:
                        first_node(c, par)
                        if L is L0:
                            add_edges(c, par, 0)
                        elif not sums:
                            spread_nodes(c, 0)
                            spread_nodes(c, 1)
                    if sums:
                        mask_scores(past, pp)
                    else:
                        v.drain()
                    masking = mask(c, par) if scores else iter(())
                    def sum_and_scan_tiles(c, par):
                        if L is L0 and not (isinstance(c, int) and c == 0):
                            accumulate(c - 1, CH - 1)
                        scan_tiles(c, par)

                    parts = iter((sum_and_scan_tiles, scan_ends, scan_carried, subtract))
                    for st in range(CH):
                        if sums and st == 0 and L is L1:
                            next(parts)(past, pp)
                        if scores:
                            if L is L0:
                                if st > 0:
                                    scores_of(c, par, st - 1)
                                products(c, par, st)
                            else:
                                dots(c, par, st)
                                if more(c, st + 2):
                                    spread_nodes(c, st + 2)
                        if sums and st == 2 and L is L0:
                            shrink_first(past)
                        if sums and st < 2 and not (st == 0 and L is L1):
                            next(parts)(past, pp)
                        if scores and L is L0 and st + 1 < CH:
                            add_edges(c, par, st + 1)
                        if L is L1 and sums and st == 0 and not (isinstance(past, int) and past == 0):
                            accumulate(past - 1, CH - 1)
                        if sums and st < 2:
                            next(parts)(past, pp)
                        if sums and st == 1 and L is L1:
                            shrink_first(past)
                        for r in L.summed[st] if sums else ():
                            weigh(past, pp, r)
                        if st >= 2:
                            next(masking, None)
                        if sums and st == 2:
                            shrink_sums(past)
                        for m, r in enumerate(L.summed[st - 1] if sums and st else ()):
                            if m:
                                v.drain()
                            accumulate(past, r)
                        v.drain()
                    if scores and L is L0:
                        scores_of(c, par, CH - 1)
                    if not scores:
                        accumulate(past, CH - 1)
                    v.drain()
                chunks(v, emit)

            edge(L0)
            end_phase(v, 2)

            def moments(h, b, norm):
                var_ready, _, stats, mv, ve, _ = norm
                yield
                v.bn_stats(stats[b][:, :], h)
                yield
                v.bn_aggr(mv[b][:, :], stats[b][:, :])
                yield
                v.tensor_scalar(ve[b][:, :], mv[b][:, 1:2], EPS, None, ALU.add).then_inc(var_ready, 1)

            def normal(out_, h, w, b, norm):
                _, rstd_ready, _, mv, _, rstd = norm
                v.wait_ge(rstd_ready, w + 1)
                return v.tensor_scalar(out_, h, mv[b][:, 0:1], rstd[b][:, 0:1], ALU.subtract, ALU.mult)

            def heads(ap):
                return ap.rearrange("p (h c) -> p h c", h=HEADS)

            mean = [nsum[b][:, 0:DM] for b in range(U)]
            more_x = [nbig[b][:, 0:DM] for b in range(U)]
            mixed = [nbig[b][:, DM:2 * DM] for b in range(U)]

            def n1_mean(w, b, k):
                v.wait_ge(n1["load"][b], 48 * (k + 1))
                sums = heads(nacc[b][:, 0:L0.AW])

                def gate_sum(m, part, scale, z):
                    return v.tensor_tensor_reduce(out=mixed[b], in0=part, in1=w_beta[:, m, :], scale=scale, scalar=z,
                                                  op0=ALU.mult, op1=ALU.add, accum_out=nz[b][:, m:m + 1])

                v.tensor_scalar(nden[b][:, :], sums[:, :, OUTC], 1e-16, None, ALU.add)
                gate_sum(1, nxr[b][:, :], 1.0, 0.0)
                yield
                v.reciprocal(nden[b][:, :], nden[b][:, :])
                yield
                v.tensor_tensor(heads(mean[b]), sums[:, :, 0:OUTC],
                                nden[b][:, :].unsqueeze(2).to_broadcast([P, HEADS, OUTC]), ALU.mult)
                yield
                v.tensor_tensor(more_x[b], nxr[b][:, :], mean[b], ALU.subtract)
                gate_sum(0, mean[b], 1.0, nz[b][:, 1:2])
                yield
                gate_sum(2, more_x[b], -1.0, nz[b][:, 0:1]).then_inc(n1["z"], 1)

            def n1_mix(w, b, k):
                v.wait_ge(n1["en"], w + 1)
                v.tensor_scalar(nz[b][:, 4:5], nz[b][:, 3:4], 1.0, None, ALU.add)
                yield
                v.reciprocal(nz[b][:, 5:6], nz[b][:, 4:5])
                yield
                v.scalar_tensor_tensor(mixed[b], more_x[b], nz[b][:, 5:6], mean[b], ALU.mult, ALU.add)\
                 .then_inc(n1["mix"], 1)

            def n1_residual(w, b, k):
                v.wait_ge(n1["y"], w + 1)
                v.tensor_tensor(nh[b][:, :], nrow[b][:, :], ps[:, 2 * b + 1, 0:D], ALU.add)
                yield from moments(nh[b][:, :], b, roots1[0])

            def n1_norm(w, b, k):
                after(v, n1["store"][b], 32 * k)
                normal(nres[b][:, 0:D], nh[b][:, :], w, b, roots1[0]).then_inc(n1["x1"], 1)
                yield

            def n1_split(w, b, k):
                v.wait_ge(n1["qk"], w + 1)
                yield from split(b, D + 1, ps[:, 2 * b, 0:D + 1], D ** -0.5, n1["split"])
            pipeline(v, [(n1_norm, 3), (n1_mix, 1), (n1_mean, 0), (n1_residual, 2), (n1_split, 4)])
            end_phase(v, 3)

            edge(L1)
            end_phase(v, 4)

            def n2_weights(w, b, k):
                v.wait_ge(n2["load"][b], LOADED1 + 48 * k + 32)
                v.tensor_scalar(nden[b][:, 0:1], nacc[b][:, D:D + 1], 1e-12, None, ALU.max)
                yield
                v.reciprocal(nden[b][:, 1:2], nden[b][:, 0:1])

            def n2_mean(w, b, k):
                v.tensor_scalar(nsum[b][:, :], nacc[b][:, :], nden[b][:, 1:2], None, ALU.mult).then_inc(n2["mean"], 1)
                yield
                v.wait_ge(n2["skip"], w + 1)
                v.scalar_tensor_tensor(nskip[b][:, :], rows1[:, BV, :], nsum[b][:, D:D + 1], nskip[b][:, :],
                                       ALU.mult, ALU.add)

            def n2_attended(w, b, k):
                v.wait_ge(n2["lin"], w + 1)
                v.tensor_tensor(natt[b][:, :], nskip[b][:, :], ps[:, 2 * b + 1, 0:D], ALU.add)
                yield from moments(natt[b][:, :], b, roots2[0])

            def n2_norm1(w, b, k):
                normal(nx2[b][:, :], natt[b][:, :], w, b, roots2[0])
                yield
                v.tensor_tensor(nx2[b][:, :], nx2[b][:, :], rows1[:, G1, :], ALU.mult)
                yield
                v.tensor_tensor(nx2[b][:, :], nx2[b][:, :], rows1[:, B1, :], ALU.add).then_inc(n2["x2"], 1)

            def n2_forward(w, b, k):
                v.wait_ge(n2["f"], w + 1)
                v.wait_ge(n2["up"], w + 1)
                v.tensor_tensor(nffn[b][:, :], nup[b][:, :], ps[:, 2 * b, 0:D], ALU.add)
                yield from moments(nffn[b][:, :], b, roots2[1])

            def n2_norm2(w, b, k):
                normal(nffn[b][:, :], nffn[b][:, :], w, b, roots2[1])
                yield
                v.tensor_tensor(nffn[b][:, :], nffn[b][:, :], rows1[:, G2, :], ALU.mult)
                yield
                v.wait_ge(n2["end"], w + 1)
                v.tensor_tensor(nend[b][:, :], nffn[b][:, :], nagain[b][:, :], ALU.add)
                yield from moments(nend[b][:, :], b, roots2[2])

            def n2_norm3(w, b, k):
                after(v, n2["store"][b], 16 * k)
                normal(nres[b][:, 0:D], nend[b][:, :], w, b, roots2[2]).then_inc(n2["res"], 1)
                yield
            pipeline(v, [(n2_forward, 4), (n2_mean, 0), (n2_norm1, 2), (n2_norm2, 5), (n2_norm3, 6), (n2_weights, -1), (n2_attended, 1)])

        @block.tensor
        def _(pe):
            gate = sem("pe_gate")

            def mm(out_, lhsT, rhs, first=True, last=True):
                return pe.matmul(out_, lhsT=lhsT, rhs=rhs, start=first, stop=last)

            pe.wait_ge(s_cst, 1)
            pe.wait_ge(s_win, 1)
            for gcol in range(SG):
                for m in range(gcol + 1):
                    i = mm(ps[:, 0, gcol:gcol + 1], tri[:, :] if m == gcol else ones[:, :], n_win[:, m:m + 1],
                           m == 0, m == gcol)
            i.then_inc(s_start, 1)
            pe.wait_ge(s_begun, 1)
            for bank, part in ((1, begun), (2, stepped)):
                for gcol in range(SG):
                    i = mm(ps[:, bank, 0:NPAIR], ones[:, :], part[:, gcol, :], gcol == 0, gcol == SG - 1)
            i.then_inc(s_pairs, 1)
            pe.wait_ge(s_w, 16 * N_WEIGHTS)
            mm(ps[0:DR, 7, 0:DM], w_edge[:, :], w_et[:, :]).then_inc(s_wcp, 1)
            pe.wait_ge(s_begun, 2)
            mm(ps[0:1, 3, 0:P], last_pair[:, 0:1], ident[:, :]).then_inc(s_pairs, 1)
            pe.wait_ge(s_tab, 1)
            pe.wait_ge(s_wc, 1)

            def n0_messages(w, b, k):
                pe.wait_ge(n0["load"][b], 16 * (k + 1))
                after(pe, n0["mT"], w - U + 1)
                for m in range(2):
                    i = mm(ps[:, 2 * b, 0:P], w_n2m[:, m, :], nx[b][:, m, :], m == 0, m == 1)
                i.then_inc(n0["m"], 1)

            def n0_project(w, b, k):
                pe.wait_ge(n0["mT"], w + 1)
                after(pe, n0["kv"], w - U + 1)
                mm(ps[:, 2 * b + 1, :], nT[b][:, 0, :], w_qkvs[:, :]).then_inc(n0["big"], 1)
            pipeline(pe, (n0_messages, 0), (n0_project, 1))
            end_phase(pe, 1)

            def edge(L):
                s, H, R = L.s, L.H, L.R

                def edge_keys(c, st):
                    c, st = c + st // CH, st % CH
                    g, b, n = CH * c + st, st % 2, CH // 2 * c + st // 2
                    if L is L0:
                        after(pe, s["added"], g - 1)
                        pe.wait_ge(s["ld_ea"][b], 16 * (n + 1))
                        for j in range(JT):
                            i = mm(e_ps(b)[:, j * DM:(j + 1) * DM], ea[st % PLACES][:, j * P:(j + 1) * P], w_c[:, :])
                        i.then_inc(s["e"], 1)

                def queries_ready(c, st):
                    g, b, n = CH * c + st, st % 2, CH // 2 * c + st // 2
                    pe.wait_ge(s["ld_q"][b], 16 * (n + 1))
                    pe.wait_ge(s["oht"], g + 1)

                def queries(c, par, st):
                    c, st = c + st // CH, st % CH
                    g, b = CH * c + st, st % 2
                    after(pe, s["score"], g - 1)
                    queries_ready(c, st)
                    for j in range(JT):
                        for m in range(3):
                            i = mm(q_ps(L, b)[:, j * L.D:(j + 1) * L.D], oht[st % PLACES][:, j * P:(j + 1) * P],
                                   qw[st % PLACES][:, m * L.QD:m * L.QD + L.D], m == 0, m == 2)
                    if L is L0 or st == 1:
                        i.then_inc(s["q"], 1)

                def bias_products(par, st):
                    if L is L1:
                        for j in range(JT):
                            n = st * JT + j
                            i = mm(qb_ps[par][:, 3 * n:3 * (n + 1)], oht[st % PLACES][:, j * P:(j + 1) * P],
                                   qw[st % PLACES][:, D::D + 1])
                        if st != 1:
                            i.then_inc(s["q"], 1)

                def turn(c):
                    stand_by(pe, gate, s["masked"], c + 1)
                    sc = biased[:, :, 0:H].rearrange("p n h -> p (n h)") if H == HEADS else biased[:, :, 0]
                    pn = pen[:, :, 0:H].rearrange("p n h -> p (n h)") if H == HEADS else pen[:, :, 0]
                    pe.transpose(turn_ps[0:R, 0:P], sc, ident[:, :])
                    pe.transpose(turn_ps[0:R, P:2 * P], pn, ident[:, :]).then_inc(s["turned"], 1)

                def arrange(c):
                    stand_by(pe, gate, s["ends"], c + 1)
                    mm(arr_ps[0:H, :], sel_h[H][0:R, :], spread[0:R, :, :].rearrange("p m n -> p (m n)"))\
                        .then_inc(s["arranged"], 1)

                def carry_back(c):
                    stand_by(pe, gate, s["carries"], c + 1)
                    mm(back_ps[0:R, :], sel_ht[H][0:H, 0:R], carry[0:H, :, :].rearrange("p m n -> p (m n)"))\
                        .then_inc(s["spreadback"], 1)

                def turn_back(c):
                    stand_by(pe, gate, s["full"], c + 1)
                    pe.transpose(turn_ps[:, 2 * P:2 * P + R], full[0:R, :], ident[0:R, 0:R]).then_inc(s["fullT"], 1)

                def shrink_first(c):
                    stand_by(pe, gate, s["so_in"], c + 1)
                    mm(so_ps[:, 0:H], first_oh[0:H, :], shrink_d[0:H, 0:H]).then_inc(s["so"], 1)

                def back(c, par, st):
                    g, b = CH * c + st, st % 2
                    pe.wait_ge(s["msg"], g + 1)
                    pe.wait_ge(s["msgp"], g + 1)
                    after(pe, s["acc"], g - 1)
                    for j in range(JT):
                        i = mm(agg_ps(L, b), oh[:, st % OHS, j, :], msg[st % OHS][:, j, 0:L.AW], j == 0, j == JT - 1)
                    i.then_inc(s["agg"], 1)

                def emit(c, par, scores, sums):
                    past, pp = c - 1, 1 - par
                    if not sums:
                        edge_keys(c, 0)
                        edge_keys(c, 1)
                        queries(c, par, 0)
                    if sums:
                        turn(past)
                    if scores:
                        bias_products(par, 0)
                    if L is L1 and sums and not (isinstance(past, int) and past == 0):
                        back(past - 1, par, CH - 1)
                    if scores and L is L0:
                        queries(c, par, 1)
                    if scores and L is L1:
                        queries_ready(c, 1)
                        bias_products(par, 1)
                    if sums:
                        arrange(past)
                    if scores and L is L1:
                        queries(c, par, 1)
                    if sums:
                        carry_back(past)
                    if scores:
                        edge_keys(c, 2)
                        queries(c, par, 2)
                    if sums:
                        turn_back(past)
                    if scores:
                        edge_keys(c, 3)
                    if sums:
                        shrink_first(past)
                    if scores:
                        bias_products(par, 2)
                    for st in range(2, CH):
                        if scores and more(c, st + 2):
                            edge_keys(c, st + 2)
                        if scores and more(c, st + 1):
                            queries(c, par, st + 1)
                            if st + 1 < CH:
                                bias_products(par, st + 1)
                        for r in L.summed[st] if sums and (L is L0 or st < CH - 1) else ():
                            back(past, pp, r)
                    if L is L1 and not scores:
                        back(past, pp, CH - 1)
                chunks(pe, emit)

            edge(L0)
            end_phase(pe, 2)

            def n1_mixedT(w, b, k):
                pe.wait_ge(n1["mix"], w + 1)
                pe.transpose(ps[:, 2 * b, 0:P], nbig[b][:, DM:2 * DM], ident[:, :]).then_inc(n1["tp"], 1)

            def n1_out(w, b, k):
                pe.wait_ge(n1["tc"], w + 1)
                mm(ps[:, 2 * b + 1, 0:D], nT[b][:, 0, :], w_m2n[:, :]).then_inc(n1["y"], 1)

            def n1_x1T(w, b, k):
                pe.wait_ge(n1["x1"], w + 1)
                for m in range(2):
                    i = pe.transpose(ps[:, 2 * b, m * P:(m + 1) * P], nres[b][:, m * P:(m + 1) * P], ident[:, :])
                i.then_inc(n1["xt"], 1)

            def n1_qT(w, b, k):
                pe.wait_ge(n1["xc"], w + 1)
                for f in range(2):
                    for m in range(2):
                        i = mm(ps[:, 2 * b + 1, f * P:(f + 1) * P], w_q1[:, m, f * P:(f + 1) * P], nT[b][:, 2 + m, :],
                               m == 0, m == 1)
                i.then_inc(n1["q"], 1)

            def n1_qk(w, b, k):
                pe.wait_ge(n1["qc"], w + 1)
                for m in range(2):
                    i = mm(ps[:, 2 * b, 0:D + 1], nT2[b][:, m, :], w_k1t[:, m, :], m == 0, m == 1)
                i.then_inc(n1["qk"], 1)
            pipeline(pe, (n1_qk, 4), (n1_x1T, 3), (n1_qT, 3), (n1_mixedT, 1), (n1_out, 1))
            end_phase(pe, 3)
            edge(L1)
            end_phase(pe, 4)

            def n2_T(w, b, k):
                pe.wait_ge(n2["mean"], w + 1)
                for m in range(4):
                    part = nsum[b] if m < 2 else nrow[b]
                    i = pe.transpose(ps[:, 2 * b, m * P:(m + 1) * P], part[:, m % 2 * P:(m % 2 + 1) * P], ident[:, :])
                i.then_inc(n2["tp"], 1)

            def n2_lin(w, b, k):
                pe.wait_ge(n2["tc"], w + 1)
                for m in range(4):
                    i = mm(ps[:, 2 * b + 1, 0:D], nT[b][:, m, :], (w_v1 if m < 2 else w_s1)[:, m % 2, :], m == 0, m == 3)
                i.then_inc(n2["lin"], 1)

            def n2_x2T(w, b, k):
                pe.wait_ge(n2["x2"], w + 1)
                for m in range(2):
                    i = pe.transpose(ps[:, 2 * b, m * P:(m + 1) * P], nx2[b][:, m * P:(m + 1) * P], ident[:, :])
                i.then_inc(n2["xt"], 1)

            def n2_up(w, b, k):
                pe.wait_ge(n2["xc"], w + 1)
                for f in range(4):
                    for m in range(2):
                        i = mm(ps[:, 2 * b + 1, f * P:(f + 1) * P], w_f1[:, m, f * P:(f + 1) * P], nT[b][:, m, :],
                               m == 0, m == 1)
                i.then_inc(n2["u"], 1)

            def n2_down(w, b, k):
                pe.wait_ge(n2["g"], w + 1)
                for m in range(4):
                    i = mm(ps[:, 2 * b, 0:D], nT2[b][:, m, :], w_f2[:, m, :], m == 0, m == 3)
                i.then_inc(n2["f"], 1)
            pipeline(pe, (n2_T, 0), (n2_up, 3), (n2_lin, 0), (n2_down, 3), (n2_x2T, 2))


N_WEIGHTS = 17


def kernel(x, src, dst, edge_attr_64, edge_weight, **w):
    import concourse.bacc as bacc
    from concourse.bass_utils import run_bass_kernel_spmd

    def arr(v):
        return np.asarray(v)

    def halves(m):
        m = arr(m)
        return m.reshape(-1, P, m.shape[1]).transpose(1, 0, 2)

    x, src, dst = arr(x), arr(src), arr(dst)
    xp = np.zeros((NP, D), x.dtype)
    xp[:N] = x

    def padded(v, fill):
        p = np.full((EP,) + v.shape[1:], fill, v.dtype)
        p[:E] = v
        return p

    def tiles(v):
        return v.reshape(NS, JT, P).transpose(0, 2, 1)

    dstp = padded(dst, NO_NODE)
    before = np.full(EP, -1, dst.dtype)
    before[1:] = dstp[:-1]
    idx = np.concatenate([tiles(v) for v in (padded(src, 0), dstp, before)], axis=2)
    sched = np.zeros((SG * P, 3), dst.dtype)
    sched[:, 1] = -P
    sched[:, 2] = -1
    lasts = [min(SUPER * (t + 1), E) - 1 for t in range(NS)]
    sched[:NS, 0] = dst[::SUPER]
    sched[:NS, 1] = dst[lasts]
    sched[1:NS, 2] = dst[lasts[:-1]]
    sched = sched.reshape(SG, P, 3).transpose(1, 0, 2)
    k1t = np.concatenate([arr(w["L1_gnn_wk"]).T, arr(w["L1_gnn_bk"])[:, None]], axis=1)

    arrays = {
        "xT": xp.T.reshape(2, P, NP).transpose(1, 0, 2), "x": xp, "idx": idx, "dst_row": dstp.reshape(NS, SUPER),
        "eaT": padded(arr(edge_attr_64), 0).T, "ew": tiles(padded(arr(edge_weight), 0)), "sched": sched,
        "w_n2m": halves(arr(w["L0_gnn_W_n2m"]).T),
        "w_qkvs": np.concatenate([arr(w["L0_gnn_" + n]).T for n in ("Wq", "Wk", "Wv", "Wskip")], axis=1),
        "b_qkvs": np.concatenate([arr(w["L0_gnn_" + n]) for n in ("bq", "bk", "bv", "bskip")])[None],
        "w_edge": arr(w["L0_gnn_W_edge"]), "w_et": arr(w["L0_gnn_We"]).T, "w_beta": arr(w["L0_gnn_Wbeta"]),
        "w_m2n": arr(w["L0_gnn_W_m2n"]).T, "w_q1": halves(w["L1_gnn_wq"]),
        "b_q1": arr(w["L1_gnn_bq"]).reshape(2, P).T, "w_k1t": halves(k1t), "w_v1": halves(w["L1_gnn_wv"]),
        "w_s1": halves(w["L1_gnn_ws"]), "w_f1": halves(w["L1_gnn_w_ff1"]), "b_f1": arr(w["L1_gnn_b_ff1"]).reshape(4, P).T,
        "w_f2": halves(w["L1_gnn_w_ff2"]),
        "rows1": np.concatenate([arr(w["L1_gnn_" + n]) for n in ("bv", "bs", "g1", "b1", "g2", "b2", "b_ff2")])[None],
        "we_be": np.concatenate([arr(w["L1_gnn_we"]).reshape(-1), arr(w["L1_gnn_be"])])[None],
    }
    arrays = {n: np.ascontiguousarray(v) for n, v in arrays.items()}
    nc = bacc.Bacc("TRN2", target_bir_lowering=False, num_devices=1)
    aps = {n: nc.dram_tensor("in_" + n, v.shape, mybir.dt.from_np(v.dtype), kind="ExternalInput").ap()
           for n, v in arrays.items()}
    out = nc.dram_tensor("out", (NP, D), F32, kind="ExternalOutput").ap()
    build(nc, aps, out)
    r = run_bass_kernel_spmd(nc, [{"in_" + n: v for n, v in arrays.items()}], core_ids=[0])
    return r.results[0]["out"][:N]
```
